# Optimizing a Trainium2 kernel written in Bass

```python
import numpy as np
import jax
import jax.numpy as jnp

def _softmax(x, axis=-1):
    return jax.nn.softmax(x, axis=axis)

def _gelu(x):
    return jax.nn.gelu(x, approximate=True)

def _silu(x):
    return jax.nn.silu(x)

def _sigmoid(x):
    return jax.nn.sigmoid(x)

def _layernorm(x, axis=-1, eps=1e-05):
    m = jnp.mean(x, axis=axis, keepdims=True)
    v = jnp.var(x, axis=axis, keepdims=True)
    return (x - m) / jnp.sqrt(v + eps)

def _scatter_add(tgt, idx, src, axis=0):
    return tgt.at[idx].add(src)

def _segment_sum(src, seg, n):
    return jax.ops.segment_sum(src, seg, n)
kernel_name = 'mk_gnn_preln_d4_gnn_r8_a5e6f6'

def setup_inputs(seed: int=0):
    np.random.seed(seed)
    _w = jnp.asarray

    def _rec_inputs():
        import jax
        import jax.numpy as jnp
        _gk = jax.random.key(seed)
        x = -0.0008691 + 1 * jax.random.normal(jax.random.fold_in(_gk, 1), (6250, 128), jnp.float32)
        _s = jax.random.randint(jax.random.fold_in(_gk, 2), (50000,), 0, 6250, jnp.int32)
        _d = jax.random.randint(jax.random.fold_in(_gk, 3), (50000,), 0, 6250, jnp.int32)
        _loop = jnp.arange(6250, dtype=jnp.int32)
        src = jnp.concatenate([_s, _d, _loop])
        dst = jnp.concatenate([_d, _s, _loop])
        _o = jnp.argsort(dst, stable=True)
        src = src[_o]
        dst = dst[_o]
        edge_attr_128 = 2.93046e-05 + 1.00006 * jax.random.normal(jax.random.fold_in(_gk, 11), (106250, 128), jnp.float32)
        edge_weight1 = jax.random.uniform(jax.random.fold_in(_gk, 13), (106250, 1), jnp.float32, 0.0, 0.999998)
        return (x, src, dst, edge_attr_128, edge_weight1)
    x, src, dst, edge_attr_128, edge_weight1 = _rec_inputs()

    def _L0_gnn_setup():
        import jax, jax.numpy as jnp
        import numpy as np
        N, E = (1250, 80000)
        IN_DIM, EDGE_DIM, OUT_DIM = (128, 128, 128)
        key = jax.random.key(seed)
        ks = jax.random.split(key, 9)
        s = 0.02
        return {'x': jax.random.normal(ks[0], (N, IN_DIM), dtype=jnp.float32), 'edge_index': jax.random.randint(ks[1], (2, E), 0, N, dtype=jnp.int64), 'edge_attr': jax.random.normal(ks[2], (E, EDGE_DIM), dtype=jnp.float32), 'We': jax.random.normal(ks[3], (EDGE_DIM, IN_DIM), dtype=jnp.float32) * s, 'be': jnp.zeros((IN_DIM,), dtype=jnp.float32), 'W1': jax.random.normal(ks[4], (2 * IN_DIM, OUT_DIM), dtype=jnp.float32) * s, 'b1': jnp.zeros((OUT_DIM,), dtype=jnp.float32), 'W2': jax.random.normal(ks[5], (OUT_DIM, OUT_DIM), dtype=jnp.float32) * s, 'b2': jnp.zeros((OUT_DIM,), dtype=jnp.float32)}
    _L0_gnn_all = _L0_gnn_setup()
    _L0_gnn_in = {k: v for k, v in _L0_gnn_all.items() if k in ('We', 'be', 'W1', 'b1', 'W2', 'b2')}
    del _L0_gnn_all

    def _L1_gnn_setup():
        import jax, jax.numpy as jnp
        import numpy as np
        N, E, IN_DIM, HID, HEADS, LAYERS = (6250, 40000, 128, 128, 4, 2)
        C = HID // HEADS
        EPS = 1e-05

        def _init(key, shape, fan_in):
            return jax.random.normal(key, shape, dtype=jnp.float32) / np.sqrt(fan_in)

        def _transformer_conv(h, src, tgt, edge_attr, Wq, bq, Wk, bk, Wv, bv, We, Wskip, bskip, Wbeta):
            n = h.shape[0]
            q = (h @ Wq + bq).reshape(n, HEADS, C)
            k = (h @ Wk + bk).reshape(n, HEADS, C)
            v = (h @ Wv + bv).reshape(n, HEADS, C)
            e = (edge_attr @ We).reshape(-1, HEADS, C)
            k_j = k[src] + e
            alpha = jnp.einsum('ehc,ehc->eh', q[tgt], k_j) / jnp.sqrt(jnp.float32(C))
            amax = jax.ops.segment_max(alpha, tgt, num_segments=n)
            ex = jnp.exp(alpha - amax[tgt])
            denom = jax.ops.segment_sum(ex, tgt, num_segments=n)
            a = ex / denom[tgt]
            msg = (v[src] + e) * a[..., None]
            out = jax.ops.segment_sum(msg, tgt, num_segments=n).reshape(n, HID)
            x_r = h @ Wskip + bskip
            beta = jax.nn.sigmoid(jnp.concatenate([out, x_r, out - x_r], axis=-1) @ Wbeta)
            return beta * x_r + (1.0 - beta) * out

        def _batchnorm(h, gamma, beta):
            mu = h.mean(axis=0)
            var = h.var(axis=0)
            return gamma * (h - mu) * jax.lax.rsqrt(var + EPS) + beta
        key = jax.random.key(seed)
        ks = jax.random.split(key, 20)
        x = jax.random.normal(ks[0], (N, IN_DIM), dtype=jnp.float32)
        edge_index = jax.random.randint(ks[1], (2, E), 0, N, dtype=jnp.int64)
        edge_attr = jax.random.uniform(ks[2], (E, 1), dtype=jnp.float32)
        inp = {'x': x, 'edge_index': edge_index, 'edge_attr': edge_attr, 'W_in': _init(ks[3], (IN_DIM, HID), IN_DIM), 'b_in': jnp.zeros((HID,), jnp.float32), 'Wq': _init(ks[4], (LAYERS, HID, HID), HID), 'bq': jnp.zeros((LAYERS, HID), jnp.float32), 'Wk': _init(ks[5], (LAYERS, HID, HID), HID), 'bk': jnp.zeros((LAYERS, HID), jnp.float32), 'Wv': _init(ks[6], (LAYERS, HID, HID), HID), 'bv': jnp.zeros((LAYERS, HID), jnp.float32), 'We': _init(ks[7], (LAYERS, 1, HID), 1), 'Wskip': _init(ks[8], (LAYERS, HID, HID), HID), 'bskip': jnp.zeros((LAYERS, HID), jnp.float32), 'Wbeta': _init(ks[9], (LAYERS, 3 * HID, 1), 3 * HID), 'bn_gamma': jnp.ones((LAYERS, HID), jnp.float32), 'bn_beta': jnp.zeros((LAYERS, HID), jnp.float32)}
        return inp
    _L1_gnn_all = _L1_gnn_setup()
    _L1_gnn_in = {k: v for k, v in _L1_gnn_all.items() if k in ('W_in', 'b_in', 'Wq', 'bq', 'Wk', 'bk', 'Wv', 'bv', 'We', 'Wskip', 'bskip', 'Wbeta', 'bn_gamma', 'bn_beta')}
    del _L1_gnn_all

    def _L2_gnn_setup():
        import jax, jax.numpy as jnp
        import numpy as np
        N_NODES = 6250
        N_EDGES = 50000
        LATENT = 128
        HIDDEN = 512
        N_HEADS = 2
        HEAD_DIM = LATENT // N_HEADS
        N_GRAPHS = 500
        LN_EPS = 1e-05

        def _layer_norm(x, scale, bias):
            mu = jnp.mean(x, axis=-1, keepdims=True)
            var = jnp.mean(jnp.square(x - mu), axis=-1, keepdims=True)
            return (x - mu) * jax.lax.rsqrt(var + LN_EPS) * scale + bias

        def _node_attn(q, k, ea, index, n_nodes, w1, b1, w2, w3, b3):
            h = jax.nn.leaky_relu(jnp.concatenate([q, k, ea], axis=-1) @ w1 + b1, 0.2)
            h = h.reshape(-1, N_HEADS, HEAD_DIM)
            logits = jnp.einsum('ehd,hd->eh', h, w2)
            m = jax.ops.segment_max(logits, index, num_segments=n_nodes)
            m = jnp.where(jnp.isfinite(m), m, 0.0)
            e = jnp.exp(logits - m[index])
            z = jax.ops.segment_sum(e, index, num_segments=n_nodes)
            alpha = e / (z[index] + 1e-16)
            v = (jnp.concatenate([k, ea], axis=-1) @ w3 + b3).reshape(-1, N_HEADS, HEAD_DIM)
            out = jax.ops.segment_sum(alpha[..., None] * v, index, num_segments=n_nodes)
            return out.reshape(n_nodes, LATENT)
        key = jax.random.key(seed)
        ks = jax.random.split(key, 24)
        s = 0.02
        inp = {'edges': jax.random.randint(ks[0], (2, N_EDGES), 0, N_NODES, dtype=jnp.int32), 'node_feat': jax.random.normal(ks[1], (N_NODES, LATENT), jnp.float32), 'edge_attr': jax.random.normal(ks[2], (N_EDGES, LATENT), jnp.float32), 'u': jax.random.normal(ks[3], (N_GRAPHS, LATENT), jnp.float32), 'num_nodes': jnp.full((N_GRAPHS,), N_NODES // N_GRAPHS, jnp.int32), 'w1': jax.random.normal(ks[4], (3 * LATENT, LATENT), jnp.float32) * s, 'b1': jnp.zeros((LATENT,), jnp.float32), 'w2': jax.random.normal(ks[5], (N_HEADS, HEAD_DIM), jnp.float32) * s, 'w3': jax.random.normal(ks[6], (2 * LATENT, LATENT), jnp.float32) * s, 'b3': jnp.zeros((LATENT,), jnp.float32), 'mw0': jax.random.normal(ks[7], (4 * LATENT, HIDDEN), jnp.float32) * s, 'mb0': jnp.zeros((HIDDEN,), jnp.float32), 'ls0': jnp.ones((HIDDEN,), jnp.float32), 'lb0': jnp.zeros((HIDDEN,), jnp.float32), 'mw1': jax.random.normal(ks[8], (HIDDEN, HIDDEN), jnp.float32) * s, 'mb1': jnp.zeros((HIDDEN,), jnp.float32), 'ls1': jnp.ones((HIDDEN,), jnp.float32), 'lb1': jnp.zeros((HIDDEN,), jnp.float32), 'mw2': jax.random.normal(ks[9], (HIDDEN, LATENT), jnp.float32) * s, 'mb2': jnp.zeros((LATENT,), jnp.float32)}
        return inp
    _L2_gnn_all = _L2_gnn_setup()
    _L2_gnn_in = {k: v for k, v in _L2_gnn_all.items() if k in ('u', 'num_nodes', 'w1', 'b1', 'w2', 'w3', 'b3', 'mw0', 'mb0', 'ls0', 'lb0', 'mw1', 'mb1', 'ls1', 'lb1', 'mw2', 'mb2')}
    del _L2_gnn_all

    def _L3_gnn_setup():
        import jax, jax.numpy as jnp
        import numpy as np
        N_NODES = 6250
        N_EDGES = 75000
        HID = 128
        key = jax.random.key(seed)
        ks = jax.random.split(key, 10)
        s = 1.0 / np.sqrt(HID)
        s2 = 1.0 / np.sqrt(2 * HID)
        return {'h': jax.random.normal(ks[0], (N_NODES, HID), dtype=jnp.float32), 'edge_index': jax.random.randint(ks[1], (2, N_EDGES), 0, N_NODES, dtype=jnp.int64), 'e_w1': jax.random.uniform(ks[2], (HID, HID), jnp.float32, -s, s), 'e_b1': jax.random.uniform(ks[3], (HID,), jnp.float32, -s, s), 'e_w2': jax.random.uniform(ks[4], (HID, HID), jnp.float32, -s, s), 'e_b2': jax.random.uniform(ks[5], (HID,), jnp.float32, -s, s), 'n_w1': jax.random.uniform(ks[6], (2 * HID, HID), jnp.float32, -s2, s2), 'n_b1': jax.random.uniform(ks[7], (HID,), jnp.float32, -s2, s2), 'n_w2': jax.random.uniform(ks[8], (HID, HID), jnp.float32, -s, s), 'n_b2': jax.random.uniform(ks[9], (HID,), jnp.float32, -s, s)}
    _L3_gnn_all = _L3_gnn_setup()
    _L3_gnn_in = {k: v for k, v in _L3_gnn_all.items() if k in ('e_w1', 'e_b1', 'e_w2', 'e_b2', 'n_w1', 'n_b1', 'n_w2', 'n_b2')}
    del _L3_gnn_all
    return {'x': x, 'src': src, 'dst': dst, 'edge_attr_128': edge_attr_128, 'edge_weight1': edge_weight1, 'L0_gnn_We': _L0_gnn_in['We'], 'L0_gnn_be': _L0_gnn_in['be'], 'L0_gnn_W1': _L0_gnn_in['W1'], 'L0_gnn_b1': _L0_gnn_in['b1'], 'L0_gnn_W2': _L0_gnn_in['W2'], 'L0_gnn_b2': _L0_gnn_in['b2'], 'L1_gnn_W_in': _L1_gnn_in['W_in'], 'L1_gnn_b_in': _L1_gnn_in['b_in'], 'L1_gnn_Wq': _L1_gnn_in['Wq'], 'L1_gnn_bq': _L1_gnn_in['bq'], 'L1_gnn_Wk': _L1_gnn_in['Wk'], 'L1_gnn_bk': _L1_gnn_in['bk'], 'L1_gnn_Wv': _L1_gnn_in['Wv'], 'L1_gnn_bv': _L1_gnn_in['bv'], 'L1_gnn_We': _L1_gnn_in['We'], 'L1_gnn_Wskip': _L1_gnn_in['Wskip'], 'L1_gnn_bskip': _L1_gnn_in['bskip'], 'L1_gnn_Wbeta': _L1_gnn_in['Wbeta'], 'L1_gnn_bn_gamma': _L1_gnn_in['bn_gamma'], 'L1_gnn_bn_beta': _L1_gnn_in['bn_beta'], 'L2_gnn_u': _L2_gnn_in['u'], 'L2_gnn_num_nodes': _L2_gnn_in['num_nodes'], 'L2_gnn_w1': _L2_gnn_in['w1'], 'L2_gnn_b1': _L2_gnn_in['b1'], 'L2_gnn_w2': _L2_gnn_in['w2'], 'L2_gnn_w3': _L2_gnn_in['w3'], 'L2_gnn_b3': _L2_gnn_in['b3'], 'L2_gnn_mw0': _L2_gnn_in['mw0'], 'L2_gnn_mb0': _L2_gnn_in['mb0'], 'L2_gnn_ls0': _L2_gnn_in['ls0'], 'L2_gnn_lb0': _L2_gnn_in['lb0'], 'L2_gnn_mw1': _L2_gnn_in['mw1'], 'L2_gnn_mb1': _L2_gnn_in['mb1'], 'L2_gnn_ls1': _L2_gnn_in['ls1'], 'L2_gnn_lb1': _L2_gnn_in['lb1'], 'L2_gnn_mw2': _L2_gnn_in['mw2'], 'L2_gnn_mb2': _L2_gnn_in['mb2'], 'L3_gnn_e_w1': _L3_gnn_in['e_w1'], 'L3_gnn_e_b1': _L3_gnn_in['e_b1'], 'L3_gnn_e_w2': _L3_gnn_in['e_w2'], 'L3_gnn_e_b2': _L3_gnn_in['e_b2'], 'L3_gnn_n_w1': _L3_gnn_in['n_w1'], 'L3_gnn_n_b1': _L3_gnn_in['n_b1'], 'L3_gnn_n_w2': _L3_gnn_in['n_w2'], 'L3_gnn_n_b2': _L3_gnn_in['n_b2']}

def reference(x, src, dst, edge_attr_128, edge_weight1, L0_gnn_We, L0_gnn_be, L0_gnn_W1, L0_gnn_b1, L0_gnn_W2, L0_gnn_b2, L1_gnn_W_in, L1_gnn_b_in, L1_gnn_Wq, L1_gnn_bq, L1_gnn_Wk, L1_gnn_bk, L1_gnn_Wv, L1_gnn_bv, L1_gnn_We, L1_gnn_Wskip, L1_gnn_bskip, L1_gnn_Wbeta, L1_gnn_bn_gamma, L1_gnn_bn_beta, L2_gnn_u, L2_gnn_num_nodes, L2_gnn_w1, L2_gnn_b1, L2_gnn_w2, L2_gnn_w3, L2_gnn_b3, L2_gnn_mw0, L2_gnn_mb0, L2_gnn_ls0, L2_gnn_lb0, L2_gnn_mw1, L2_gnn_mb1, L2_gnn_ls1, L2_gnn_lb1, L2_gnn_mw2, L2_gnn_mb2, L3_gnn_e_w1, L3_gnn_e_b1, L3_gnn_e_w2, L3_gnn_e_b2, L3_gnn_n_w1, L3_gnn_n_b1, L3_gnn_n_w2, L3_gnn_n_b2):
    import jax
    import jax.numpy as jnp

    def _L0_gnn_ref(x, edge_index, edge_attr, We, be, W1, b1, W2, b2):
        import jax, jax.numpy as jnp
        import numpy as np
        N, E = (1250, 80000)
        IN_DIM, EDGE_DIM, OUT_DIM = (128, 128, 128)
        src, dst = (edge_index[0], edge_index[1])
        num_nodes = x.shape[0]
        edge_emb = edge_attr @ We + be
        edge_agg = jax.ops.segment_sum(edge_emb, dst, num_segments=num_nodes)
        x_comb = jnp.concatenate([x, edge_agg], axis=-1)
        neigh = jax.ops.segment_sum(x_comb[src], dst, num_segments=num_nodes)
        h = x_comb + neigh
        return jax.nn.relu(h @ W1 + b1) @ W2 + b2

    def _L1_gnn_ref(x, edge_index, edge_attr, W_in, b_in, Wq, bq, Wk, bk, Wv, bv, We, Wskip, bskip, Wbeta, bn_gamma, bn_beta):
        import jax, jax.numpy as jnp
        import numpy as np
        N, E, IN_DIM, HID, HEADS, LAYERS = (6250, 40000, 128, 128, 4, 2)
        C = HID // HEADS
        EPS = 1e-05

        def _init(key, shape, fan_in):
            return jax.random.normal(key, shape, dtype=jnp.float32) / np.sqrt(fan_in)

        def _transformer_conv(h, src, tgt, edge_attr, Wq, bq, Wk, bk, Wv, bv, We, Wskip, bskip, Wbeta):
            n = h.shape[0]
            q = (h @ Wq + bq).reshape(n, HEADS, C)
            k = (h @ Wk + bk).reshape(n, HEADS, C)
            v = (h @ Wv + bv).reshape(n, HEADS, C)
            e = (edge_attr @ We).reshape(-1, HEADS, C)
            k_j = k[src] + e
            alpha = jnp.einsum('ehc,ehc->eh', q[tgt], k_j) / jnp.sqrt(jnp.float32(C))
            amax = jax.ops.segment_max(alpha, tgt, num_segments=n)
            ex = jnp.exp(alpha - amax[tgt])
            denom = jax.ops.segment_sum(ex, tgt, num_segments=n)
            a = ex / denom[tgt]
            msg = (v[src] + e) * a[..., None]
            out = jax.ops.segment_sum(msg, tgt, num_segments=n).reshape(n, HID)
            x_r = h @ Wskip + bskip
            beta = jax.nn.sigmoid(jnp.concatenate([out, x_r, out - x_r], axis=-1) @ Wbeta)
            return beta * x_r + (1.0 - beta) * out

        def _batchnorm(h, gamma, beta):
            mu = h.mean(axis=0)
            var = h.var(axis=0)
            return gamma * (h - mu) * jax.lax.rsqrt(var + EPS) + beta
        src, tgt = (edge_index[0], edge_index[1])
        h = jax.nn.relu(x @ W_in + b_in)
        for l in range(LAYERS):
            h_res = h
            h = _transformer_conv(h, src, tgt, edge_attr, Wq[l], bq[l], Wk[l], bk[l], Wv[l], bv[l], We[l], Wskip[l], bskip[l], Wbeta[l])
            h = jax.nn.relu(_batchnorm(h, bn_gamma[l], bn_beta[l]))
            h = h + h_res
        return h

    def _L2_gnn_ref(edges, node_feat, edge_attr, u, num_nodes, w1, b1, w2, w3, b3, mw0, mb0, ls0, lb0, mw1, mb1, ls1, lb1, mw2, mb2):
        import jax, jax.numpy as jnp
        import numpy as np
        N_NODES = 6250
        N_EDGES = 50000
        LATENT = 128
        HIDDEN = 512
        N_HEADS = 2
        HEAD_DIM = LATENT // N_HEADS
        N_GRAPHS = 500
        LN_EPS = 1e-05

        def _layer_norm(x, scale, bias):
            mu = jnp.mean(x, axis=-1, keepdims=True)
            var = jnp.mean(jnp.square(x - mu), axis=-1, keepdims=True)
            return (x - mu) * jax.lax.rsqrt(var + LN_EPS) * scale + bias

        def _node_attn(q, k, ea, index, n_nodes, w1, b1, w2, w3, b3):
            h = jax.nn.leaky_relu(jnp.concatenate([q, k, ea], axis=-1) @ w1 + b1, 0.2)
            h = h.reshape(-1, N_HEADS, HEAD_DIM)
            logits = jnp.einsum('ehd,hd->eh', h, w2)
            m = jax.ops.segment_max(logits, index, num_segments=n_nodes)
            m = jnp.where(jnp.isfinite(m), m, 0.0)
            e = jnp.exp(logits - m[index])
            z = jax.ops.segment_sum(e, index, num_segments=n_nodes)
            alpha = e / (z[index] + 1e-16)
            v = (jnp.concatenate([k, ea], axis=-1) @ w3 + b3).reshape(-1, N_HEADS, HEAD_DIM)
            out = jax.ops.segment_sum(alpha[..., None] * v, index, num_segments=n_nodes)
            return out.reshape(n_nodes, LATENT)
        n = node_feat.shape[0]
        row, col = (edges[0], edges[1])
        sent = _node_attn(node_feat[row], node_feat[col], edge_attr, row, n, w1, b1, w2, w3, b3)
        recv = _node_attn(node_feat[col], node_feat[row], edge_attr, col, n, w1, b1, w2, w3, b3)
        glob = jnp.repeat(u, num_nodes, axis=0, total_repeat_length=n)
        x = jnp.concatenate([node_feat, sent, recv, glob], axis=1)
        h = jax.nn.relu(_layer_norm(x @ mw0 + mb0, ls0, lb0))
        h = jax.nn.relu(_layer_norm(h @ mw1 + mb1, ls1, lb1))
        return h @ mw2 + mb2

    def _L3_gnn_ref(h, edge_index, e_w1, e_b1, e_w2, e_b2, n_w1, n_b1, n_w2, n_b2):
        import jax, jax.numpy as jnp
        import numpy as np
        N_NODES = 6250
        N_EDGES = 75000
        HID = 128
        row, col = (edge_index[0], edge_index[1])
        diff = h[row] - h[col]
        e = jax.nn.relu(diff @ e_w1 + e_b1) @ e_w2 + e_b2
        agg = jax.ops.segment_sum(e, row, num_segments=h.shape[0])
        z = jnp.concatenate([h, agg], axis=1)
        out = jax.nn.relu(z @ n_w1 + n_b1) @ n_w2 + n_b2
        return out
    edge_index = jnp.stack([src, dst])
    h = jnp.maximum(_layernorm(x, axis=-1), 0.0)
    x = x + _L0_gnn_ref(h, edge_index, edge_attr_128, L0_gnn_We, L0_gnn_be, L0_gnn_W1, L0_gnn_b1, L0_gnn_W2, L0_gnn_b2)
    h = jnp.maximum(_layernorm(x, axis=-1), 0.0)
    x = x + _L1_gnn_ref(h, edge_index, edge_weight1, L1_gnn_W_in, L1_gnn_b_in, L1_gnn_Wq, L1_gnn_bq, L1_gnn_Wk, L1_gnn_bk, L1_gnn_Wv, L1_gnn_bv, L1_gnn_We, L1_gnn_Wskip, L1_gnn_bskip, L1_gnn_Wbeta, L1_gnn_bn_gamma, L1_gnn_bn_beta)
    h = jnp.maximum(_layernorm(x, axis=-1), 0.0)
    x = x + _L2_gnn_ref(edge_index, h, edge_attr_128, L2_gnn_u, L2_gnn_num_nodes, L2_gnn_w1, L2_gnn_b1, L2_gnn_w2, L2_gnn_w3, L2_gnn_b3, L2_gnn_mw0, L2_gnn_mb0, L2_gnn_ls0, L2_gnn_lb0, L2_gnn_mw1, L2_gnn_mb1, L2_gnn_ls1, L2_gnn_lb1, L2_gnn_mw2, L2_gnn_mb2)
    h = jnp.maximum(_layernorm(x, axis=-1), 0.0)
    x = x + _L3_gnn_ref(h, edge_index, L3_gnn_e_w1, L3_gnn_e_b1, L3_gnn_e_w2, L3_gnn_e_b2, L3_gnn_n_w1, L3_gnn_n_b1, L3_gnn_n_w2, L3_gnn_n_b2)
    return x

_drawn_inputs = setup_inputs


def setup_inputs(seed=0):
    import zlib

    import numpy as np

    out = dict(_drawn_inputs(seed))
    spreads = {'L0_gnn_be': (0.0, 0.1),
     'L0_gnn_b1': (0.0, 0.7),
     'L0_gnn_b2': (0.0, 0.1),
     'L1_gnn_b_in': (0.0, 0.1),
     'L1_gnn_bq': (0.0, 0.8),
     'L1_gnn_bk': (0.0, 0.8),
     'L1_gnn_bv': (0.0, 0.315),
     'L1_gnn_bskip': (0.0, 0.313),
     'L1_gnn_bn_gamma': (1.0, 0.2),
     'L1_gnn_bn_beta': (0.0, 0.1),
     'L2_gnn_b1': (0.0, 0.8),
     'L2_gnn_b3': (0.0, 0.539),
     'L2_gnn_mb0': (0.0, 0.1),
     'L2_gnn_ls0': (1.0, 0.562),
     'L2_gnn_lb0': (0.0, 0.579),
     'L2_gnn_mb1': (0.0, 0.1),
     'L2_gnn_ls1': (1.0, 0.566),
     'L2_gnn_lb1': (0.0, 0.62),
     'L2_gnn_mb2': (0.0, 0.1)}
    factors = {'L2_gnn_w1': 8.0,
     'L2_gnn_w2': 8.0,
     'L2_gnn_w3': 2.871,
     'L3_gnn_e_b1': 2.69,
     'L3_gnn_n_b1': 8.0}
    for name, (base, spread) in spreads.items():
        noise = np.random.default_rng([zlib.crc32(name.encode()), seed]).standard_normal(out[name].shape)
        drawn = base * np.exp(spread * noise) if base else spread * noise
        out[name] = jnp.asarray(drawn.astype(out[name].dtype))
    for name, factor in factors.items():
        out[name] = (out[name] * factor).astype(out[name].dtype)
    return out
```

```python
from contextlib import ExitStack

import concourse.bass as bass
from concourse import mybir

F32 = mybir.dt.float32
I32 = mybir.dt.int32
BF16 = mybir.dt.bfloat16
ALU = mybir.AluOpType
ACT = mybir.ActivationFunctionType
AX = mybir.AxisListType

P = 128
NODES, EDGES, D = 6250, 106250, 128
NT = -(-NODES // P)
LAST = NODES - (NT - 1) * P
G = 4
NG = -(-NT // G)
NTG = NG * G
COLS = EDGES // P
REST = EDGES - COLS * P
TILES = (EDGES + NT * (P - 1)) // P
GROUPS = -(-TILES // (2 * G)) * 2
TILES = GROUPS * G
SLOTS = TILES * P
SPARE = TILES - (EDGES // P + 1) + 1
EB = 5
assert COLS % (2 * EB) == 0
REC = 4
ROW = REC + 3 * D + REC
DROW, SROW0 = REC + 3 * D, REC + D
SROW = ROW - SROW0
HEADS1, HEADS2 = 4, 2
BIG = 1.0e30
EPS = 1e-5
SLOPE = 0.2
ACCW = 136


class Steps:

    def __init__(self, eng, sem, base=0):
        self.eng, self.sem, self.base, self.n = eng, sem, base, 0

    def mark(self, ins):
        ins.then_inc(self.sem, 1)
        self.n += 1
        return self.n

    def need(self, n):
        self.eng.wait_ge(self.sem, self.base + n)

    def link(self, ins):
        self.need(self.mark(ins))


class Count:

    def __init__(self, pool, name):
        self.pool, self.reg = pool, pool.alloc_register(name)
        pool.reg_mov(self.reg, 0)

    def step(self, n):
        self.pool.reg_add(self.reg, self.reg, n)

    def wait(self, sem):
        self.pool.wait_ge(sem, self.reg)


def rows_of(ap):
    return ap.rearrange("(o n) -> o n", o=1)


class Kit:

    def __init__(self, nc, ctx):
        self.nc = nc

        def sb(name, shape, dt=F32):
            return ctx.enter_context(nc.sbuf_tensor(name, shape, dt))

        self.ident = sb("ident", [P, P])
        self.neg_ident = sb("neg_ident", [P, P])
        self.ident4_bf = sb("ident4_bf", [P, G, P], BF16)
        self.ones = sb("ones", [P, P])
        self.before = sb("before", [P, P])
        self.node_of_col = sb("node_of_col", [P, P])
        self.part = sb("part", [P, 1])
        self.acc = sb("acc", [P, NTG, ACCW])
        self.rec_d = sb("rec_d", [P, TILES, REC])
        self.rec_s = sb("rec_s", [P, TILES, REC])
        self.tile_d = sb("tile_d", [1, TILES], I32)
        self.tile_s = sb("tile_s", [1, TILES], I32)
        self.bank = [ctx.enter_context(nc.psum_tensor(f"bank{b}", [P, 512], F32)) for b in range(8)]

        def dram(name, shape, dt=F32):
            return nc.dram_tensor(name, shape, dt, kind="Internal").ap()

        self.rows_d = dram("rows_by_dst", (SLOTS, DROW))
        self.rows_s = dram("rows_by_src", (SLOTS, SROW))
        self.dram = dram


class Phase:

    def __init__(self, kit, name):
        self.kit, self.name = kit, name

    def __enter__(self):
        self.ctx = ExitStack()
        self.nc = self.kit.nc
        self.sems = []
        return self

    def sb(self, name, shape, dt=F32):
        return self.ctx.enter_context(self.nc.sbuf_tensor(f"{self.name}_{name}", shape, dt))

    def sem(self, name):
        self.sems.append(self.nc.alloc_semaphore(name=f"{self.name}_{name}"))
        return self.sems[-1]

    def block(self):
        return self.ctx.enter_context(self.nc.Block())

    def __exit__(self, *exc):
        self.ctx.__exit__(*exc)
        if self.sems and exc[0] is None:
            self.nc.clear_and_free_semaphores(self.sems)
            self.nc.all_engine_barrier()


def constants(kit):
    nc = kit.nc
    with Phase(kit, "const") as ph:
        filled, made, col_i = ph.sem("filled"), ph.sem("made"), ph.sem("col_i")
        cast = ph.sem("cast")
        col_int = ph.sb("col_int", [P, P], I32)
        part_int = ph.sb("part_int", [P, 1], I32)
        block = ph.block()

        @block.gpsimd
        def _(pool):
            pool.memset(kit.ident[:, :], 0.0).then_inc(filled, 1)
            pool.memset(kit.neg_ident[:, :], 0.0).then_inc(filled, 1)
            pool.memset(kit.ones[:, :], 1.0).then_inc(filled, 1)
            pool.iota(col_int[:, :], pattern=[[1, P]], base=0, channel_multiplier=0).then_inc(col_i, 1)
            pool.iota(part_int[:, :], pattern=[[1, 1]], base=0, channel_multiplier=1).then_inc(col_i, 1)
            pool.wait_ge(filled, 3)
            pool.affine_select(out=kit.ident[:, :], in_=kit.ident[:, :], compare_op=ALU.not_equal, fill=1.0,
                               base=0, pattern=[[-1, P]], channel_multiplier=1).then_inc(made, 1)
            pool.affine_select(out=kit.neg_ident[:, :], in_=kit.neg_ident[:, :], compare_op=ALU.not_equal,
                               fill=-1.0, base=0, pattern=[[-1, P]], channel_multiplier=1).then_inc(made, 1)
            pool.affine_select(out=kit.before[:, :], in_=kit.ones[:, :], compare_op=ALU.is_gt, fill=0.0,
                               base=0, pattern=[[1, P]], channel_multiplier=-1).then_inc(made, 1)

        @block.vector
        def _(dve):
            dve.wait_ge(col_i, 2)
            nc.vector.tensor_copy(kit.node_of_col[:, :], col_int[:, :])
            nc.vector.tensor_copy(kit.part[:, :], part_int[:, :])
            dve.wait_ge(made, 3)
            nc.vector.tensor_copy(kit.ident4_bf[:, :, :], kit.ident[:, :].unsqueeze(1).broadcast_to([P, G, P])).then_inc(cast, 1)
            dve.wait_ge(cast, 1)


def sort_positions(kit, ins, pos_d, pos_s, pads_d, pads_s, recs_d, recs_s):
    nc = kit.nc
    with Phase(kit, "sort") as ph:
        key = [ph.sb("key_d", [P, COLS + 1], I32), ph.sb("key_s", [P, COLS + 1], I32)]
        low = ph.sb("low", [P, COLS + 1], I32)
        bucket = ph.sb("bucket", [P, COLS + 1])
        here = ph.sb("here", [P, COLS + 1])
        count = ph.sb("count", [P, COLS + 1])
        rank = ph.sb("rank", [P, COLS + 1])
        weight = ph.sb("weight", [P, COLS + 1])
        one = ph.sb("one", [P, COLS + 1])
        total = ph.sb("total", [P, NT])
        size = ph.sb("size", [P, NT])
        size_i = ph.sb("size_i", [P, NT], I32)
        tiles_of = ph.sb("tiles_of", [P, NT])
        ends = ph.sb("ends", [P, NT])
        start = ph.sb("start", [P, NT])
        base = ph.sb("base", [P, NT])
        bucket_no = ph.sb("bucket_no", [P, NT])
        pad = ph.sb("pad", [P, NT + SPARE])
        limit = ph.sb("limit", [P, NT + SPARE])
        tile_no = ph.sb("tile_no", [1, TILES])
        tile_of = ph.sb("tile_of", [1, TILES])
        tile_int = ph.sb("tile_int", [1, TILES], I32)
        cleared, loaded = ph.sem("cleared"), ph.sem("loaded")
        numbered = ph.sem("numbered")
        step, totals, summed = ph.sem("step"), ph.sem("totals"), ph.sem("summed")
        block = ph.block()

        def main(ap):
            return ap[0:COLS * P].rearrange("(p c) -> p c", c=COLS)

        def rest(ap):
            return ap[COLS * P:EDGES].rearrange("(p c) -> p c", c=1)

        @block.sync
        def _(sp):
            sp.wait_ge(cleared, 1)
            weights = ins["edge_weight1"].rearrange("e o -> (e o)")
            for out, src in ((key[0], ins["dst"]), (key[1], ins["src"]), (weight, weights)):
                sp.dma_start(out[:, 0:COLS], main(src)).then_inc(loaded, 16)
                sp.dma_start(out[0:REST, COLS:COLS + 1], rest(src)).then_inc(loaded, 16)

        @block.gpsimd
        def _(pool):
            pool.iota(tile_int[:, :], pattern=[[1, TILES]], base=0, channel_multiplier=0).then_inc(numbered, 1)

        @block.tensor
        def _(pe):
            for k in range(2):
                pe.wait_ge(totals, k + 1)
                nc.tensor.matmul(kit.bank[0][:, 0:NT], kit.before[:, :], total[:, :], start=True, stop=True)
                nc.tensor.matmul(kit.bank[1][:, 0:NT], kit.ones[:, :], total[:, :], start=True, stop=True)\
                    .then_inc(summed, 1)

        @block.vector
        def _(dve):
            s = Steps(dve, step)
            nc.vector.memset(key[0][:, COLS:COLS + 1], -P)
            nc.vector.memset(weight[:, COLS:COLS + 1], 0.0)
            nc.vector.memset(one[:, :], 1.0)
            s.link(nc.vector.memset(key[1][:, COLS:COLS + 1], -P))
            nc.vector.tensor_copy(bucket_no[:, :], kit.node_of_col[:, 0:NT]).then_inc(cleared, 1)
            dve.wait_ge(numbered, 1)
            s.link(nc.vector.tensor_copy(tile_no[:, :], tile_int[:, :]))
            dve.wait_ge(loaded, 6 * 16)
            for k, (pos, pads, recs, tab) in enumerate(((pos_d, pads_d, recs_d, kit.tile_d),
                                                        (pos_s, pads_s, recs_s, kit.tile_s))):
                s.link(nc.vector.tensor_single_scalar(low[:, :], key[k][:, :], P - 1, ALU.bitwise_and))
                s.mark(nc.vector.tensor_copy(recs[:, :, 0], low[:, :]))
                s.mark(nc.vector.tensor_copy(recs[:, :, 1], key[1 - k][:, :]))
                s.mark(nc.vector.tensor_copy(recs[:, :, 2], weight[:, :]))
                s.mark(nc.vector.memset(recs[:, :, 3], 0.0))
                s.mark(nc.vector.memset(rank[:, :], 0.0))
                s.need(s.n)
                s.link(nc.vector.tensor_single_scalar(low[:, :], key[k][:, :], P.bit_length() - 1, ALU.arith_shift_right))
                s.link(nc.vector.tensor_copy(bucket[:, :], low[:, :]))
                at = s.n
                with dve.Fori(0, NT) as b:
                    t = Steps(dve, step, at + 5 * b)
                    t.link(nc.vector.tensor_scalar(here[:, :], bucket[:, :], bucket_no[:, bass.ds(b, 1)], None, ALU.is_equal))
                    t.link(nc.vector.tensor_tensor_scan(count[:, :], one[:, :], here[:, :], 0.0, ALU.mult, ALU.add))
                    t.link(nc.vector.tensor_copy(total[:, bass.ds(b, 1)], count[:, COLS:COLS + 1]))
                    t.link(nc.vector.tensor_tensor(here[:, :], here[:, :], count[:, :], ALU.mult))
                    t.link(nc.vector.tensor_tensor(rank[:, :], rank[:, :], here[:, :], ALU.add))
                s.n = at + 5 * NT
                nc.vector.memset(tile_of[:, :], 0.0).then_inc(totals, 1)
                dve.wait_ge(summed, k + 1)
                s.link(nc.vector.tensor_scalar(size[:, :], kit.bank[1][:, 0:NT], float(P - 1), None, ALU.add))
                s.link(nc.vector.tensor_copy(size_i[:, :], size[:, :]))
                s.link(nc.vector.tensor_single_scalar(size_i[:, :], size_i[:, :], P.bit_length() - 1, ALU.arith_shift_right))
                s.link(nc.vector.tensor_copy(tiles_of[:, :], size_i[:, :]))
                s.link(nc.vector.tensor_tensor_scan(ends[:, :], one[:, 0:NT], tiles_of[:, :], 0.0, ALU.mult, ALU.add))
                s.link(nc.vector.tensor_tensor(start[:, :], ends[:, :], tiles_of[:, :], ALU.subtract))
                s.link(nc.vector.tensor_scalar(start[:, :], start[:, :], float(P), None, ALU.mult))
                s.link(nc.vector.scalar_tensor_tensor(out=base[:, :], in0=start[:, :], scalar=-1.0,
                                                      in1=kit.bank[0][:, 0:NT], op0=ALU.add, op1=ALU.add))
                at = s.n
                with dve.Fori(0, NT) as b:
                    t = Steps(dve, step, at + 2 * b)
                    t.link(nc.vector.tensor_scalar(here[:, :], bucket[:, :], bucket_no[:, bass.ds(b, 1)],
                                                   base[:, bass.ds(b, 1)], ALU.is_equal, ALU.mult))
                    t.link(nc.vector.tensor_tensor(rank[:, :], rank[:, :], here[:, :], ALU.add))
                s.n = at + 2 * NT
                s.link(nc.vector.tensor_copy(pos[:, :], rank[:, :]))
                s.link(nc.vector.tensor_tensor(pad[:, 0:NT], start[:, :], kit.bank[1][:, 0:NT], ALU.add))
                s.link(nc.vector.tensor_scalar(limit[:, 0:NT], ends[:, :], float(P), None, ALU.mult))
                s.link(nc.vector.tensor_scalar(pad[:, NT:], kit.node_of_col[:, 0:SPARE], ends[:, NT - 1:NT], float(P), ALU.add, ALU.mult))
                s.link(nc.vector.memset(limit[:, NT:], float(SLOTS)))
                s.link(nc.vector.tensor_scalar(pad[:, :], pad[:, :], kit.part[:, :], None, ALU.add))
                s.link(nc.vector.tensor_tensor(limit[:, :], pad[:, :], limit[:, :], ALU.is_ge))
                s.link(nc.vector.scalar_tensor_tensor(out=pad[:, :], in0=limit[:, :], scalar=float(SLOTS), in1=pad[:, :],
                                                      op0=ALU.mult, op1=ALU.add))
                s.link(nc.vector.tensor_copy(pads[:, :], pad[:, :]))
                at = s.n
                with dve.Fori(0, NT - 1) as b:
                    t = Steps(dve, step, at + b)
                    t.link(nc.vector.scalar_tensor_tensor(out=tile_of[:, :], in0=tile_no[:, :], scalar=ends[0:1, bass.ds(b, 1)],
                                                          in1=tile_of[:, :], op0=ALU.is_ge, op1=ALU.add))
                s.n = at + NT - 1
                s.link(nc.vector.tensor_copy(tab[:, :], tile_of[:, :]))


def scatter_edges(kit, ins, pos_d, pos_s, pads_d, pads_s, recs_d, recs_s):
    nc = kit.nc
    STEPS = COLS // (2 * EB)
    with Phase(kit, "scat") as ph:
        w_edge = ph.sb("w_edge", [P, 2 * D])
        row = [ph.sb(f"row{u}", [P, EB, ROW]) for u in range(2)]
        idx = [ph.sb(f"idx{u}", [P, 2, EB], I32) for u in range(2)]
        attr_t = [ph.sb(f"attr_t{u}", [P, 3, P]) for u in range(2)]
        zero = ph.sb("zero", [P, ROW])
        rest_row = ph.sb("rest_row", [P, ROW])
        w_in = ph.sem("w_in")
        attr_in = [ph.sem(f"attr_in{u}") for u in range(2)]
        turned = ph.sem("turned")
        copied = ph.sem("copied")
        made = ph.sem("made")
        filled = ph.sem("filled")
        recs_in = [ph.sem(f"recs_in{u}") for u in range(2)]
        idx_in = ph.sem("idx_in")
        gone = [ph.sem(f"gone{u}") for u in range(2)]
        pads_gone, rest_in, cleared = ph.sem("pads_gone"), ph.sem("rest_in"), ph.sem("cleared")
        rest_done = ph.sem("rest_done")
        rest_gone = ph.sem("rest_gone")
        rest_turned, rest_copied, rest_made = ph.sem("rest_turned"), ph.sem("rest_copied"), ph.sem("rest_made")
        idx_order = ph.sem("idx_order")
        block = ph.block()
        attr = ins["edge_attr_128"][0:COLS * P, :].rearrange("(p c) f -> p c f", c=COLS)

        @block.sync
        def _(sp):
            sp.dma_start(w_edge[:, 0:D], ins["L2_gnn_w1"][2 * D:3 * D, :]).then_inc(w_in, 16)
            sp.dma_start(w_edge[:, D:], ins["L2_gnn_w3"][D:2 * D, :]).then_inc(w_in, 16)
            sp.wait_ge(cleared, 1)
            sp.dma_start(rest_row[0:REST, REC:REC + D], ins["edge_attr_128"][COLS * P:EDGES, :]).then_inc(rest_in, 16)
            with sp.Fori(0, STEPS) as it:
                for u in range(2):
                    sp.wait_ge(gone[u], it * (2 * EB * 16))
                    sp.dma_start(row[u][:, :, REC:REC + D], attr[:, bass.ds((it * 2 + u) * EB, EB), :])\
                        .then_inc(attr_in[u], 16)

        @block.tensor
        def _(pe):
            pe.wait_ge(w_in, 32)
            pe.wait_ge(rest_in, 16)
            nc.tensor.transpose(kit.bank[7][:, 0:P], rest_row[:, REC:REC + D], kit.ident[:, :]).then_inc(rest_turned, 1)
            pe.wait_ge(rest_copied, 1)
            nc.tensor.matmul(kit.bank[7][:, 0:2 * D], attr_t[0][:, 0, :], w_edge[:, :], start=True, stop=True)\
                .then_inc(rest_made, 1)
            pe.wait_ge(rest_done, 1)
            with pe.Fori(0, STEPS) as it:
                for u in range(2):
                    pe.wait_ge(attr_in[u], (it + 1) * 16)
                    for half, (c0, n) in enumerate(((0, 3), (3, 2))):
                        t = kit.bank[half]
                        pe.wait_ge(copied, it * 4 + 2 * u + half)
                        for c in range(n):
                            last = nc.tensor.transpose(t[:, c * P:(c + 1) * P], row[u][:, c0 + c, REC:REC + D], kit.ident[:, :])
                        last.then_inc(turned, 1)
                        pe.wait_ge(copied, it * 4 + 2 * u + half + 1)
                        pe.wait_ge(filled, it * 4 + 2 * u + half)
                        for c in range(n):
                            b = kit.bank[2 + 2 * half + c // 2]
                            last = nc.tensor.matmul(b[:, (c % 2) * 2 * D:(c % 2 + 1) * 2 * D], attr_t[half][:, c, :], w_edge[:, :],
                                                    start=True, stop=True)
                        last.then_inc(made, 1)

        @block.scalar
        def _(act):
            act.wait_ge(rest_turned, 1)
            nc.scalar.copy(attr_t[0][:, 0, :], kit.bank[7][:, 0:P]).then_inc(rest_copied, 1)
            act.wait_ge(rest_done, 1)
            with act.Fori(0, STEPS) as it:
                for u in range(2):
                    for half, n in enumerate((3, 2)):
                        act.wait_ge(turned, it * 4 + 2 * u + half + 1)
                        nc.scalar.copy(attr_t[half][:, 0:n, :], kit.bank[half][:, 0:n * P].rearrange("p (c e) -> p c e", c=n))\
                            .then_inc(copied, 1)

        @block.vector
        def _(dve):
            nc.vector.memset(rest_row[:, :], 0.0).then_inc(cleared, 1)
            nc.vector.memset(zero[:, :], 0.0).then_inc(cleared, 1)
            dve.wait_ge(cleared, 2)
            nc.vector.memset(zero[:, 0:1], -1.0).then_inc(cleared, 1)
            nc.vector.memset(zero[:, ROW - REC:ROW - REC + 1], -1.0).then_inc(cleared, 1)
            dve.wait_ge(rest_in, 16)
            nc.vector.tensor_copy(rest_row[:, 0:REC], recs_d[:, COLS, :])
            nc.vector.tensor_copy(rest_row[:, ROW - REC:], recs_s[:, COLS, :])
            dve.wait_ge(rest_made, 1)
            nc.vector.tensor_copy(rest_row[:, SROW0:SROW0 + 2 * D], kit.bank[7][:, 0:2 * D]).then_inc(rest_done, 1)
            with dve.Fori(0, STEPS) as it:
                for u in range(2):
                    dve.wait_ge(gone[u], it * (2 * EB * 16))
                    nc.vector.tensor_copy(row[u][:, :, 0:REC], recs_d[:, bass.ds((it * 2 + u) * EB, EB), :]).then_inc(recs_in[u], 1)
                    nc.vector.tensor_copy(row[u][:, :, ROW - REC:], recs_s[:, bass.ds((it * 2 + u) * EB, EB), :]).then_inc(recs_in[u], 1)
                    for half, (c0, n) in enumerate(((0, 3), (3, 2))):
                        dve.wait_ge(made, it * 4 + 2 * u + half + 1)
                        for b in range((n + 1) // 2):
                            m = min(2, n - 2 * b)
                            last = nc.vector.tensor_copy(
                                row[u][:, c0 + 2 * b:c0 + 2 * b + m, SROW0:SROW0 + 2 * D],
                                kit.bank[2 + 2 * half + b][:, 0:m * 2 * D].rearrange("p (c f) -> p c f", c=m))
                        last.then_inc(filled, 1)

        @block.gpsimd
        def _(pool):
            def scatter(src, index, n, done, skip=False):
                for table, lo, hi, k in ((kit.rows_d, 0, DROW, 0), (kit.rows_s, SROW0, ROW, 1)):
                    pool.indirect_dma_start(
                        out=table[:, :], out_offset=bass.IndirectOffsetOnAxis(ap=index[k], axis=0),
                        in_=src[0:n, lo:hi], in_offset=None,
                        **(dict(bounds_check=SLOTS - 1, oob_is_err=False) if skip else {})).then_inc(done, 16)

            pool.wait_ge(rest_done, 1)
            scatter(rest_row, (pos_d[0:REST, COLS:COLS + 1], pos_s[0:REST, COLS:COLS + 1]), REST, rest_gone)
            pool.wait_ge(cleared, 4)
            for c in range(NT + SPARE):
                scatter(zero, (pads_d[:, c:c + 1], pads_s[:, c:c + 1]), P, pads_gone, skip=True)
            idx_ready = Count(pool, "idx_ready")
            recs_ready = [Count(pool, f"recs_ready{u}") for u in range(2)]
            products_ready = Count(pool, "products_ready")
            with pool.Fori(0, STEPS) as it:
                for u in range(2):
                    pool.wait_ge(gone[u], it * (2 * EB * 16))
                    pool.tensor_copy(idx[u][:, 0, :], pos_d[:, bass.ds((it * 2 + u) * EB, EB)]).then_inc(idx_in, 1)
                    pool.tensor_copy(idx[u][:, 1, :], pos_s[:, bass.ds((it * 2 + u) * EB, EB)]).then_inc(idx_in, 1)
                    for count in (idx_ready, recs_ready[u], products_ready):
                        count.step(2)
                    pool.wait_ge(rest_done, 1)
                    idx_ready.wait(idx_in)
                    recs_ready[u].wait(recs_in[u])
                    products_ready.wait(filled)
                    for c in range(EB):
                        scatter(row[u][:, c, :], (idx[u][:, 0, c:c + 1], idx[u][:, 1, c:c + 1]), P, gone[u])
            for u in range(2):
                pool.wait_ge(gone[u], STEPS * 2 * EB * 16)
            pool.wait_ge(pads_gone, 2 * 16 * (NT + SPARE))
            pool.wait_ge(rest_gone, 32)


ITERS = GROUPS // 2


def side(kit, by_src):
    return (kit.rec_s, kit.tile_s, kit.rows_s) if by_src else (kit.rec_d, kit.tile_d, kit.rows_d)


def tile_rows(ap, first, n):
    return ap[bass.ds(first * P, n * P), :].rearrange("(c p) f -> p c f", p=P)


def load_records(kit, name):
    nc = kit.nc
    with Phase(kit, name) as ph:
        done = ph.sem("done")
        block = ph.block()

        @block.sync
        def _(sp):
            sp.dma_start(kit.rec_d[:, :, :], kit.rows_d[:, 0:REC].rearrange("(c p) f -> p c f", p=P)).then_inc(done, 16)
            sp.dma_start(kit.rec_s[:, :, :], kit.rows_s[:, SROW - REC:SROW].rearrange("(c p) f -> p c f", p=P)).then_inc(done, 16)
            sp.wait_ge(done, 32)


def make_one_hot(kit, dve, oh, rec, first):
    return kit.nc.vector.tensor_tensor(
        oh[:, :, :], kit.node_of_col[:, :].unsqueeze(1).broadcast_to([P, G, P]),
        rec[:, bass.ds(first, G), 0:1].broadcast_to([P, G, P]), ALU.is_equal)


def add_sums(kit, dve, tab, it, u, banks, width, added):
    nc = kit.nc
    for c in range(G):
        t = dve.value_load(tab[0:1, bass.ds((it * 2 + u) * G + c, 1)], min_val=0, max_val=NT - 1)
        if c:
            dve.wait_ge(added[u], it * G + c)
        else:
            dve.wait_ge(added[1 - u], (it + u) * G)
        into = kit.acc[:, bass.ds(t, 1), 0:width].rearrange("p o w -> p (o w)")
        nc.vector.tensor_tensor(into, into, kit.bank[banks[c // 2]][:, (c % 2) * ACCW:(c % 2) * ACCW + width], ALU.add)\
            .then_inc(added[u], 1)


def sum_pass(kit, name, by_src, rows=None, table=None, own=None):
    nc = kit.nc
    rec, tab, sorted_rows = side(kit, by_src)
    W = D + 1
    with Phase(kit, name) as ph:
        oh = [ph.sb(f"oh{u}", [P, G, P]) for u in range(2)]
        x = [ph.sb(f"x{u}", [P, G, W]) for u in range(2)]
        idx = [ph.sb(f"idx{u}", [P, G], I32) for u in range(2)]
        if own is not None:
            gat = [ph.sb(f"gat{u}", [P, G, D]) for u in range(2)]
            oht = [ph.sb(f"oht{u}", [P, G, P]) for u in range(2)]
        else:
            gat = x
        ready = ph.sem("ready")
        oh_in = [ph.sem(f"oh_in{u}") for u in range(2)]
        x_in = [ph.sem(f"x_in{u}") for u in range(2)]
        idx_in = ph.sem("idx_in")
        summed = [ph.sem(f"summed{u}") for u in range(2)]
        added = [ph.sem(f"added{u}") for u in range(2)]
        step = ph.sem("step")
        if own is not None:
            turned = [ph.sem(f"turned{u}") for u in range(2)]
            oht_in = [ph.sem(f"oht_in{u}") for u in range(2)]
            diff = [ph.sem(f"diff{u}") for u in range(2)]
            relued = [ph.sem(f"relued{u}") for u in range(2)]
        block = ph.block()

        @block.vector
        def _(dve):
            s = Steps(dve, step)
            for u in range(2):
                s.mark(nc.vector.memset(x[u][:, :, D:W], 1.0))
            s.mark(nc.vector.memset(kit.acc[:, :, :], 0.0))
            s.need(s.n)
            nc.vector.engine_nop().then_inc(ready, 1)
            with dve.Fori(0, ITERS) as it:
                for u in range(2):
                    dve.wait_ge(summed[u], it)
                    if own is not None:
                        dve.wait_ge(turned[u], it)
                    make_one_hot(kit, dve, oh[u], rec, (it * 2 + u) * G).then_inc(oh_in[u], 1)
                for u in range(2):
                    dve.wait_ge(summed[u], it + 1)
                    add_sums(kit, dve, tab, it, u, (2 * u, 2 * u + 1), W, added)

        @block.tensor
        def _(pe):
            pe.wait_ge(ready, 1)
            with pe.Fori(0, ITERS) as it:
                if own is not None:
                    for u in range(2):
                        pe.wait_ge(oh_in[u], it + 1)
                        pe.wait_ge(oht_in[u], it)
                        for c in range(G):
                            last = nc.tensor.transpose(kit.bank[4 + u][:, c * P:(c + 1) * P], oh[u][:, c, :], kit.ident[:, :])
                        last.then_inc(turned[u], 1)
                    for u in range(2):
                        pe.wait_ge(oht_in[u], it + 1)
                        pe.wait_ge(x_in[u], (it + 1) * (16 * G))
                        pe.wait_ge(relued[u], it)
                        nc.tensor.matmul(kit.bank[6 + u][:, :], kit.neg_ident[:, :], gat[u][:, :, :], start=True, stop=False)
                        for c in range(G):
                            t = pe.value_load(tab[0:1, bass.ds((it * 2 + u) * G + c, 1)], min_val=0, max_val=NT - 1)
                            last = nc.tensor.matmul(kit.bank[6 + u][:, c * P:(c + 1) * P], oht[u][:, c, :],
                                                    own[:, bass.ds(t, 1), :].rearrange("p o f -> p (o f)"), start=False, stop=c == G - 1)
                        last.then_inc(diff[u], 1)
                for u in range(2):
                    if own is not None:
                        pe.wait_ge(relued[u], it + 1)
                    else:
                        pe.wait_ge(oh_in[u], it + 1)
                        pe.wait_ge(x_in[u], (it + 1) * (16 if rows is not None else 16 * G))
                    pe.wait_ge(added[u], it * G)
                    for c in range(G):
                        last = nc.tensor.matmul(kit.bank[2 * u + c // 2][:, (c % 2) * ACCW:(c % 2) * ACCW + W],
                                                oh[u][:, c, :], x[u][:, c, :], start=True, stop=True)
                    last.then_inc(summed[u], 1)

        if own is not None:
            @block.scalar
            def _(act):
                with act.Fori(0, ITERS) as it:
                    for u in range(2):
                        act.wait_ge(turned[u], it + 1)
                        act.wait_ge(diff[u], it)
                        nc.scalar.copy(oht[u][:, :, :], kit.bank[4 + u][:, :].rearrange("p (c e) -> p c e", c=G)).then_inc(oht_in[u], 1)
                    for u in range(2):
                        act.wait_ge(diff[u], it + 1)
                        act.wait_ge(summed[u], it)
                        nc.scalar.activation(x[u][:, :, 0:D], kit.bank[6 + u][:, :].rearrange("p (c e) -> p c e", c=G), ACT.Relu)\
                            .then_inc(relued[u], 1)

        if rows is not None:
            @block.sync
            def _(sp):
                with sp.Fori(0, ITERS) as it:
                    for u in range(2):
                        sp.wait_ge(summed[u], it)
                        sp.dma_start(x[u][:, :, 0:D], tile_rows(sorted_rows[:, rows:rows + D], (it * 2 + u) * G, G)).then_inc(x_in[u], 16)
        else:
            @block.gpsimd
            def _(pool):
                idx_count = Count(pool, name + "_idx")
                x_free = [Count(pool, f"{name}_x_free{u}") for u in range(2)]
                pool.wait_ge(ready, 1)
                with pool.Fori(0, ITERS) as it:
                    for u in range(2):
                        free = diff[u] if own is not None else summed[u]
                        pool.wait_ge(x_in[u], it * (16 * G))
                        pool.tensor_copy(idx[u][:, :], rec[:, bass.ds((it * 2 + u) * G, G), 1]).then_inc(idx_in, 1)
                        idx_count.step(1)
                        pool.wait_ge(ready, 1)
                        idx_count.wait(idx_in)
                        x_free[u].wait(free)
                        for c in range(G):
                            pool.indirect_dma_start(
                                out=gat[u][:, c, 0:D], out_offset=None, in_=table,
                                in_offset=bass.IndirectOffsetOnAxis(ap=idx[u][:, c:c + 1], axis=0)).then_inc(x_in[u], 16)
                        x_free[u].step(1)


def score_pass(kit, name, by_src, layer, table, v_rows, own, alpha, node_max, extra):
    nc = kit.nc
    rec, tab, sorted_rows = side(kit, by_src)
    H = HEADS1 if layer == 1 else HEADS2
    C = D // H
    CHUNK = 512 // (H * P)
    CHUNKS = G // CHUNK
    first_col = DROW - 2 * D if not by_src else 0

    def max_bank(u, q):
        return (1, 4, 5, 6)[q if layer == 1 else 2 * u + q]

    def bank_uses(it, u):
        return it * 2 + u if layer == 1 else it

    with Phase(kit, name) as ph:
        oh = [ph.sb(f"oh{u}", [P, G, P]) for u in range(2)]
        oht = [ph.sb(f"oht{u}", [P, G, P]) for u in range(2)]
        out_of = [ph.sb(f"out_of{u}", [P, G, P], BF16) for u in range(2)]
        gat = [ph.sb(f"gat{u}", [P, G, 2 * D]) for u in range(2)]
        prod = [ph.sb(f"prod{u}", [P, G, D]) for u in range(2)]
        logit = [ph.sb(f"logit{u}", [P, G, H]) for u in range(2)]
        most = [ph.sb(f"most{u}", [P, G, H]) for u in range(2)]
        idx = [ph.sb(f"idx{u}", [P, G], I32) for u in range(2)]
        if layer == 1:
            term = [ph.sb(f"term{u}", [P, G, H]) for u in range(2)]
            value = [g[:, :, D:2 * D] for g in gat]
        else:
            edge = [ph.sb(f"edge{u}", [P, G, 2 * D]) for u in range(2)]
            act_out = [ph.sb(f"act_out{u}", [P, G, D]) for u in range(2)]
            value_sb = [ph.sb(f"value{u}", [P, G, D]) for u in range(2)]
            value = [v[:, :, :] for v in value_sb]
        ready = ph.sem("ready")
        oh_in = [ph.sem(f"oh_in{u}") for u in range(2)]
        gat_in = [ph.sem(f"gat_in{u}") for u in range(2)]
        idx_in = ph.sem("idx_in")
        turned = [ph.sem(f"turned{u}") for u in range(2)]
        oht_in = [ph.sem(f"oht_in{u}") for u in range(2)]
        out_in = [ph.sem(f"out_in{u}") for u in range(2)]
        spread = [ph.sem(f"spread{u}") for u in range(2)]
        multiplied = [ph.sem(f"multiplied{u}") for u in range(2)]
        reduced = ph.sem("reduced")
        scored = [ph.sem(f"scored{u}") for u in range(2)]
        kept = [ph.sem(f"kept{u}") for u in range(2)]
        lined = [[ph.sem(f"lined{u}_{q}") for q in range(CHUNKS)] for u in range(2)]
        found = [ph.sem(f"found{u}") for u in range(2)]
        maxed = [ph.sem(f"maxed{u}") for u in range(2)]
        kept_v = [ph.sem(f"kept_v{u}") for u in range(2)]
        if layer == 1:
            termed = ph.sem("termed")
        else:
            edge_in = [ph.sem(f"edge_in{u}") for u in range(2)]
            valued = [ph.sem(f"valued{u}") for u in range(2)]
            value_in = [ph.sem(f"value_in{u}") for u in range(2)]
            leaked = [ph.sem(f"leaked{u}") for u in range(2)]
            hidden = [ph.sem(f"hidden{u}") for u in range(2)]
        block = ph.block()

        @block.vector
        def _(dve):
            nc.vector.memset(node_max[:, :, :], -BIG).then_inc(ready, 1)
            dve.wait_ge(ready, 1)
            with dve.Fori(0, ITERS) as it:
                for u in range(2):
                    dve.wait_ge(turned[u], it)
                    dve.wait_ge(out_in[u], it)
                    make_one_hot(kit, dve, oh[u], rec, (it * 2 + u) * G).then_inc(oh_in[u], 1)
                for u in range(2):
                    if layer == 1:
                        dve.wait_ge(spread[u], it + 1)
                        dve.wait_ge(gat_in[u], (it + 1) * (16 * G))
                        nc.vector.tensor_tensor(prod[u][:, :, :], kit.bank[2 + u][:, :].rearrange("p (c f) -> p c f", c=G),
                                                gat[u][:, :, 0:D], ALU.mult).then_inc(multiplied[u], 1)
                        nc.vector.tensor_tensor(term[u][:, :, :], kit.bank[7][:, 0:G * H].rearrange("p (c h) -> p c h", c=G),
                                                rec[:, bass.ds((it * 2 + u) * G, G), 2:3].broadcast_to([P, G, H]), ALU.mult).then_inc(termed, 1)
                    else:
                        dve.wait_ge(leaked[u], it + 1)
                        nc.vector.scalar_tensor_tensor(out=act_out[u][:, :, :], in0=kit.bank[2 + u][:, :].rearrange("p (c f) -> p c f", c=G),
                                                       scalar=SLOPE, in1=act_out[u][:, :, :], op0=ALU.mult, op1=ALU.add).then_inc(hidden[u], 1)
                        dve.wait_ge(hidden[u], it + 1)
                        nc.vector.tensor_tensor(prod[u][:, :, :], act_out[u][:, :, :], extra[:, :].unsqueeze(1).broadcast_to([P, G, D]),
                                                ALU.mult).then_inc(multiplied[u], 1)
                    dve.wait_ge(multiplied[u], it + 1)
                    dve.wait_ge(kept[u], it)
                    dve.wait_ge(lined[u][CHUNKS - 1], it)
                    sums = nc.vector.tensor_reduce(out=logit[u][:, :, :], in_=prod[u][:, :, :].rearrange("p c (h f) -> p c h f", h=H),
                                                   axis=AX.X, op=ALU.add)
                    if layer == 1:
                        sums.then_inc(reduced, 1)
                        dve.wait_ge(termed, it * 2 + u + 1)
                        dve.wait_ge(reduced, it * 2 + u + 1)
                        nc.vector.tensor_tensor(logit[u][:, :, :], logit[u][:, :, :], term[u][:, :, :], ALU.add).then_inc(scored[u], 1)
                    else:
                        sums.then_inc(scored[u], 1)
                for u in range(2):
                    for q in range(CHUNKS):
                        dve.wait_ge(lined[u][q], it + 1)
                        nc.vector.tensor_reduce(out=most[u][:, q * CHUNK:(q + 1) * CHUNK, :].rearrange("p c h -> p (c h)"),
                                                in_=kit.bank[max_bank(u, q)][:, :].rearrange("p (c e) -> p c e", e=P),
                                                axis=AX.X, op=ALU.max).then_inc(found[u], 1)
                    dve.wait_ge(found[u], (it + 1) * CHUNKS)
                    for c in range(G):
                        t = dve.value_load(tab[0:1, bass.ds((it * 2 + u) * G + c, 1)], min_val=0, max_val=NT - 1)
                        if c:
                            dve.wait_ge(maxed[u], it * G + c)
                        else:
                            dve.wait_ge(maxed[1 - u], (it + u) * G)
                        into = node_max[:, bass.ds(t, 1), 0:H].rearrange("p o w -> p (o w)")
                        nc.vector.tensor_tensor(into, into, most[u][:, c, :], ALU.max).then_inc(maxed[u], 1)

        @block.tensor
        def _(pe):
            with pe.Fori(0, ITERS) as it:
                for u in range(2):
                    pe.wait_ge(oh_in[u], it + 1)
                    pe.wait_ge(oht_in[1 - u], it + u)
                    for c in range(G):
                        last = nc.tensor.transpose(kit.bank[0][:, c * P:(c + 1) * P], oh[u][:, c, :], kit.ident[:, :])
                    last.then_inc(turned[u], 1)
                for u in range(2):
                    pe.wait_ge(oht_in[u], it + 1)
                    if layer == 1:
                        pe.wait_ge(multiplied[u], it)
                    else:
                        pe.wait_ge(hidden[u], it)
                        pe.wait_ge(gat_in[u], (it + 1) * (16 * G))
                        pe.wait_ge(edge_in[u], (it + 1) * 16)
                        nc.tensor.matmul(kit.bank[2 + u][:, :], kit.ident[:, :], gat[u][:, :, 0:D], start=True, stop=False)
                        nc.tensor.matmul(kit.bank[2 + u][:, :], kit.ident[:, :], edge[u][:, :, 0:D], start=False, stop=False)
                    tiles = [pe.value_load(tab[0:1, bass.ds((it * 2 + u) * G + c, 1)], min_val=0, max_val=NT - 1) for c in range(G)]
                    for c, t in enumerate(tiles):
                        last = nc.tensor.matmul(kit.bank[2 + u][:, c * P:(c + 1) * P], oht[u][:, c, :],
                                                own[:, bass.ds(t, 1), :].rearrange("p o f -> p (o f)"),
                                                start=layer == 1, stop=layer == 1 or c == G - 1)
                    if layer == 1:
                        pe.wait_ge(scored[1 - u], it + u)
                        for c, t in enumerate(tiles):
                            last = nc.tensor.matmul(kit.bank[7][:, c * H:(c + 1) * H], oht[u][:, c, :],
                                                    extra[:, bass.ds(t, 1), :].rearrange("p o f -> p (o f)"), start=True, stop=True)
                    last.then_inc(spread[u], 1)
                    if layer == 2:
                        pe.wait_ge(value_in[1 - u], it + u)
                        nc.tensor.matmul(kit.bank[7][:, :], kit.ident[:, :], gat[u][:, :, D:2 * D], start=True, stop=False)
                        nc.tensor.matmul(kit.bank[7][:, :], kit.ident[:, :], edge[u][:, :, D:2 * D], start=False, stop=True)\
                            .then_inc(valued[u], 1)
                for u in range(2):
                    pe.wait_ge(scored[u], it + 1)
                    pe.wait_ge(out_in[u], it + 1)
                    for q in range(CHUNKS):
                        b = kit.bank[max_bank(u, q)]
                        if layer == 1:
                            pe.wait_ge(found[1 - u], (it + u) * CHUNKS)
                        else:
                            pe.wait_ge(found[u], it * CHUNKS)
                        for k in range(CHUNK):
                            c = q * CHUNK + k
                            nc.tensor.matmul(b[:, k * H * P:(k + 1) * H * P], out_of[u][:, c, :], kit.ident4_bf[:, 0:H, :], start=True, stop=False)
                            for h in range(H):
                                o = (k * H + h) * P
                                last = nc.tensor.matmul(b[:, o:o + P], logit[u][:, c, h:h + 1].broadcast_to([P, P]), kit.ident[:, :],
                                                        start=False, stop=h == H - 1)
                        last.then_inc(lined[u][q], 1)

        @block.scalar
        def _(act):
            with act.Fori(0, ITERS) as it:
                for u in range(2):
                    act.wait_ge(turned[u], it + 1)
                    act.wait_ge(spread[u], it)
                    nc.scalar.copy(oht[u][:, :, :], kit.bank[0][:, :].rearrange("p (c e) -> p c e", c=G)).then_inc(oht_in[u], 1)
                    act.wait_ge(lined[u][CHUNKS - 1], it)
                    nc.scalar.activation(out_of[u][:, :, :], oh[u][:, :, :], ACT.Copy, bias=-BIG, scale=BIG).then_inc(out_in[u], 1)
                if layer == 2:
                    for u in range(2):
                        act.wait_ge(spread[u], it + 1)
                        act.wait_ge(multiplied[u], it)
                        nc.scalar.activation(act_out[u][:, :, :], kit.bank[2 + u][:, :].rearrange("p (c e) -> p c e", c=G), ACT.Relu,
                                             scale=1.0 - SLOPE).then_inc(leaked[u], 1)
                        act.wait_ge(valued[u], it + 1)
                        act.wait_ge(kept_v[u], it * 16)
                        nc.scalar.copy(value[u], kit.bank[7][:, :].rearrange("p (c e) -> p c e", c=G)).then_inc(value_in[u], 1)
                for u in range(2):
                    act.wait_ge(scored[u], it + 1)
                    nc.scalar.copy(alpha[:, bass.ds((it * 2 + u) * G, G), 0:H], logit[u][:, :, :]).then_inc(kept[u], 1)

        @block.sync
        def _(sp):
            with sp.Fori(0, ITERS) as it:
                if layer == 2:
                    for u in range(2):
                        sp.wait_ge(valued[u], it)
                        sp.dma_start(edge[u][:, :, :], tile_rows(sorted_rows[:, first_col:first_col + 2 * D], (it * 2 + u) * G, G))\
                            .then_inc(edge_in[u], 16)
                for u in range(2):
                    first = sp.snap((it * 2 + u) * (G * D), min_val=0, max_val=(TILES - G) * D)
                    if layer == 1:
                        sp.wait_ge(gat_in[u], (it + 1) * (16 * G))
                    else:
                        sp.wait_ge(value_in[u], it + 1)
                    sp.dma_start(v_rows.rearrange("p c f -> p (c f)")[:, bass.ds(first, G * D)].rearrange("p (c f) -> p c f", f=D), value[u]).then_inc(kept_v[u], 16)
            for u in range(2):
                sp.wait_ge(kept_v[u], ITERS * 16)

        @block.gpsimd
        def _(pool):
            idx_count = Count(pool, name + "_idx")
            turn = Count(pool, name + "_turn")
            kept_count = Count(pool, name + "_kept")
            with pool.Fori(0, ITERS) as it:
                for u in range(2):
                    pool.wait_ge(gat_in[u], it * (16 * G))
                    pool.tensor_copy(idx[u][:, :], rec[:, bass.ds((it * 2 + u) * G, G), 1]).then_inc(idx_in, 1)
                    idx_count.step(1)
                    pool.wait_ge(ready, 1)
                    idx_count.wait(idx_in)
                    if layer == 1:
                        turn.wait(multiplied[u])
                        kept_count.wait(kept_v[u])
                    else:
                        turn.wait(valued[u])
                    for c in range(G):
                        pool.indirect_dma_start(
                            out=gat[u][:, c, :], out_offset=None, in_=table,
                            in_offset=bass.IndirectOffsetOnAxis(ap=idx[u][:, c:c + 1], axis=0)).then_inc(gat_in[u], 16)
                turn.step(1)
                kept_count.step(16)


def weigh_pass(kit, name, by_src, layer, v_rows, alpha, node_max):
    nc = kit.nc
    rec, tab, _ = side(kit, by_src)
    H = HEADS1 if layer == 1 else HEADS2
    C = D // H
    W = D + 2 * H if layer == 1 else D + H
    with Phase(kit, name) as ph:
        oh = [ph.sb(f"oh{u}", [P, G, P]) for u in range(2)]
        oht = [ph.sb(f"oht{u}", [P, G, P]) for u in range(2)]
        value = [ph.sb(f"value{u}", [P, G, D]) for u in range(2)]
        w = [ph.sb(f"w{u}", [P, G, W]) for u in range(2)]
        below = [ph.sb(f"below{u}", [P, G, H]) for u in range(2)]
        ready = ph.sem("ready")
        oh_in = [ph.sem(f"oh_in{u}") for u in range(2)]
        turned = [ph.sem(f"turned{u}") for u in range(2)]
        oht_in = [ph.sem(f"oht_in{u}") for u in range(2)]
        spread = [ph.sem(f"spread{u}") for u in range(2)]
        less = ph.sem("less")
        capped = [ph.sem(f"capped{u}") for u in range(2)]
        raised = [ph.sem(f"raised{u}") for u in range(2)]
        value_in = [ph.sem(f"value_in{u}") for u in range(2)]
        weighed = [ph.sem(f"weighed{u}") for u in range(2)]
        summed = [ph.sem(f"summed{u}") for u in range(2)]
        added = [ph.sem(f"added{u}") for u in range(2)]
        PARTS = 2 if layer == 1 else 1
        block = ph.block()

        @block.vector
        def _(dve):
            nc.vector.memset(kit.acc[:, :, :], 0.0).then_inc(ready, 1)
            dve.wait_ge(ready, 1)
            with dve.Fori(0, ITERS) as it:
                for u in range(2):
                    dve.wait_ge(summed[u], it)
                    make_one_hot(kit, dve, oh[u], rec, (it * 2 + u) * G).then_inc(oh_in[u], 1)
                for u in range(2):
                    dve.wait_ge(spread[u], it + 1)
                    dve.wait_ge(raised[u], it)
                    nc.vector.tensor_tensor(below[u][:, :, :], alpha[:, bass.ds((it * 2 + u) * G, G), 0:H],
                                            kit.bank[6 + u][:, 0:G * H].rearrange("p (c h) -> p c h", c=G), ALU.subtract).then_inc(less, 1)
                    dve.wait_ge(less, it * 2 + u + 1)
                    nc.vector.tensor_scalar(below[u][:, :, :], below[u][:, :, :], 0.0, None, ALU.min).then_inc(capped[u], 1)
                for u in range(2):
                    dve.wait_ge(raised[u], it + 1)
                    dve.wait_ge(value_in[u], (it + 1) * 16)
                    if layer == 1:
                        nc.vector.tensor_tensor(w[u][:, :, D + H:W], w[u][:, :, D:D + H],
                                                rec[:, bass.ds((it * 2 + u) * G, G), 2:3].broadcast_to([P, G, H]), ALU.mult).then_inc(weighed[u], 1)
                    nc.vector.tensor_tensor(w[u][:, :, 0:D].rearrange("p c (h f) -> p c h f", h=H),
                                            value[u][:, :, :].rearrange("p c (h f) -> p c h f", h=H),
                                            w[u][:, :, D:D + H].unsqueeze(3).broadcast_to([P, G, H, C]), ALU.mult).then_inc(weighed[u], 1)
                for u in range(2):
                    dve.wait_ge(summed[u], it + 1)
                    add_sums(kit, dve, tab, it, u, (2 * u, 2 * u + 1), W, added)

        @block.tensor
        def _(pe):
            with pe.Fori(0, ITERS) as it:
                for u in range(2):
                    pe.wait_ge(oh_in[u], it + 1)
                    pe.wait_ge(oht_in[u], it)
                    for c in range(G):
                        last = nc.tensor.transpose(kit.bank[4 + u][:, c * P:(c + 1) * P], oh[u][:, c, :], kit.ident[:, :])
                    last.then_inc(turned[u], 1)
                for u in range(2):
                    pe.wait_ge(oht_in[u], it + 1)
                    pe.wait_ge(capped[u], it)
                    for c in range(G):
                        t = pe.value_load(tab[0:1, bass.ds((it * 2 + u) * G + c, 1)], min_val=0, max_val=NT - 1)
                        last = nc.tensor.matmul(kit.bank[6 + u][:, c * H:(c + 1) * H], oht[u][:, c, :],
                                                node_max[:, bass.ds(t, 1), 0:H].rearrange("p o f -> p (o f)"), start=True, stop=True)
                    last.then_inc(spread[u], 1)
                for u in range(2):
                    pe.wait_ge(weighed[u], (it + 1) * PARTS)
                    pe.wait_ge(added[u], it * G)
                    for c in range(G):
                        last = nc.tensor.matmul(kit.bank[2 * u + c // 2][:, (c % 2) * ACCW:(c % 2) * ACCW + W],
                                                oh[u][:, c, :], w[u][:, c, :], start=True, stop=True)
                    last.then_inc(summed[u], 1)

        @block.scalar
        def _(act):
            with act.Fori(0, ITERS) as it:
                for u in range(2):
                    act.wait_ge(turned[u], it + 1)
                    act.wait_ge(spread[u], it)
                    nc.scalar.copy(oht[u][:, :, :], kit.bank[4 + u][:, :].rearrange("p (c e) -> p c e", c=G)).then_inc(oht_in[u], 1)
                for u in range(2):
                    act.wait_ge(capped[u], it + 1)
                    act.wait_ge(summed[u], it)
                    nc.scalar.activation(w[u][:, :, D:D + H], below[u][:, :, :], ACT.Exp).then_inc(raised[u], 1)

        @block.sync
        def _(sp):
            with sp.Fori(0, ITERS) as it:
                for u in range(2):
                    sp.wait_ge(weighed[u], it * PARTS)
                    sp.dma_start(value[u][:, :, :], v_rows[:, bass.ds((it * 2 + u) * G, G), :]).then_inc(value_in[u], 16)


class Norm:

    def __init__(self, kit, ph, groups, width, tag="norm"):
        self.kit, self.width, self.groups = kit, width, groups
        self.sq = ph.sb(f"{tag}_sq", [P, groups, width])
        self.mean = ph.sb(f"{tag}_mean", [P, groups])
        self.var = ph.sb(f"{tag}_var", [P, groups])
        self.std = ph.sb(f"{tag}_std", [P, groups])
        self.inv = ph.sb(f"{tag}_inv", [P, groups])
        self.asked, self.rooted = ph.sem(f"{tag}_asked"), ph.sem(f"{tag}_rooted")

    def wide(self, ap):
        return ap[:, :].unsqueeze(2).broadcast_to([P, self.groups, self.width])

    def on_vector(self, dve, s, x, out, turn, scale=None, shift=None):
        v, n = self.kit.nc.vector, self.width
        s.link(v.tensor_reduce(out=self.mean[:, :], in_=x, axis=AX.X, op=ALU.add))
        s.link(v.tensor_scalar(self.mean[:, :], self.mean[:, :], 1.0 / n, None, ALU.mult))
        s.link(v.tensor_tensor(out, x, self.wide(self.mean), ALU.subtract))
        s.link(v.tensor_tensor(self.sq[:, :, :], out, out, ALU.mult))
        s.link(v.tensor_reduce(out=self.var[:, :], in_=self.sq[:, :, :], axis=AX.X, op=ALU.add))
        v.tensor_scalar(self.var[:, :], self.var[:, :], 1.0 / n, EPS, ALU.mult, ALU.add).then_inc(self.asked, 1)
        dve.wait_ge(self.rooted, turn)
        s.link(v.reciprocal(self.inv[:, :], self.std[:, :]))
        s.link(v.tensor_tensor(out, out, self.wide(self.inv), ALU.mult))
        if scale is not None:
            s.link(v.tensor_tensor(out, out, scale, ALU.mult))
            s.link(v.tensor_tensor(out, out, shift, ALU.add))
        s.link(v.tensor_scalar(out, out, 0.0, None, ALU.max))

    def on_scalar(self, act, turn):
        act.wait_ge(self.asked, turn)
        self.kit.nc.scalar.activation(self.std[:, :], self.var[:, :], ACT.Sqrt).then_inc(self.rooted, 1)


NORM_STEPS = 8


def node_pass(kit, name, loads, sources, weights, outputs, stores, scratch=(), wide=(), before=None, after=None,
              norm_before=False, norm_after=False, steps=0):
    nc = kit.nc
    wide = dict(wide)
    biases = {f"bias{o}": b for o, (_, b) in enumerate(outputs) if b is not None}
    with Phase(kit, name) as ph:
        t = {n: ph.sb(n, [P, G, D]) for n in {**loads, **{x: 0 for x in scratch}}}
        t.update({n: ph.sb(n, [P, D]) for n in weights})
        t.update({n: ph.sb(n, [P, D]) for n in wide})
        t.update({n: ph.sb(n, [1, D]) for n in biases})
        src_t = [ph.sb(f"src_t{k}", [P, G, P]) for k in range(len(sources))]
        norm = Norm(kit, ph, G, D) if norm_before or norm_after else None
        t["norm"] = norm
        const_in = ph.sem("const_in")
        loaded = ph.sem("loaded")
        prepared = ph.sem("prepared")
        turned = ph.sem("turned")
        copied = ph.sem("copied")
        made = ph.sem("made")
        ended = ph.sem("ended")
        stored = ph.sem("stored")
        step = ph.sem("step")
        block = ph.block()
        consts = len(weights) + len(wide) + len(biases)
        mark = ph.sb("mark", [1, 1])
        mark2 = ph.sb("mark2", [1, 1])

        @block.sync
        def _(sp):
            for n, ap in weights.items():
                sp.dma_start(t[n][:, :], ap).then_inc(const_in, 16)
            for n, ap in wide.items():
                sp.dma_start(t[n][:, :], rows_of(ap).broadcast_to([P, D])).then_inc(const_in, 16)
            for n, ap in biases.items():
                sp.dma_start(t[n][:, :], rows_of(ap)).then_inc(const_in, 16)
            with sp.Fori(0, NG) as g:
                if loads:
                    sp.wait_ge(ended, g)
                for n, ap in loads.items():
                    sp.dma_start(t[n][:, :, :], tile_rows(ap, g * G, G)).then_inc(loaded, 16)
                sp.wait_ge(ended, g + 1)
                for n, ap in stores:
                    sp.dma_start(tile_rows(ap, g * G, G), t[n][:, :, :]).then_inc(stored, 16)
            if stores:
                sp.wait_ge(stored, NG * 16 * len(stores))

        @block.vector
        def _(dve):
            if consts:
                dve.wait_ge(const_in, 16 * consts)
            with dve.Fori(0, NG) as g:
                s = Steps(dve, step, g * steps)
                if loads:
                    dve.wait_ge(loaded, (g + 1) * (16 * len(loads)))
                if stores:
                    dve.wait_ge(stored, g * (16 * len(stores)))
                if before:
                    before(dve, s, g, t)
                nc.vector.memset(mark[:, :], 0.0).then_inc(prepared, 1)
                if outputs:
                    dve.wait_ge(made, g + 1)
                if after:
                    after(dve, s, g, t, kit.bank[4:8])
                nc.vector.memset(mark2[:, :], 0.0).then_inc(ended, 1)
                dve.wait_ge(ended, g + 1)
                assert s.n == steps, (name, s.n)

        if outputs:
            @block.tensor
            def _(pe):
                if consts:
                    pe.wait_ge(const_in, 16 * consts)
                with pe.Fori(0, NG) as g:
                    pe.wait_ge(prepared, g + 1)
                    for k, n in enumerate(sources):
                        for c in range(G):
                            last = nc.tensor.transpose(kit.bank[k][:, c * P:(c + 1) * P], t[n][:, c, :], kit.ident[:, :])
                    last.then_inc(turned, 1)
                    pe.wait_ge(copied, (g + 1) * len(sources))
                    for o, (terms, bias) in enumerate(outputs):
                        for c in range(G):
                            out = kit.bank[4 + o][:, c * P:(c + 1) * P]
                            for m, (k, n) in enumerate(terms):
                                last = nc.tensor.matmul(out, src_t[k][:, c, :], t[n][:, :], start=m == 0,
                                                        stop=bias is None and m == len(terms) - 1)
                            if bias is not None:
                                last = nc.tensor.matmul(out, kit.ones[0:1, :], t[f"bias{o}"][:, :], start=False, stop=True)
                    last.then_inc(made, 1)

        @block.scalar
        def _(act):
            if outputs or norm:
                with act.Fori(0, NG) as g:
                    per = int(norm_before) + int(norm_after)
                    if norm_before:
                        norm.on_scalar(act, g * per + 1)
                    if outputs:
                        act.wait_ge(turned, g + 1)
                        for k in range(len(sources)):
                            nc.scalar.copy(src_t[k][:, :, :], kit.bank[k][:, :].rearrange("p (c e) -> p c e", c=G)).then_inc(copied, 1)
                    if norm_after:
                        norm.on_scalar(act, g * per + per)


def by_tile(bank):
    return bank[:, :].rearrange("p (c f) -> p c f", c=G)


def each(ap):
    return ap[:, :].unsqueeze(1).broadcast_to([P, G, D])


def degree(kit, g, t):
    return kit.acc[:, bass.ds(g * G, G), D:D + 1].broadcast_to([P, G, D])


def pad_nodes(kit, x, padded, late):
    nc = kit.nc
    with Phase(kit, "pad") as ph:
        zeros = ph.sb("zeros", [P, D])
        clear, done = ph.sem("clear"), ph.sem("done")
        block = ph.block()
        over = NTG * P - NODES

        @block.vector
        def _(dve):
            nc.vector.memset(zeros[:, :], 0.0).then_inc(clear, 1)

        @block.sync
        def _(sp):
            sp.dma_start(padded[0:NODES, :], x).then_inc(done, 16)
            sp.wait_ge(clear, 1)
            n = 1
            for r in range(0, over, P):
                m = min(P, over - r)
                sp.dma_start(padded[NODES + r:NODES + r + m, :], zeros[0:m, :]).then_inc(done, 16)
                n += 1
            for rows in late:
                for c in range(NT, NTG):
                    sp.dma_start(rows[c * P:(c + 1) * P, :], zeros[:, :]).then_inc(done, 16)
                    n += 1
            sp.wait_ge(done, 16 * n)


def layer_0(kit, ins, x0, x1, h1):
    nc, v = kit.nc, kit.nc.vector
    edge_agg, y = kit.dram("edge_agg", (NTG * P, D)), kit.dram("y0", (NTG * P, D))
    sum_pass(kit, "l0_edges", False, rows=REC)

    def take_sums(dve, s, g, t):
        s.link(v.tensor_copy(t["sums"][:, :, :], kit.acc[:, bass.ds(g * G, G), 0:D]))
        s.link(v.tensor_tensor(t["out"][:, :, :], degree(kit, g, t), each(t["be"]), ALU.mult))

    def add_bias(dve, s, g, t, banks):
        s.link(v.tensor_tensor(t["out"][:, :, :], t["out"][:, :, :], by_tile(banks[0]), ALU.add))

    node_pass(kit, "l0_agg", {}, ["sums"], {"we": ins["L0_gnn_We"]}, [([(0, "we")], None)], [("out", edge_agg)],
              scratch=("sums", "out"), wide={"be": ins["L0_gnn_be"]}, before=take_sums, after=add_bias, steps=3)

    def norm(dve, s, g, t):
        t["norm"].on_vector(dve, s, t["x"][:, :, :], t["h"][:, :, :], g + 1)

    def keep(dve, s, g, t, banks):
        s.link(v.tensor_copy(t["out"][:, :, :], by_tile(banks[0])))

    node_pass(kit, "l0_y", {"x": x0, "agg": edge_agg}, ["h", "agg"], {"w1a": ins["L0_gnn_W1"][0:D, :], "w1b": ins["L0_gnn_W1"][D:2 * D, :]},
              [([(0, "w1a"), (1, "w1b")], None)], [("out", y)], scratch=("h", "out"), before=norm, after=keep,
              norm_before=True, steps=NORM_STEPS + 1)
    sum_pass(kit, "l0_neigh", False, table=y)

    def inner(dve, s, g, t):
        s.link(v.tensor_tensor(t["u"][:, :, :], t["y"][:, :, :], kit.acc[:, bass.ds(g * G, G), 0:D], ALU.add))
        s.link(v.tensor_tensor(t["u"][:, :, :], t["u"][:, :, :], each(t["b1"]), ALU.add))
        s.link(v.tensor_scalar(t["u"][:, :, :], t["u"][:, :, :], 0.0, None, ALU.max))

    node_pass(kit, "l0_out", {"x": x0, "y": y}, ["u"], {"w2": ins["L0_gnn_W2"]}, [([(0, "w2")], ins["L0_gnn_b2"])],
              [("x", x1), ("h", h1)], scratch=("u", "h"), wide={"b1": ins["L0_gnn_b1"]}, before=inner, after=add_and_norm,
              norm_after=True, steps=3 + 1 + NORM_STEPS)


def add_and_norm(dve, s, g, t, banks):
    v = t["norm"].kit.nc.vector
    s.link(v.tensor_tensor(t["x"][:, :, :], t["x"][:, :, :], by_tile(banks[0]), ALU.add))
    t["norm"].on_vector(dve, s, t["x"][:, :, :], t["h"][:, :, :], g + 1)


def layer_1(kit, ins, ph, h1, h_out, own, alpha, node_max, v_rows, kv):
    nc, v = kit.nc, kit.nc.vector
    h = [kit.dram(f"l1_h{k}", (NTG * P, D)) for k in range(2)] + [h_out]
    skip = kit.dram("l1_skip", (NTG * P, D))
    q_we = ph.sb("q_we", [P, NTG, HEADS1])
    C = D // HEADS1

    def relu(dve, s, g, t, banks):
        s.link(v.tensor_scalar(t["out"][:, :, :], by_tile(banks[0]), 0.0, None, ALU.max))

    node_pass(kit, "l1_in", {"x": h1}, ["x"], {"w": ins["L1_gnn_W_in"]}, [([(0, "w")], ins["L1_gnn_b_in"])], [("out", h[0])],
              scratch=("out",), after=relu, steps=1)
    for l in range(2):
        def tables(dve, s, g, t, banks):
            mine = own[:, bass.ds(g * G, G), :]
            s.mark(v.tensor_scalar(mine, by_tile(banks[0]), float(C) ** -0.5, None, ALU.mult))
            s.mark(v.tensor_copy(t["k"][:, :, :], by_tile(banks[1])))
            s.mark(v.tensor_copy(t["v"][:, :, :], by_tile(banks[2])))
            s.mark(v.tensor_copy(t["r"][:, :, :], by_tile(banks[3])))
            s.need(s.n)
            s.link(v.tensor_tensor(t["qw"][:, :, :], mine, each(t["we"]), ALU.mult))
            s.link(v.tensor_reduce(out=q_we[:, bass.ds(g * G, G), :].rearrange("p c h -> p (c h)"),
                                   in_=t["qw"][:, :, :].rearrange("p c (h f) -> p (c h) f", h=HEADS1), axis=AX.X, op=ALU.add))

        node_pass(kit, f"l1_tables{l}", {"h": h[l]}, ["h"],
                  {n: ins[f"L1_gnn_{n}"][l] for n in ("Wq", "Wk", "Wv", "Wskip")},
                  [([(0, "Wq")], ins["L1_gnn_bq"][l]), ([(0, "Wk")], ins["L1_gnn_bk"][l]), ([(0, "Wv")], ins["L1_gnn_bv"][l]),
                   ([(0, "Wskip")], ins["L1_gnn_bskip"][l])],
                  [("k", kv[:, 0:D]), ("v", kv[:, D:2 * D]), ("r", skip)], scratch=("k", "v", "r", "qw"),
                  wide={"we": ins["L1_gnn_We"][l, 0]}, after=tables, steps=6)
        score_pass(kit, f"l1_score{l}", False, 1, kv, v_rows, own, alpha, node_max, q_we)
        weigh_pass(kit, f"l1_weigh{l}", False, 1, v_rows, alpha, node_max)
        mix_and_batchnorm(kit, ins, l, skip, h[l], h[l + 1], own)


def mix_and_batchnorm(kit, ins, l, skip, h_in, h_out, out):
    nc, v = kit.nc, kit.nc.vector
    C = D // HEADS1
    H = HEADS1
    whole = [P, NTG, D]
    with Phase(kit, f"mix{l}") as ph:
        r = ph.sb("r", whole)
        tmp = ph.sb("tmp", whole)
        den = ph.sb("den", [P, NTG, H])
        beta = ph.sb("beta", [P, NTG])
        more = ph.sb("more", [P, NTG])
        vec = {n: ph.sb(n, [P, D]) for n in ("we", "wb_out", "wb_r", "wb_diff", "gamma", "shift")}
        wb = ph.sb("wb", [P, 2, D])
        real = ph.sb("real", [P, 1])
        mean, var, std, factor = (ph.sb(n, [P, D]) for n in ("mean", "var", "std", "factor"))
        loaded, step, stored = ph.sem("loaded"), ph.sem("step"), ph.sem("stored")
        free_r = ph.sem("free_r")
        sig_in, sig_out = ph.sem("sig_in"), ph.sem("sig_out")
        to_sum, summed = ph.sem("to_sum"), ph.sem("summed")
        root_in, root_out = ph.sem("root_in"), ph.sem("root_out")
        block = ph.block()
        wbeta = ins["L1_gnn_Wbeta"][l].rearrange("(k f) o -> k (f o)", k=3)
        small = (("we", ins["L1_gnn_We"][l, 0]), ("wb_out", wbeta[0]), ("wb_r", wbeta[1]), ("wb_diff", wbeta[2]),
                 ("gamma", ins["L1_gnn_bn_gamma"][l]), ("shift", ins["L1_gnn_bn_beta"][l]))

        def all_rows(ap):
            return ap.rearrange("(c p) f -> p c f", p=P)

        def over(ap):
            return ap[:, :].unsqueeze(1).broadcast_to(whole)

        def along(ap):
            return ap[:, :].unsqueeze(2).broadcast_to(whole)

        def by_head(ap):
            return ap.rearrange("p c (h f) -> p c h f", h=H)

        @block.sync
        def _(sp):
            sp.dma_start(r[:, :, :], all_rows(skip)).then_inc(loaded, 16)
            for n, ap in small:
                sp.dma_start(vec[n][:, :], rows_of(ap).broadcast_to([P, D])).then_inc(loaded, 16)
            sp.wait_ge(free_r, 1)
            sp.dma_start(r[:, :, :], all_rows(h_in)).then_inc(loaded, 16)
            sp.wait_ge(free_r, 2)
            sp.dma_start(all_rows(h_out), out[:, :, :]).then_inc(stored, 16)
            sp.wait_ge(stored, 16)

        @block.tensor
        def _(pe):
            for k in range(2):
                pe.wait_ge(to_sum, k + 1)
                x = out if k == 0 else tmp
                for g in range(NG):
                    last = nc.tensor.matmul(kit.bank[k][:, :], kit.ones[:, :], x[:, g * G:(g + 1) * G, :], start=g == 0, stop=g == NG - 1)
                last.then_inc(summed, 1)

        @block.scalar
        def _(act):
            act.wait_ge(sig_in, 1)
            nc.scalar.activation(beta[:, :], more[:, :], ACT.Exp, scale=-1.0).then_inc(sig_out, 1)
            act.wait_ge(root_in, 1)
            nc.scalar.activation(std[:, :], var[:, :], ACT.Sqrt).then_inc(root_out, 1)

        @block.vector
        def _(dve):
            s = Steps(dve, step)
            acc = kit.acc
            dve.wait_ge(loaded, 16 * 7)
            s.link(v.tensor_scalar(den[:, :, :], acc[:, :, D:D + H], 1e-30, None, ALU.max))
            s.link(v.reciprocal(den[:, :, :], den[:, :, :]))
            for h in range(H):
                cols = slice(h * C, (h + 1) * C)
                s.mark(v.tensor_tensor(tmp[:, :, cols], vec["we"][:, cols].unsqueeze(1).broadcast_to([P, NTG, C]),
                                       acc[:, :, D + H + h:D + H + h + 1].broadcast_to([P, NTG, C]), ALU.mult))
            s.need(s.n)
            s.link(v.tensor_tensor(out[:, :, :], tmp[:, :, :], acc[:, :, 0:D], ALU.add))
            for h in range(H):
                cols = slice(h * C, (h + 1) * C)
                s.mark(v.tensor_tensor(out[:, :, cols], out[:, :, cols], den[:, :, h:h + 1].broadcast_to([P, NTG, C]), ALU.mult))
            s.need(s.n)
            s.mark(v.tensor_tensor(wb[:, 0, :], vec["wb_out"][:, :], vec["wb_diff"][:, :], ALU.add))
            s.link(v.tensor_tensor(wb[:, 1, :], vec["wb_r"][:, :], vec["wb_diff"][:, :], ALU.subtract))
            s.link(v.tensor_tensor(tmp[:, :, :], out[:, :, :], wb[:, 0:1, :].broadcast_to(whole), ALU.mult))
            s.link(v.tensor_reduce(out=beta[:, :], in_=tmp[:, :, :], axis=AX.X, op=ALU.add))
            s.link(v.tensor_tensor(tmp[:, :, :], r[:, :, :], wb[:, 1:2, :].broadcast_to(whole), ALU.mult))
            s.link(v.tensor_reduce(out=more[:, :], in_=tmp[:, :, :], axis=AX.X, op=ALU.add))
            v.tensor_tensor(more[:, :], more[:, :], beta[:, :], ALU.add).then_inc(sig_in, 1)
            dve.wait_ge(sig_out, 1)
            s.link(v.tensor_scalar(beta[:, :], beta[:, :], 1.0, None, ALU.add))
            s.link(v.reciprocal(beta[:, :], beta[:, :]))
            s.link(v.tensor_tensor(tmp[:, :, :], r[:, :, :], out[:, :, :], ALU.subtract))
            s.link(v.tensor_tensor(tmp[:, :, :], tmp[:, :, :], along(beta), ALU.mult))
            s.link(v.tensor_tensor(out[:, :, :], out[:, :, :], tmp[:, :, :], ALU.add))
            s.mark(v.tensor_scalar(real[:, :], kit.part[:, :], float(LAST), None, ALU.is_lt))
            s.mark(v.memset(out[:, NT:, :], 0.0))
            s.need(s.n)
            v.tensor_scalar(out[:, NT - 1, :], out[:, NT - 1, :], real[:, :], None, ALU.mult).then_inc(to_sum, 1)
            v.memset(more[0:1, 0:1], 0.0).then_inc(free_r, 1)
            dve.wait_ge(summed, 1)
            four = kit.bank[0][:, :].rearrange("p (c f) -> p f c", c=G)
            s.link(v.tensor_reduce(out=mean[:, :], in_=four, axis=AX.X, op=ALU.add))
            s.link(v.tensor_scalar(mean[:, :], mean[:, :], 1.0 / NODES, None, ALU.mult))
            s.link(v.tensor_tensor(out[:, :, :], out[:, :, :], over(mean), ALU.subtract))
            s.link(v.tensor_tensor(tmp[:, :, :], out[:, :, :], out[:, :, :], ALU.mult))
            s.mark(v.memset(tmp[:, NT:, :], 0.0))
            v.tensor_scalar(tmp[:, NT - 1, :], tmp[:, NT - 1, :], real[:, :], None, ALU.mult).then_inc(to_sum, 1)
            dve.wait_ge(summed, 2)
            four = kit.bank[1][:, :].rearrange("p (c f) -> p f c", c=G)
            s.link(v.tensor_reduce(out=var[:, :], in_=four, axis=AX.X, op=ALU.add))
            v.tensor_scalar(var[:, :], var[:, :], 1.0 / NODES, EPS, ALU.mult, ALU.add).then_inc(root_in, 1)
            dve.wait_ge(root_out, 1)
            s.link(v.reciprocal(factor[:, :], std[:, :]))
            s.link(v.tensor_tensor(factor[:, :], factor[:, :], vec["gamma"][:, :], ALU.mult))
            s.link(v.tensor_tensor(out[:, :, :], out[:, :, :], over(factor), ALU.mult))
            s.link(v.tensor_tensor(out[:, :, :], out[:, :, :], over(vec["shift"]), ALU.add))
            dve.wait_ge(loaded, 16 * 8)
            s.link(v.scalar_tensor_tensor(out=out[:, :, :], in0=out[:, :, :], scalar=0.0, in1=r[:, :, :], op0=ALU.max, op1=ALU.add))
            v.memset(more[0:1, 0:1], 0.0).then_inc(free_r, 1)


def attended(kit, name, rows):
    nc, v = kit.nc, kit.nc.vector
    H = HEADS2
    C = D // H
    with Phase(kit, name) as ph:
        out = ph.sb("out", [P, NTG, D])
        inv = ph.sb("inv", [P, NTG, H])
        step, stored = ph.sem("step"), ph.sem("stored")
        block = ph.block()

        @block.vector
        def _(dve):
            s = Steps(dve, step)
            s.link(v.tensor_scalar(inv[:, :, :], kit.acc[:, :, D:D + H], 1e-16, None, ALU.add))
            s.link(v.reciprocal(inv[:, :, :], inv[:, :, :]))
            s.mark(v.tensor_tensor(out[:, :, 0:C], kit.acc[:, :, 0:C], inv[:, :, 0:1].broadcast_to([P, NTG, C]), ALU.mult))
            s.mark(v.tensor_tensor(out[:, :, C:D], kit.acc[:, :, C:D], inv[:, :, 1:2].broadcast_to([P, NTG, C]), ALU.mult))

        @block.sync
        def _(sp):
            sp.wait_ge(step, 4)
            sp.dma_start(rows.rearrange("(c p) f -> p c f", p=P), out[:, :, :]).then_inc(stored, 16)
            sp.wait_ge(stored, 16)


def layer_2(kit, ins, x1, l1_out, x2, own, alpha, node_max, v_rows, table):
    nc, v = kit.nc, kit.nc.vector
    h2, sent, recv = (kit.dram(n, (NTG * P, D)) for n in ("l2_h", "l2_sent", "l2_recv"))

    def norm(dve, s, g, t):
        s.link(v.tensor_tensor(t["x"][:, :, :], t["x"][:, :, :], t["l1"][:, :, :], ALU.add))
        t["norm"].on_vector(dve, s, t["x"][:, :, :], t["h"][:, :, :], g + 1)

    def tables(dve, s, g, t, banks):
        s.mark(v.tensor_copy(own[:, bass.ds(g * G, G), :], by_tile(banks[0])))
        s.mark(v.tensor_copy(t["b"][:, :, :], by_tile(banks[1])))
        s.mark(v.tensor_copy(t["v"][:, :, :], by_tile(banks[2])))
        s.need(s.n)

    w1 = ins["L2_gnn_w1"]
    node_pass(kit, "l2_tables", {"x": x1, "l1": l1_out}, ["h"], {"w1a": w1[0:D, :], "w1b": w1[D:2 * D, :], "w3a": ins["L2_gnn_w3"][0:D, :]},
              [([(0, "w1a")], ins["L2_gnn_b1"]), ([(0, "w1b")], None), ([(0, "w3a")], ins["L2_gnn_b3"])],
              [("b", table[:, 0:D]), ("v", table[:, D:2 * D]), ("x", x2), ("h", h2)], scratch=("h", "b", "v"),
              before=norm, after=tables, norm_before=True, steps=1 + NORM_STEPS + 3)
    with Phase(kit, "l2_w2") as ph:
        w2 = ph.sb("w2", [P, D])
        with Phase(kit, "l2_w2_in") as inner:
            done = inner.sem("done")
            block = inner.block()

            @block.sync
            def _(sp):
                sp.dma_start(w2[:, :], rows_of(ins["L2_gnn_w2"].rearrange("h f -> (h f)")).broadcast_to([P, D])).then_inc(done, 16)
                sp.wait_ge(done, 16)

        for name, by_src, rows in (("sent", True, sent), ("recv", False, recv)):
            score_pass(kit, f"l2_score_{name}", by_src, 2, table, v_rows, own, alpha, node_max, w2)
            weigh_pass(kit, f"l2_weigh_{name}", by_src, 2, v_rows, alpha, node_max)
            attended(kit, f"l2_out_{name}", rows)
    return h2, sent, recv


def layer_2_mlp(kit, ins, x2, x3, h3, h2, sent, recv):
    nc, v = kit.nc, kit.nc.vector
    GRAPHS, HID = 500, 512
    CH = 4
    GP = GRAPHS // CH
    with Phase(kit, "mlp") as ph:
        mw0 = ph.sb("mw0", [P, 4, HID])
        mw1 = ph.sb("mw1", [P, 4, HID])
        mw2 = ph.sb("mw2", [P, 4, D])
        rows = {n: ph.sb(n, [1, HID]) for n in ("mb0", "mb1")}
        mb2 = ph.sb("mb2", [1, D])
        vec = {n: ph.sb(n, [P, HID]) for n in ("ls0", "lb0", "ls1", "lb1")}
        u = ph.sb("u", [P, CH, D])
        u_t = ph.sb("u_t", [P, P])
        gu = ph.sb("gu", [P, CH, HID])
        count_i = ph.sb("count_i", [P, CH], I32)
        count = ph.sb("count", [P, CH])
        first = ph.sb("first", [P, CH])
        behind = ph.sb("behind", [P, CH])
        node_no = ph.sb("node_no", [P, P])
        ge = ph.sb("ge", [P, CH, P])
        member = ph.sb("member", [P, CH, P])
        part = {n: ph.sb(n, [P, D]) for n in ("h", "s", "r", "x")}
        part_t = ph.sb("part_t", [P, 4, P])
        hid = ph.sb("hid", [P, 1, HID])
        hid_t = ph.sb("hid_t", [P, 4, P])
        out_h = ph.sb("out_h", [P, 1, D])
        mark = ph.sb("mark", [1, 1])
        norm, norm_out = Norm(kit, ph, 1, HID, "wide"), Norm(kit, ph, 1, D, "last")
        loaded, counted, placed, u_turned, u_copied, u_made, u_kept = (
            ph.sem(n) for n in ("loaded", "counted", "placed", "u_turned", "u_copied", "u_made", "u_kept"))
        tile_in, stored, step = ph.sem("tile_in"), ph.sem("stored"), ph.sem("step")
        membered, turned, copied, made, normed, ended = (ph.sem(n) for n in ("membered", "turned", "copied", "made", "normed", "ended"))
        set_up = ph.sem("set_up")
        block = ph.block()
        SETUP = 6
        LOADS = 11 + CH
        STEPS = 4 + 1 + 2 * (NORM_STEPS + 2) + 1 + NORM_STEPS + 1

        @block.sync
        def _(sp):
            sp.dma_start(mw0[:, :, :], ins["L2_gnn_mw0"].rearrange("(k p) f -> p k f", p=P)).then_inc(loaded, 16)
            sp.dma_start(mw1[:, :, :], ins["L2_gnn_mw1"].rearrange("(k p) f -> p k f", p=P)).then_inc(loaded, 16)
            sp.dma_start(mw2[:, :, :], ins["L2_gnn_mw2"].rearrange("(k p) f -> p k f", p=P)).then_inc(loaded, 16)
            for n in rows:
                sp.dma_start(rows[n][:, :], rows_of(ins[f"L2_gnn_{n}"])).then_inc(loaded, 16)
            sp.dma_start(mb2[:, :], rows_of(ins["L2_gnn_mb2"])).then_inc(loaded, 16)
            for n in vec:
                sp.dma_start(vec[n][:, :], rows_of(ins[f"L2_gnn_{n}"]).broadcast_to([P, HID])).then_inc(loaded, 16)
            sp.dma_start(u[0:GP, :, :], ins["L2_gnn_u"].rearrange("(k p) f -> p k f", p=GP)).then_inc(loaded, 16)
            for k in range(CH):
                sp.dma_start(count_i[0:GP, k:k + 1], ins["L2_gnn_num_nodes"][k * GP:(k + 1) * GP].rearrange("(p o) -> p o", o=1)).then_inc(loaded, 16)
            with sp.Fori(0, NT) as t:
                sp.wait_ge(stored, t * 32)
                for n, ap in (("h", h2), ("s", sent), ("r", recv), ("x", x2)):
                    sp.dma_start(part[n][:, :], ap[bass.ds(t * P, P), :]).then_inc(tile_in, 16)
                sp.wait_ge(ended, t + 1)
                sp.dma_start(x3[bass.ds(t * P, P), :], part["x"][:, :]).then_inc(stored, 16)
                sp.dma_start(h3[bass.ds(t * P, P), :], out_h[:, 0, :]).then_inc(stored, 16)
            sp.wait_ge(stored, NT * 32)

        @block.vector
        def _(dve):
            s = Steps(dve, step)
            dve.wait_ge(loaded, LOADS * 16)
            v.tensor_copy(count[0:GP, :], count_i[0:GP, :]).then_inc(counted, 1)
            for k in range(CH):
                dve.wait_ge(u_made, k + 1)
                v.tensor_copy(gu[0:GP, k, :], kit.bank[2][0:GP, :]).then_inc(u_kept, 1)
            dve.wait_ge(placed, 1)
            s.mark(v.tensor_copy(first[0:GP, :], kit.bank[7][0:GP, 0:CH]))
            s.link(v.tensor_copy(node_no[:, :], kit.node_of_col[:, :]))
            s.link(v.tensor_tensor(behind[0:GP, :], first[0:GP, :], count[0:GP, :], ALU.add))
            s.link(v.tensor_scalar(count[0:GP, 0:1], kit.part[0:GP, :], float(GP - 1), BIG, ALU.is_equal, ALU.mult))
            s.link(v.tensor_tensor(behind[0:GP, CH - 1:CH], behind[0:GP, CH - 1:CH], count[0:GP, 0:1], ALU.add))
            s.link(v.memset(mark[:, :], 0.0))
            assert s.n == SETUP
            with dve.Fori(0, NT) as t:
                s = Steps(dve, step, SETUP + t * STEPS)
                for k in range(CH):
                    s.mark(v.tensor_scalar(ge[0:GP, k, :], node_no[0:GP, :], first[0:GP, k:k + 1], None, ALU.is_ge))
                s.need(s.n)
                for k in range(CH):
                    ins_ = v.scalar_tensor_tensor(out=member[0:GP, k, :], in0=node_no[0:GP, :], scalar=behind[0:GP, k:k + 1],
                                                  in1=ge[0:GP, k, :], op0=ALU.is_lt, op1=ALU.mult).then_inc(membered, 1)
                dve.wait_ge(membered, (t + 1) * CH)
                s.link(v.tensor_scalar(node_no[:, :], node_no[:, :], float(P), None, ALU.add))
                for k in range(2):
                    dve.wait_ge(made, t * 3 + k + 1)
                    norm.on_vector(dve, s, kit.bank[2 + k][:, :].rearrange("p (o f) -> p o f", o=1), hid[:, :, :], t * 2 + k + 1,
                                   vec[f"ls{k}"][:, :].unsqueeze(1), vec[f"lb{k}"][:, :].unsqueeze(1))
                    v.memset(mark[:, :], 0.0).then_inc(normed, 1)
                    dve.wait_ge(normed, t * 2 + k + 1)
                dve.wait_ge(made, t * 3 + 3)
                dve.wait_ge(tile_in, (t + 1) * 64)
                s.link(v.tensor_tensor(part["x"][:, :], part["x"][:, :], kit.bank[4][:, 0:D], ALU.add))
                norm_out.on_vector(dve, s, part["x"][:, :].unsqueeze(1), out_h[:, :, :], t + 1)
                s.link(v.memset(mark[:, :], 0.0))
                v.memset(mark[:, :], 0.0).then_inc(ended, 1)
                dve.wait_ge(ended, t + 1)
                assert s.n == STEPS, s.n

        @block.tensor
        def _(pe):
            pe.wait_ge(loaded, LOADS * 16)
            pe.wait_ge(counted, 1)
            for k in range(CH):
                for j in range(k):
                    nc.tensor.matmul(kit.bank[7][0:GP, k:k + 1], kit.ones[0:GP, 0:GP], count[0:GP, j:j + 1], start=j == 0, stop=False)
                last = nc.tensor.matmul(kit.bank[7][0:GP, k:k + 1], kit.before[0:GP, 0:GP], count[0:GP, k:k + 1], start=k == 0, stop=True)
            last.then_inc(placed, 1)
            for k in range(CH):
                pe.wait_ge(u_copied, k)
                nc.tensor.transpose(kit.bank[1][:, 0:GP], u[0:GP, k, :], kit.ident[0:GP, 0:GP]).then_inc(u_turned, 1)
                pe.wait_ge(u_copied, k + 1)
                pe.wait_ge(u_kept, k)
                nc.tensor.matmul(kit.bank[2][0:GP, :], u_t[:, 0:GP], mw0[:, 3, :], start=True, stop=True).then_inc(u_made, 1)
            pe.wait_ge(u_kept, CH)
            with pe.Fori(0, NT) as t:
                pe.wait_ge(tile_in, (t + 1) * 64)
                for k, n in enumerate(("h", "s", "r")):
                    last = nc.tensor.transpose(kit.bank[0][:, k * P:(k + 1) * P], part[n][:, :], kit.ident[:, :])
                last.then_inc(turned, 1)
                pe.wait_ge(copied, t * 3 + 1)
                pe.wait_ge(membered, (t + 1) * CH)
                for k in range(3):
                    nc.tensor.matmul(kit.bank[2][:, :], part_t[:, k, :], mw0[:, k, :], start=k == 0, stop=False)
                for k in range(CH):
                    nc.tensor.matmul(kit.bank[2][:, :], member[0:GP, k, :], gu[0:GP, k, :], start=False, stop=False)
                nc.tensor.matmul(kit.bank[2][:, :], kit.ones[0:1, :], rows["mb0"][:, :], start=False, stop=True).then_inc(made, 1)
                for r in range(2):
                    pe.wait_ge(normed, t * 2 + r + 1)
                    for k in range(4):
                        last = nc.tensor.transpose(kit.bank[0][:, k * P:(k + 1) * P], hid[:, 0, k * P:(k + 1) * P], kit.ident[:, :])
                    last.then_inc(turned, 1)
                    pe.wait_ge(copied, t * 3 + r + 2)
                    out, w, bias = (kit.bank[3][:, :], mw1, rows["mb1"]) if r == 0 else (kit.bank[4][:, 0:D], mw2, mb2)
                    for k in range(4):
                        nc.tensor.matmul(out, hid_t[:, k, :], w[:, k, :], start=k == 0, stop=False)
                    nc.tensor.matmul(out, kit.ones[0:1, :], bias[:, :], start=False, stop=True).then_inc(made, 1)

        @block.scalar
        def _(act):
            for k in range(CH):
                act.wait_ge(u_turned, k + 1)
                act.wait_ge(u_made, k)
                nc.scalar.copy(u_t[:, 0:GP], kit.bank[1][:, 0:GP]).then_inc(u_copied, 1)
            with act.Fori(0, NT) as t:
                act.wait_ge(turned, t * 3 + 1)
                nc.scalar.copy(part_t[:, 0:3, :], kit.bank[0][:, 0:3 * P].rearrange("p (c e) -> p c e", c=3)).then_inc(copied, 1)
                for r in range(2):
                    norm.on_scalar(act, t * 2 + r + 1)
                    act.wait_ge(turned, t * 3 + r + 2)
                    nc.scalar.copy(hid_t[:, :, :], kit.bank[0][:, :].rearrange("p (c e) -> p c e", c=4)).then_inc(copied, 1)
                norm_out.on_scalar(act, t + 1)


def layer_3(kit, ins, x3, h3, x4, own):
    nc, v = kit.nc, kit.nc.vector
    hw, agg, u = (kit.dram(n, (NTG * P, D)) for n in ("l3_hw", "l3_agg", "l3_u"))

    def tables(dve, s, g, t, banks):
        s.mark(v.tensor_copy(t["out"][:, :, :], by_tile(banks[0])))
        s.mark(v.tensor_tensor(own[:, bass.ds(g * G, G), :], by_tile(banks[0]), each(t["b1"]), ALU.add))
        s.need(s.n)

    node_pass(kit, "l3_tables", {"h": h3}, ["h"], {"w1": ins["L3_gnn_e_w1"]}, [([(0, "w1")], None)], [("out", hw)],
              scratch=("out",), wide={"b1": ins["L3_gnn_e_b1"]}, after=tables, steps=2)
    sum_pass(kit, "l3_sum", True, table=hw, own=own)

    def take_sums(dve, s, g, t):
        s.link(v.tensor_copy(t["sums"][:, :, :], kit.acc[:, bass.ds(g * G, G), 0:D]))
        s.link(v.tensor_tensor(t["out"][:, :, :], degree(kit, g, t), each(t["b2"]), ALU.mult))

    def add_bias(dve, s, g, t, banks):
        s.link(v.tensor_tensor(t["out"][:, :, :], t["out"][:, :, :], by_tile(banks[0]), ALU.add))

    node_pass(kit, "l3_agg_", {}, ["sums"], {"w2": ins["L3_gnn_e_w2"]}, [([(0, "w2")], None)], [("out", agg)],
              scratch=("sums", "out"), wide={"b2": ins["L3_gnn_e_b2"]}, before=take_sums, after=add_bias, steps=3)

    def relu(dve, s, g, t, banks):
        s.link(v.tensor_scalar(t["out"][:, :, :], by_tile(banks[0]), 0.0, None, ALU.max))

    node_pass(kit, "l3_inner", {"h": h3, "agg": agg}, ["h", "agg"], {"w1a": ins["L3_gnn_n_w1"][0:D, :], "w1b": ins["L3_gnn_n_w1"][D:2 * D, :]},
              [([(0, "w1a"), (1, "w1b")], ins["L3_gnn_n_b1"])], [("out", u)], scratch=("out",), after=relu, steps=1)

    def add(dve, s, g, t, banks):
        s.link(v.tensor_tensor(t["x"][:, :, :], t["x"][:, :, :], by_tile(banks[0]), ALU.add))

    node_pass(kit, "l3_out", {"u": u, "x": x3}, ["u"], {"w2": ins["L3_gnn_n_w2"]}, [([(0, "w2")], ins["L3_gnn_n_b2"])], [("x", x4)],
              after=add, steps=1)


def build_program(nc, ins, outs, stop=None):
    with ExitStack() as ctx:
        kit = Kit(nc, ctx)
        constants(kit)
        with Phase(kit, "edges") as ph:
            pos = [ph.sb(f"pos{k}", [P, COLS + 1], I32) for k in range(2)]
            pads = [ph.sb(f"pads{k}", [P, NT + SPARE], I32) for k in range(2)]
            recs = [ph.sb(f"recs{k}", [P, COLS + 1, REC]) for k in range(2)]
            sort_positions(kit, ins, *pos, *pads, *recs)
            scatter_edges(kit, ins, *pos, *pads, *recs)
        load_records(kit, "recs")
        if stop:
            return stop(kit, outs)
        x = [kit.dram(f"x{k}", (NTG * P, D)) for k in range(5)]
        h1, l1_out, h3 = (kit.dram(n, (NTG * P, D)) for n in ("h1", "l1_out", "h3"))
        pad_nodes(kit, ins["x"], x[0], (x[3], h3))
        layer_0(kit, ins, x[0], x[1], h1)
        table = kit.dram("pair_table", (NTG * P, 2 * D))
        v_rows = kit.dram("values", (P, TILES, D))
        with Phase(kit, "attention") as ph:
            own = ph.sb("own", [P, NTG, D])
            alpha = ph.sb("alpha", [P, TILES, HEADS1])
            node_max = ph.sb("node_max", [P, NTG, HEADS1])
            layer_1(kit, ins, ph, h1, l1_out, own, alpha, node_max, v_rows, table)
            h2, sent, recv = layer_2(kit, ins, x[1], l1_out, x[2], own, alpha, node_max, v_rows, table)
        layer_2_mlp(kit, ins, x[2], x[3], h3, h2, sent, recv)
        with Phase(kit, "last") as ph:
            own = ph.sb("own", [P, NTG, D])
            layer_3(kit, ins, x[3], h3, x[4], own)
        with Phase(kit, "out") as ph:
            done = ph.sem("done")
            block = ph.block()

            @block.sync
            def _(sp):
                sp.dma_start(outs["out"], x[4][0:NODES, :]).then_inc(done, 16)
                sp.wait_ge(done, 16)


def kernel(**inputs):
    import concourse.bacc as bacc
    import numpy as np
    from concourse.bass_utils import run_bass_kernel_spmd

    nc = bacc.Bacc("TRN2", target_bir_lowering=False, num_devices=1)
    arrays, ins = {}, {}
    for name, a in inputs.items():
        a = np.ascontiguousarray(a)
        arrays[f"in_{name}"] = a
        ins[name] = nc.dram_tensor(f"in_{name}", a.shape, mybir.dt.from_np(a.dtype), kind="ExternalInput").ap()
    out = nc.dram_tensor("out_x", (NODES, D), F32, kind="ExternalOutput").ap()
    build_program(nc, ins, {"out": out})
    ran = run_bass_kernel_spmd(nc, [arrays], core_ids=[0])
    return ran.results[0]["out_x"]
```

```python
from contextlib import ExitStack

import concourse.bass as bass
from concourse import mybir

F32 = mybir.dt.float32
I32 = mybir.dt.int32
BF16 = mybir.dt.bfloat16
ALU = mybir.AluOpType
ACT = mybir.ActivationFunctionType
AX = mybir.AxisListType

P = 128
NODES, EDGES, D = 6250, 106250, 128
NT = -(-NODES // P)
LAST = NODES - (NT - 1) * P
G = 4
NG = -(-NT // (2 * G)) * 2
NTG = NG * G
COLS = EDGES // P
REST = EDGES - COLS * P
U = 4
GROUPS = -(-((EDGES + NT * (G * P - 1)) // (G * P)) // U) * U
TURNS = GROUPS // U
TILES = GROUPS * G
SLOTS = TILES * P
PADS = -(-(SLOTS - EDGES) // P)
EB = 5
assert COLS % (2 * EB) == 0
REC = 4
ROW = REC + 3 * D + REC
DROW, SROW0 = REC + 3 * D, REC + D
SROW = ROW - SROW0
HEADS1, HEADS2 = 4, 2
BIG = 1.0e30
EPS = 1e-5
SLOPE = 0.2
ACCW = 136


class Steps:

    def __init__(self, eng, sem, base=0):
        self.eng, self.sem, self.base, self.n = eng, sem, base, 0

    def mark(self, ins):
        ins.then_inc(self.sem, 1)
        self.n += 1
        return self.n

    def need(self, n):
        self.eng.wait_ge(self.sem, self.base + n)

    def link(self, ins):
        self.need(self.mark(ins))


class Count:

    def __init__(self, pool, name, start):
        self.pool, self.reg = pool, pool.alloc_register(name)
        pool.reg_mov(self.reg, start)

    def step(self, n):
        self.pool.reg_add(self.reg, self.reg, n)

    def wait(self, sem):
        self.pool.wait_ge(sem, self.reg)


def wait_from(eng, sem, value):
    if not isinstance(value, int) or value > 0:
        eng.wait_ge(sem, value)


def rows_of(ap):
    return ap.rearrange("(o n) -> o n", o=1)


class Kit:

    def __init__(self, nc, ctx):
        self.nc = nc

        def sb(name, shape, dt=F32):
            return ctx.enter_context(nc.sbuf_tensor(name, shape, dt))

        self.ident = sb("ident", [P, P])
        self.neg_ident = sb("neg_ident", [P, P])
        self.ident4_bf = sb("ident4_bf", [P, G, P], BF16)
        self.ones = sb("ones", [P, P])
        self.before = sb("before", [P, P])
        self.node_of_col = sb("node_of_col", [P, P])
        self.part = sb("part", [P, 1])
        self.acc = sb("acc", [P, NTG, ACCW])
        self.rec_d = sb("rec_d", [P, TILES, REC])
        self.rec_s = sb("rec_s", [P, TILES, REC])
        self.tile_d = sb("tile_d", [1, GROUPS], I32)
        self.tile_s = sb("tile_s", [1, GROUPS], I32)
        self.bank = [ctx.enter_context(nc.psum_tensor(f"bank{b}", [P, 512], F32)) for b in range(8)]

        def dram(name, shape, dt=F32):
            return nc.dram_tensor(name, shape, dt, kind="Internal").ap()

        self.rows_d = dram("rows_by_dst", (SLOTS, DROW))
        self.rows_s = dram("rows_by_src", (SLOTS, SROW))
        self.dram = dram


class Phase:

    def __init__(self, kit, name):
        self.kit, self.name = kit, name

    def __enter__(self):
        self.ctx = ExitStack()
        self.nc = self.kit.nc
        self.sems = []
        return self

    def sb(self, name, shape, dt=F32):
        return self.ctx.enter_context(self.nc.sbuf_tensor(f"{self.name}_{name}", shape, dt))

    def sem(self, name):
        self.sems.append(self.nc.alloc_semaphore(name=f"{self.name}_{name}"))
        return self.sems[-1]

    def block(self):
        return self.ctx.enter_context(self.nc.Block())

    def __exit__(self, *exc):
        self.ctx.__exit__(*exc)
        if self.sems and exc[0] is None:
            self.nc.clear_and_free_semaphores(self.sems)
            self.nc.all_engine_barrier()


def constants(kit):
    nc = kit.nc
    with Phase(kit, "const") as ph:
        filled, made, col_i = ph.sem("filled"), ph.sem("made"), ph.sem("col_i")
        cast = ph.sem("cast")
        col_int = ph.sb("col_int", [P, P], I32)
        part_int = ph.sb("part_int", [P, 1], I32)
        block = ph.block()

        @block.gpsimd
        def _(pool):
            pool.memset(kit.ident[:, :], 0.0).then_inc(filled, 1)
            pool.memset(kit.neg_ident[:, :], 0.0).then_inc(filled, 1)
            pool.memset(kit.ones[:, :], 1.0).then_inc(filled, 1)
            pool.iota(col_int[:, :], pattern=[[1, P]], base=0, channel_multiplier=0).then_inc(col_i, 1)
            pool.iota(part_int[:, :], pattern=[[1, 1]], base=0, channel_multiplier=1).then_inc(col_i, 1)
            pool.wait_ge(filled, 3)
            pool.affine_select(out=kit.ident[:, :], in_=kit.ident[:, :], compare_op=ALU.not_equal, fill=1.0,
                               base=0, pattern=[[-1, P]], channel_multiplier=1).then_inc(made, 1)
            pool.affine_select(out=kit.neg_ident[:, :], in_=kit.neg_ident[:, :], compare_op=ALU.not_equal,
                               fill=-1.0, base=0, pattern=[[-1, P]], channel_multiplier=1).then_inc(made, 1)
            pool.affine_select(out=kit.before[:, :], in_=kit.ones[:, :], compare_op=ALU.is_gt, fill=0.0,
                               base=0, pattern=[[1, P]], channel_multiplier=-1).then_inc(made, 1)

        @block.vector
        def _(dve):
            dve.wait_ge(col_i, 2)
            nc.vector.tensor_copy(kit.node_of_col[:, :], col_int[:, :])
            nc.vector.tensor_copy(kit.part[:, :], part_int[:, :])
            dve.wait_ge(made, 3)
            nc.vector.tensor_copy(kit.ident4_bf[:, :, :], kit.ident[:, :].unsqueeze(1).broadcast_to([P, G, P])).then_inc(cast, 1)
            dve.wait_ge(cast, 1)


def sort_positions(kit, ins, pos_d, pos_s, pads_d, pads_s, recs_d, recs_s):
    nc = kit.nc
    with Phase(kit, "sort") as ph:
        key = [ph.sb("key_d", [P, COLS + 1], I32), ph.sb("key_s", [P, COLS + 1], I32)]
        low = ph.sb("low", [P, COLS + 1], I32)
        bucket = ph.sb("bucket", [P, COLS + 1])
        here = ph.sb("here", [P, COLS + 1])
        count = ph.sb("count", [P, COLS + 1])
        rank = ph.sb("rank", [P, COLS + 1])
        weight = ph.sb("weight", [P, COLS + 1])
        one = ph.sb("one", [P, COLS + 1])
        total = ph.sb("total", [P, NT])
        size = ph.sb("size", [P, NT])
        size_i = ph.sb("size_i", [P, NT], I32)
        groups_of = ph.sb("groups_of", [P, NT])
        ends = ph.sb("ends", [P, NT])
        earlier = ph.sb("earlier", [P, NT])
        start = ph.sb("start", [P, NT])
        base = ph.sb("base", [P, NT])
        bucket_no = ph.sb("bucket_no", [P, NT])
        pad_no = ph.sb("pad_no", [P, PADS])
        pad_int = ph.sb("pad_int", [P, PADS], I32)
        pad = ph.sb("pad", [P, PADS])
        more = ph.sb("more", [P, PADS])
        group_no = ph.sb("group_no", [1, GROUPS])
        tile_of = ph.sb("tile_of", [1, GROUPS])
        group_int = ph.sb("group_int", [1, GROUPS], I32)
        cleared, loaded = ph.sem("cleared"), ph.sem("loaded")
        numbered = ph.sem("numbered")
        step, totals, summed = ph.sem("step"), ph.sem("totals"), ph.sem("summed")
        block = ph.block()

        def main(ap):
            return ap[0:COLS * P].rearrange("(p c) -> p c", c=COLS)

        def rest(ap):
            return ap[COLS * P:EDGES].rearrange("(p c) -> p c", c=1)

        @block.sync
        def _(sp):
            sp.wait_ge(cleared, 1)
            weights = ins["edge_weight1"].rearrange("e o -> (e o)")
            for out, src in ((key[0], ins["dst"]), (key[1], ins["src"]), (weight, weights)):
                sp.dma_start(out[:, 0:COLS], main(src)).then_inc(loaded, 16)
                sp.dma_start(out[0:REST, COLS:COLS + 1], rest(src)).then_inc(loaded, 16)

        @block.gpsimd
        def _(pool):
            pool.iota(group_int[:, :], pattern=[[1, GROUPS]], base=0, channel_multiplier=0).then_inc(numbered, 1)
            pool.iota(pad_int[:, :], pattern=[[P, PADS]], base=0, channel_multiplier=1).then_inc(numbered, 1)

        @block.tensor
        def _(pe):
            for k in range(2):
                pe.wait_ge(totals, k + 1)
                nc.tensor.matmul(kit.bank[0][:, 0:NT], kit.before[:, :], total[:, :], start=True, stop=True)
                nc.tensor.matmul(kit.bank[1][:, 0:NT], kit.ones[:, :], total[:, :], start=True, stop=True)\
                    .then_inc(summed, 1)

        @block.vector
        def _(dve):
            s = Steps(dve, step)
            nc.vector.memset(key[0][:, COLS:COLS + 1], -P)
            nc.vector.memset(weight[:, COLS:COLS + 1], 0.0)
            nc.vector.memset(one[:, :], 1.0)
            s.link(nc.vector.memset(key[1][:, COLS:COLS + 1], -P))
            nc.vector.tensor_copy(bucket_no[:, :], kit.node_of_col[:, 0:NT]).then_inc(cleared, 1)
            dve.wait_ge(numbered, 2)
            s.link(nc.vector.tensor_copy(group_no[:, :], group_int[:, :]))
            s.link(nc.vector.tensor_copy(pad_no[:, :], pad_int[:, :]))
            dve.wait_ge(loaded, 6 * 16)
            for k, (pos, pads, recs, tab) in enumerate(((pos_d, pads_d, recs_d, kit.tile_d),
                                                        (pos_s, pads_s, recs_s, kit.tile_s))):
                s.link(nc.vector.tensor_single_scalar(low[:, :], key[k][:, :], P - 1, ALU.bitwise_and))
                s.mark(nc.vector.tensor_copy(recs[:, :, 0], low[:, :]))
                s.mark(nc.vector.tensor_copy(recs[:, :, 1], key[1 - k][:, :]))
                s.mark(nc.vector.tensor_copy(recs[:, :, 2], weight[:, :]))
                s.mark(nc.vector.memset(recs[:, :, 3], 0.0))
                s.mark(nc.vector.memset(rank[:, :], 0.0))
                s.need(s.n)
                s.link(nc.vector.tensor_single_scalar(low[:, :], key[k][:, :], P.bit_length() - 1, ALU.arith_shift_right))
                s.link(nc.vector.tensor_copy(bucket[:, :], low[:, :]))
                at = s.n
                with dve.Fori(0, NT) as b:
                    t = Steps(dve, step, at + 5 * b)
                    t.link(nc.vector.tensor_scalar(here[:, :], bucket[:, :], bucket_no[:, bass.ds(b, 1)], None, ALU.is_equal))
                    t.link(nc.vector.tensor_tensor_scan(count[:, :], one[:, :], here[:, :], 0.0, ALU.mult, ALU.add))
                    t.link(nc.vector.tensor_copy(total[:, bass.ds(b, 1)], count[:, COLS:COLS + 1]))
                    t.link(nc.vector.tensor_tensor(here[:, :], here[:, :], count[:, :], ALU.mult))
                    t.link(nc.vector.tensor_tensor(rank[:, :], rank[:, :], here[:, :], ALU.add))
                s.n = at + 5 * NT
                nc.vector.memset(tile_of[:, :], 0.0).then_inc(totals, 1)
                dve.wait_ge(summed, k + 1)
                s.link(nc.vector.tensor_scalar(size[:, :], kit.bank[1][:, 0:NT], float(G * P - 1), None, ALU.add))
                s.link(nc.vector.tensor_copy(size_i[:, :], size[:, :]))
                s.link(nc.vector.tensor_single_scalar(size_i[:, :], size_i[:, :], (G * P).bit_length() - 1, ALU.arith_shift_right))
                s.link(nc.vector.tensor_copy(groups_of[:, :], size_i[:, :]))
                s.link(nc.vector.tensor_tensor_scan(ends[:, :], one[:, 0:NT], groups_of[:, :], 0.0, ALU.mult, ALU.add))
                s.link(nc.vector.tensor_tensor(start[:, :], ends[:, :], groups_of[:, :], ALU.subtract))
                s.link(nc.vector.tensor_scalar(start[:, :], start[:, :], float(G * P), None, ALU.mult))
                s.link(nc.vector.scalar_tensor_tensor(out=base[:, :], in0=start[:, :], scalar=-1.0,
                                                      in1=kit.bank[0][:, 0:NT], op0=ALU.add, op1=ALU.add))
                at = s.n
                with dve.Fori(0, NT) as b:
                    t = Steps(dve, step, at + 2 * b)
                    t.link(nc.vector.tensor_scalar(here[:, :], bucket[:, :], bucket_no[:, bass.ds(b, 1)],
                                                   base[:, bass.ds(b, 1)], ALU.is_equal, ALU.mult))
                    t.link(nc.vector.tensor_tensor(rank[:, :], rank[:, :], here[:, :], ALU.add))
                s.n = at + 2 * NT
                s.link(nc.vector.tensor_copy(pos[:, :], rank[:, :]))
                s.link(nc.vector.tensor_copy(size[:, :], kit.bank[1][:, 0:NT]))
                s.link(nc.vector.tensor_tensor_scan(earlier[:, :], one[:, 0:NT], size[:, :], 0.0, ALU.mult, ALU.add))
                s.link(nc.vector.tensor_tensor(earlier[:, :], earlier[:, :], size[:, :], ALU.subtract))
                s.link(nc.vector.tensor_tensor(earlier[:, :], start[:, :], earlier[:, :], ALU.subtract))
                s.link(nc.vector.tensor_copy(pad[:, :], pad_no[:, :]))
                at = s.n
                with dve.Fori(0, NT) as b:
                    t = Steps(dve, step, at + 2 * b)
                    t.link(nc.vector.tensor_scalar(more[:, :], pad_no[:, :], earlier[:, bass.ds(b, 1)],
                                                   size[:, bass.ds(b, 1)], ALU.is_ge, ALU.mult))
                    t.link(nc.vector.tensor_tensor(pad[:, :], pad[:, :], more[:, :], ALU.add))
                s.n = at + 2 * NT
                s.link(nc.vector.tensor_copy(pads[:, :], pad[:, :]))
                at = s.n
                with dve.Fori(0, NT - 1) as b:
                    t = Steps(dve, step, at + b)
                    t.link(nc.vector.scalar_tensor_tensor(out=tile_of[:, :], in0=group_no[:, :], scalar=ends[0:1, bass.ds(b, 1)],
                                                          in1=tile_of[:, :], op0=ALU.is_ge, op1=ALU.add))
                s.n = at + NT - 1
                s.link(nc.vector.tensor_copy(tab[:, :], tile_of[:, :]))


def scatter_edges(kit, ins, pos_d, pos_s, pads_d, pads_s, recs_d, recs_s):
    nc = kit.nc
    STEPS = COLS // (2 * EB)
    with Phase(kit, "scat") as ph:
        w_edge = ph.sb("w_edge", [P, 2 * D])
        row = [ph.sb(f"row{u}", [P, EB, ROW]) for u in range(2)]
        idx = [ph.sb(f"idx{u}", [P, 2, EB], I32) for u in range(2)]
        attr_t = [ph.sb(f"attr_t{u}", [P, 3, P]) for u in range(2)]
        zero = ph.sb("zero", [P, ROW])
        rest_row = ph.sb("rest_row", [P, ROW])
        w_in = ph.sem("w_in")
        attr_in = [ph.sem(f"attr_in{u}") for u in range(2)]
        turned = ph.sem("turned")
        copied = ph.sem("copied")
        made = ph.sem("made")
        filled = ph.sem("filled")
        recs_in = [ph.sem(f"recs_in{u}") for u in range(2)]
        idx_in = ph.sem("idx_in")
        gone = [ph.sem(f"gone{u}") for u in range(2)]
        pads_gone, rest_in, cleared = ph.sem("pads_gone"), ph.sem("rest_in"), ph.sem("cleared")
        rest_done = ph.sem("rest_done")
        rest_gone = ph.sem("rest_gone")
        rest_turned, rest_copied, rest_made = ph.sem("rest_turned"), ph.sem("rest_copied"), ph.sem("rest_made")
        idx_order = ph.sem("idx_order")
        block = ph.block()

        def in_turns(eng, step):
            step(0)
            with eng.Fori(1, STEPS) as it:
                step(it)

        attr = ins["edge_attr_128"][0:COLS * P, :].rearrange("(p c) f -> p c f", c=COLS)

        @block.sync
        def _(sp):
            sp.dma_start(w_edge[:, 0:D], ins["L2_gnn_w1"][2 * D:3 * D, :]).then_inc(w_in, 16)
            sp.dma_start(w_edge[:, D:], ins["L2_gnn_w3"][D:2 * D, :]).then_inc(w_in, 16)
            sp.wait_ge(cleared, 1)
            sp.dma_start(rest_row[0:REST, REC:REC + D], ins["edge_attr_128"][COLS * P:EDGES, :]).then_inc(rest_in, 16)

            def step(it):
                for u in range(2):
                    wait_from(sp, gone[u], it * (EB * 2 * 16))
                    sp.dma_start(row[u][:, :, REC:REC + D], attr[:, bass.ds((it * 2 + u) * EB, EB), :])\
                        .then_inc(attr_in[u], 16)

            in_turns(sp, step)

        @block.tensor
        def _(pe):
            pe.wait_ge(w_in, 32)
            pe.wait_ge(rest_in, 16)
            nc.tensor.transpose(kit.bank[7][:, 0:P], rest_row[:, REC:REC + D], kit.ident[:, :]).then_inc(rest_turned, 1)
            pe.wait_ge(rest_copied, 1)
            nc.tensor.matmul(kit.bank[7][:, 0:2 * D], attr_t[0][:, 0, :], w_edge[:, :], start=True, stop=True)\
                .then_inc(rest_made, 1)
            pe.wait_ge(rest_done, 1)

            def step(it):
                for u in range(2):
                    pe.wait_ge(attr_in[u], (it + 1) * 16)
                    for half, (c0, n) in enumerate(((0, 3), (3, 2))):
                        t = kit.bank[half]
                        wait_from(pe, copied, it * 4 + 2 * u + half)
                        for c in range(n):
                            last = nc.tensor.transpose(t[:, c * P:(c + 1) * P], row[u][:, c0 + c, REC:REC + D], kit.ident[:, :])
                        last.then_inc(turned, 1)
                        pe.wait_ge(copied, it * 4 + 2 * u + half + 1)
                        wait_from(pe, filled, it * 4 + 2 * u + half)
                        for c in range(n):
                            b = kit.bank[2 + 2 * half + c // 2]
                            last = nc.tensor.matmul(b[:, (c % 2) * 2 * D:(c % 2 + 1) * 2 * D], attr_t[half][:, c, :], w_edge[:, :],
                                                    start=True, stop=True)
                        last.then_inc(made, 1)

            in_turns(pe, step)

        @block.scalar
        def _(act):
            act.wait_ge(rest_turned, 1)
            nc.scalar.copy(attr_t[0][:, 0, :], kit.bank[7][:, 0:P]).then_inc(rest_copied, 1)
            act.wait_ge(rest_done, 1)

            def step(it):
                for u in range(2):
                    for half, n in enumerate((3, 2)):
                        act.wait_ge(turned, it * 4 + 2 * u + half + 1)
                        nc.scalar.copy(attr_t[half][:, 0:n, :], kit.bank[half][:, 0:n * P].rearrange("p (c e) -> p c e", c=n))\
                            .then_inc(copied, 1)

            in_turns(act, step)

        @block.vector
        def _(dve):
            nc.vector.memset(rest_row[:, :], 0.0).then_inc(cleared, 1)
            nc.vector.memset(zero[:, :], 0.0).then_inc(cleared, 1)
            dve.wait_ge(cleared, 2)
            nc.vector.memset(zero[:, 0:1], -1.0).then_inc(cleared, 1)
            nc.vector.memset(zero[:, ROW - REC:ROW - REC + 1], -1.0).then_inc(cleared, 1)
            dve.wait_ge(rest_in, 16)
            nc.vector.tensor_copy(rest_row[:, 0:REC], recs_d[:, COLS, :])
            nc.vector.tensor_copy(rest_row[:, ROW - REC:], recs_s[:, COLS, :])
            dve.wait_ge(rest_made, 1)
            nc.vector.tensor_copy(rest_row[:, SROW0:SROW0 + 2 * D], kit.bank[7][:, 0:2 * D]).then_inc(rest_done, 1)

            def step(it):
                for u in range(2):
                    wait_from(dve, gone[u], it * (EB * 2 * 16))
                    nc.vector.tensor_copy(row[u][:, :, 0:REC], recs_d[:, bass.ds((it * 2 + u) * EB, EB), :]).then_inc(recs_in[u], 1)
                    nc.vector.tensor_copy(row[u][:, :, ROW - REC:], recs_s[:, bass.ds((it * 2 + u) * EB, EB), :]).then_inc(recs_in[u], 1)
                    for half, (c0, n) in enumerate(((0, 3), (3, 2))):
                        dve.wait_ge(made, it * 4 + 2 * u + half + 1)
                        for b in range((n + 1) // 2):
                            m = min(2, n - 2 * b)
                            last = nc.vector.tensor_copy(
                                row[u][:, c0 + 2 * b:c0 + 2 * b + m, SROW0:SROW0 + 2 * D],
                                kit.bank[2 + 2 * half + b][:, 0:m * 2 * D].rearrange("p (c f) -> p c f", c=m))
                        last.then_inc(filled, 1)

            in_turns(dve, step)

        @block.gpsimd
        def _(pool):
            def scatter(src, index, n, done, skip=False):
                for table, lo, hi, k in ((kit.rows_d, 0, DROW, 0), (kit.rows_s, SROW0, ROW, 1)):
                    pool.indirect_dma_start(
                        out=table[:, :], out_offset=bass.IndirectOffsetOnAxis(ap=index[k], axis=0),
                        in_=src[0:n, lo:hi], in_offset=None,
                        **(dict(bounds_check=SLOTS - 1, oob_is_err=False) if skip else {})).then_inc(done, 16)

            pool.wait_ge(rest_done, 1)
            scatter(rest_row, (pos_d[0:REST, COLS:COLS + 1], pos_s[0:REST, COLS:COLS + 1]), REST, rest_gone)
            pool.wait_ge(cleared, 4)
            for c in range(PADS):
                scatter(zero, (pads_d[:, c:c + 1], pads_s[:, c:c + 1]), P, pads_gone, skip=True)
            idx_ready, products_ready = Count(pool, "idx_ready", 4), Count(pool, "products_ready", 4)
            recs_ready = [Count(pool, f"recs_ready{u}", 2) for u in range(2)]


            def step(it):
                for u in range(2):
                    wait_from(pool, gone[u], it * (EB * 2 * 16))
                    pool.tensor_copy(idx[u][:, 0, :], pos_d[:, bass.ds((it * 2 + u) * EB, EB)]).then_inc(idx_in, 1)
                    pool.tensor_copy(idx[u][:, 1, :], pos_s[:, bass.ds((it * 2 + u) * EB, EB)]).then_inc(idx_in, 1)
                    if isinstance(it, int):
                        pool.wait_ge(idx_in, it * 4 + 2 * u + 2)
                        pool.wait_ge(recs_in[u], it * 2 + 2)
                        pool.wait_ge(filled, it * 4 + 2 * u + 2)
                    else:
                        for count in (idx_ready, recs_ready[u], products_ready):
                            count.step(2)
                        pool.wait_ge(rest_done, 1)
                        idx_ready.wait(idx_in)
                        recs_ready[u].wait(recs_in[u])
                        products_ready.wait(filled)
                    for c in range(EB):
                        scatter(row[u][:, c, :], (idx[u][:, 0, c:c + 1], idx[u][:, 1, c:c + 1]), P, gone[u])

            in_turns(pool, step)
            for u in range(2):
                pool.wait_ge(gone[u], STEPS * 2 * EB * 16)
            pool.wait_ge(pads_gone, 2 * 16 * PADS)
            pool.wait_ge(rest_gone, 32)


class Gather:

    def __init__(self, pool, name, kit, rec, table, idx, gat, width, gat_in, idx_in, ready, free):
        self.pool, self.rec, self.table, self.idx, self.gat, self.width = pool, rec, table, idx, gat, width
        self.gat_in, self.idx_in, self.ready, self.free = gat_in, idx_in, ready, free
        self.idx_count = Count(pool, name + "_idx", PEELED * U)
        self.counts = [Count(pool, f"{name}_free{k}", PEELED * per) for k, (_, per) in enumerate(free)]

    def __call__(self, g):
        pool, u = self.pool, g.u
        g.back(U).wait(self.gat_in, 16 * G)
        pool.tensor_copy(self.idx[u][:, :], self.rec[:, bass.ds(g.times(G), G), 1]).then_inc(self.idx_in, 1)
        if isinstance(g.it, int):
            pool.wait_ge(self.idx_in, g.times(1, 1))
            for sems, per in self.free:
                g.back(U).wait(sems, per)
        else:
            self.idx_count.step(1)
            pool.wait_ge(self.ready, 1)
            self.idx_count.wait(self.idx_in)
            for count, (sems, _) in zip(self.counts, self.free):
                count.wait(sems[u])
        for c in range(G):
            pool.indirect_dma_start(
                out=self.gat[u][:, c, 0:self.width], out_offset=None, in_=self.table,
                in_offset=bass.IndirectOffsetOnAxis(ap=self.idx[u][:, c:c + 1], axis=0)).then_inc(self.gat_in[u], 16)
        if not isinstance(g.it, int) and u == U - 1:
            for count, (_, per) in zip(self.counts, self.free):
                count.step(per)


class Group:

    def __init__(self, eng, known, it, offset, slots, turns):
        self.eng, self.known, self.it, self.offset, self.slots, self.turns = eng, known, it, offset, slots, turns
        self.u = offset % slots

    def value(self, mult, add):
        v = self.it * mult + add
        if isinstance(self.it, int):
            return v
        if (mult, add) not in self.known:
            self.known[mult, add] = self.eng.snap(v, min_val=PEELED * mult + add, max_val=mult * self.turns + add)
        return self.known[mult, add]

    def times(self, n, more=0):
        return self.value(self.slots * n, self.offset * n + more)

    def count(self, per=1, more=0):
        return self.value(per, (self.offset // self.slots + 1) * per + more)

    def wait(self, sems, per=1, before=0):
        if isinstance(self.it, int) and self.count(per) <= 0:
            return
        assert isinstance(self.it, int) or PEELED * self.slots + self.offset >= 0
        self.eng.wait_ge(sems[self.u], self.count(per, -before))

    def past(self, sem, per=1):
        if isinstance(self.it, int) and self.times(per, per) <= 0:
            return
        assert isinstance(self.it, int) or PEELED * self.slots + self.offset >= 0
        self.eng.wait_ge(sem, self.times(per, per))

    def back(self, n):
        return Group(self.eng, self.known, self.it, self.offset - n, self.slots, self.turns)


PEELED = 2


def over_groups(eng, *stages, slots=U, count=GROUPS):
    assert count % slots == 0
    turns = count // slots

    def turn(it):
        known = {}
        for u in range(slots):
            for lag, stage in stages:
                assert lag <= slots
                n = it * slots + u - lag if isinstance(it, int) else 0
                if 0 <= n < count:
                    stage(Group(eng, known, it, u - lag, slots, turns))

    for it in range(PEELED):
        turn(it)
    with eng.Fori(PEELED, turns) as it:
        turn(it)
    turn(turns)


def side(kit, by_src):
    return (kit.rec_s, kit.tile_s, kit.rows_s) if by_src else (kit.rec_d, kit.tile_d, kit.rows_d)


def load_records(kit, name):
    nc = kit.nc
    with Phase(kit, name) as ph:
        done = ph.sem("done")
        block = ph.block()

        @block.sync
        def _(sp):
            sp.dma_start(kit.rec_d[:, :, :], kit.rows_d[:, 0:REC].rearrange("(c p) f -> p c f", p=P)).then_inc(done, 16)
            sp.dma_start(kit.rec_s[:, :, :], kit.rows_s[:, SROW - REC:SROW].rearrange("(c p) f -> p c f", p=P)).then_inc(done, 16)
            sp.wait_ge(done, 32)


def make_one_hot(kit, oh, rec, g):
    return kit.nc.vector.tensor_tensor(
        oh[:, :, :], kit.node_of_col[:, :].unsqueeze(1).broadcast_to([P, G, P]),
        rec[:, bass.ds(g.times(G), G), 0:1].broadcast_to([P, G, P]), ALU.is_equal)


def node_tile(eng, tab, g):
    return eng.value_load(tab[0:1, bass.ds(g.times(1), 1)], min_val=0, max_val=NT - 1)


def turn_one_hot(kit, oh, bank):
    for c in range(G):
        last = kit.nc.tensor.matmul(bank[:, c * P:(c + 1) * P], oh[:, c, :], kit.ident4_bf[:, 0, :], start=True, stop=True)
    return last


def sum_group(kit, oh, x, width, bank):
    for c in range(G):
        last = kit.nc.tensor.matmul(bank[:, 0:width], oh[:, c, :], x[:, c, :], start=c == 0, stop=c == G - 1)
    return last


def add_sums(kit, dve, tab, g, summed, added, width):
    t = node_tile(dve, tab, g)
    g.wait(summed)
    g.back(1).wait(added)
    into = kit.acc[:, bass.ds(t, 1), 0:width].rearrange("p o w -> p (o w)")
    kit.nc.vector.tensor_tensor(into, into, kit.bank[g.u][:, 0:width], ALU.add).then_inc(added[g.u], 1)


def sum_pass(kit, name, by_src, rows=None, table=None, own=None):
    nc = kit.nc
    rec, tab, sorted_rows = side(kit, by_src)
    W = D + 1
    with Phase(kit, name) as ph:
        def each_slot(make, what, *args):
            return [make(f"{what}{u}", *args) for u in range(U)]

        oh = each_slot(ph.sb, "oh", [P, G, P])
        x = each_slot(ph.sb, "x", [P, G, W])
        idx = each_slot(ph.sb, "idx", [P, G], I32)
        if own is not None:
            gat = each_slot(ph.sb, "gat", [P, G, D])
            oht = each_slot(ph.sb, "oht", [P, G, P])
            oh_bf = each_slot(ph.sb, "oh_bf", [P, G, P], BF16)
        else:
            gat = x
        ready = ph.sem("ready")
        oh_in = each_slot(ph.sem, "oh_in")
        x_in = each_slot(ph.sem, "x_in")
        idx_in = ph.sem("idx_in")
        summed = each_slot(ph.sem, "summed")
        added = each_slot(ph.sem, "added")
        step = ph.sem("step")
        if own is not None:
            narrow = each_slot(ph.sem, "narrow")
            turned = each_slot(ph.sem, "turned")
            oht_in = each_slot(ph.sem, "oht_in")
            diff = each_slot(ph.sem, "diff")
            relued = each_slot(ph.sem, "relued")
        block = ph.block()

        @block.vector
        def _(dve):
            s = Steps(dve, step)
            for u in range(U):
                s.mark(nc.vector.memset(x[u][:, :, D:W], 1.0))
            s.mark(nc.vector.memset(kit.acc[:, :, :], 0.0))
            s.need(s.n)
            nc.vector.engine_nop().then_inc(ready, 1)

            def one_hot(g):
                g.back(U).wait(summed)
                make_one_hot(kit, oh[g.u], rec, g).then_inc(oh_in[g.u], 1)

            def add(g):
                add_sums(kit, dve, tab, g, summed, added, W)

            over_groups(dve, (0, one_hot), (3, add))

        @block.tensor
        def _(pe):
            pe.wait_ge(ready, 1)

            def turn(g):
                g.wait(narrow)
                g.back(2).wait(oht_in)
                turn_one_hot(kit, oh_bf[g.u], kit.bank[4 + g.u % 2]).then_inc(turned[g.u], 1)

            def difference(g):
                bank = kit.bank[6 + g.u % 2]
                t = node_tile(pe, tab, g)
                g.wait(x_in, 16 * G)
                g.back(2).wait(relued)
                nc.tensor.matmul(bank[:, :], kit.neg_ident[:, :], gat[g.u][:, :, :], start=True, stop=False)
                g.wait(oht_in)
                for c in range(G):
                    last = nc.tensor.matmul(bank[:, c * P:(c + 1) * P], oht[g.u][:, c, :],
                                            own[:, bass.ds(t, 1), :].rearrange("p o f -> p (o f)"), start=False, stop=c == G - 1)
                last.then_inc(diff[g.u], 1)

            def sums(g):
                if own is not None:
                    g.wait(relued)
                else:
                    g.wait(oh_in)
                    g.wait(x_in, 16 if rows is not None else 16 * G)
                g.back(U).wait(added)
                sum_group(kit, oh[g.u], x[g.u], W, kit.bank[g.u]).then_inc(summed[g.u], 1)

            if own is not None:
                over_groups(pe, (0, turn), (1, difference), (2, sums))
            else:
                over_groups(pe, (0, sums))

        if own is not None:
            @block.scalar
            def _(act):
                def narrow_oh(g):
                    g.wait(oh_in)
                    g.back(U).wait(turned)
                    nc.scalar.copy(oh_bf[g.u][:, :, :], oh[g.u][:, :, :]).then_inc(narrow[g.u], 1)

                def copy(g):
                    g.wait(turned)
                    g.back(U).wait(diff)
                    nc.scalar.copy(oht[g.u][:, :, :], by_tile(kit.bank[4 + g.u % 2])).then_inc(oht_in[g.u], 1)

                def relu(g):
                    g.wait(diff)
                    g.back(U).wait(summed)
                    nc.scalar.activation(x[g.u][:, :, 0:D], by_tile(kit.bank[6 + g.u % 2]), ACT.Relu).then_inc(relued[g.u], 1)

                over_groups(act, (0, narrow_oh), (0, copy), (1, relu))

        if rows is not None:
            @block.sync
            def _(sp):
                def load(g):
                    first = g.times(G * P)
                    g.back(U).wait(summed)
                    sp.dma_start(x[g.u][:, :, 0:D], slot_rows(sorted_rows[:, rows:rows + D], first)).then_inc(x_in[g.u], 16)

                over_groups(sp, (0, load))
        else:
            @block.gpsimd
            def _(pool):
                pool.wait_ge(ready, 1)
                free = diff if own is not None else summed
                over_groups(pool, (0, Gather(pool, name, kit, rec, table, idx, gat, D, x_in, idx_in, ready, [(free, 1)])))


def slot_rows(ap, first):
    return ap[bass.ds(first, G * P), :].rearrange("(c p) f -> p c f", p=P)


def score_pass(kit, name, by_src, layer, table, v_rows, own, alpha, node_max, extra):
    nc = kit.nc
    rec, tab, sorted_rows = side(kit, by_src)
    H = HEADS1 if layer == 1 else HEADS2
    CHUNK = 512 // (H * P)
    CHUNKS = G // CHUNK
    first_col = DROW - 2 * D if not by_src else 0
    LINED = 4 // CHUNKS

    def max_bank(g, q):
        return kit.bank[4 + (q if layer == 1 else 2 * (g.u % 2) + q)]

    with Phase(kit, name) as ph:
        def each_slot(make, what, *args):
            return [make(f"{what}{u}", *args) for u in range(U)]

        oh = each_slot(ph.sb, "oh", [P, G, P], BF16)
        oht = each_slot(ph.sb, "oht", [P, G, P])
        out_of = each_slot(ph.sb, "out_of", [P, G, P], BF16)
        gat = each_slot(ph.sb, "gat", [P, G, 2 * D])
        prod = each_slot(ph.sb, "prod", [P, G, D])
        logit = each_slot(ph.sb, "logit", [P, G, H])
        most = each_slot(ph.sb, "most", [P, G * H])
        most_of = each_slot(ph.sb, "most_of", [P, H])
        idx = each_slot(ph.sb, "idx", [P, G], I32)
        if layer == 1:
            term = each_slot(ph.sb, "term", [P, G, H])
            part = [each_slot(ph.sb, f"part{k}_", [P, G, H], BF16) for k in range(3)]
            rest = each_slot(ph.sb, "rest", [P, G, H])
        else:
            edge = each_slot(ph.sb, "edge", [P, G, 2 * D])
        ready = ph.sem("ready")
        oh_in = each_slot(ph.sem, "oh_in")
        gat_in = each_slot(ph.sem, "gat_in")
        idx_in = ph.sem("idx_in")
        turned = each_slot(ph.sem, "turned")
        oht_in = each_slot(ph.sem, "oht_in")
        out_in = each_slot(ph.sem, "out_in")
        spread = each_slot(ph.sem, "spread")
        multiplied = each_slot(ph.sem, "multiplied")
        reduced = each_slot(ph.sem, "reduced")
        scored = each_slot(ph.sem, "scored")
        kept = each_slot(ph.sem, "kept")
        lined = [each_slot(ph.sem, f"lined{q}_") for q in range(CHUNKS)]
        found = each_slot(ph.sem, "found")
        joined = each_slot(ph.sem, "joined")
        maxed = each_slot(ph.sem, "maxed")
        kept_v = each_slot(ph.sem, "kept_v")
        if layer == 1:
            splits = each_slot(ph.sem, "splits")
            termed = each_slot(ph.sem, "termed")
        else:
            edge_in = each_slot(ph.sem, "edge_in")
            joint = each_slot(ph.sem, "joint")
            leaked = each_slot(ph.sem, "leaked")
            hidden = each_slot(ph.sem, "hidden")
        block = ph.block()

        SPLITS = 5

        def turn_bank(g):
            return kit.bank[0 if layer == 1 else g.u % 2]

        @block.vector
        def _(dve):
            nc.vector.memset(node_max[:, :, :], -BIG).then_inc(ready, 1)
            dve.wait_ge(ready, 1)

            def one_hot(g):
                g.back(U).wait(turned)
                g.back(U).wait(out_in)
                make_one_hot(kit, oh[g.u], rec, g).then_inc(oh_in[g.u], 1)

            def join_edge(g):
                g.wait(edge_in, 16)
                g.wait(gat_in, 16 * G)
                nc.vector.tensor_tensor(edge[g.u][:, :, :], edge[g.u][:, :, :], gat[g.u][:, :, :], ALU.add).then_inc(joint[g.u], 1)

            def multiply(g):
                u, wide = g.u, D + H
                g.wait(spread)
                g.wait(gat_in, 16 * G)
                parts = [(0, G - 1, kit.bank[2 + u % 2][:, 0:(G - 1) * wide].rearrange("p (c f) -> p c f", f=wide)),
                         (G - 1, 1, kit.bank[1][:, 0:wide].rearrange("p (c f) -> p c f", f=wide))]
                for c, n, bank in parts:
                    last = nc.vector.tensor_tensor(prod[u][:, c:c + n, :], bank[:, :, 0:D], gat[u][:, c:c + n, 0:D], ALU.mult)
                last.then_inc(multiplied[u], 1)
                for c, n, bank in parts:
                    last = nc.vector.tensor_tensor(term[u][:, c:c + n, :], bank[:, :, D:wide],
                                                   rec[:, bass.ds(g.times(G, c), n), 2:3].broadcast_to([P, n, H]), ALU.mult)
                last.then_inc(termed[u], 1)

            def leaky(g):
                u = g.u
                g.wait(leaked)
                nc.vector.scalar_tensor_tensor(out=prod[u][:, :, :], in0=by_tile(kit.bank[2 + u % 2]),
                                               scalar=SLOPE, in1=prod[u][:, :, :], op0=ALU.mult, op1=ALU.add).then_inc(hidden[u], 1)

            def times_w2(g):
                u = g.u
                g.wait(hidden)
                nc.vector.tensor_tensor(prod[u][:, :, :], prod[u][:, :, :], each(extra), ALU.mult).then_inc(multiplied[u], 1)

            def reduce(g):
                u = g.u
                g.wait(multiplied)
                g.back(U).wait(kept)
                g.back(U).wait(lined[CHUNKS - 1])
                nc.vector.tensor_reduce(out=logit[u][:, :, :], in_=prod[u][:, :, :].rearrange("p c (h f) -> p c h f", h=H),
                                        axis=AX.X, op=ALU.add).then_inc((reduced if layer == 1 else scored)[u], 1)

            def add_term(g):
                u = g.u
                g.wait(termed)
                g.wait(reduced)
                nc.vector.tensor_tensor(logit[u][:, :, :], logit[u][:, :, :], term[u][:, :, :], ALU.add).then_inc(scored[u], 1)

            def split(k):
                def take(g):
                    u = g.u
                    left = logit[u] if k < 2 else rest[u]
                    if k:
                        g.wait(splits, SPLITS, SPLITS - k)
                    else:
                        g.wait(scored)
                    if k % 2:
                        nc.vector.tensor_tensor(rest[u][:, :, :], left[:, :, :], part[k // 2][u][:, :, :], ALU.subtract).then_inc(splits[u], 1)
                    else:
                        nc.vector.tensor_copy(part[k // 2][u][:, :, :], left[:, :, :]).then_inc(splits[u], 1)
                return take

            tiles = {}

            def chunk_max(q):
                def take(g):
                    if q == CHUNKS - 1:
                        tiles[g.u] = node_tile(dve, tab, g)
                    g.wait(lined[q])
                    nc.vector.tensor_reduce(out=most[g.u][:, q * CHUNK * H:(q + 1) * CHUNK * H],
                                            in_=max_bank(g, q)[:, :].rearrange("p (c e) -> p c e", e=P),
                                            axis=AX.X, op=ALU.max).then_inc(found[g.u], 1)
                return take

            def join(g):
                g.wait(found, CHUNKS)
                nc.vector.tensor_reduce(out=most_of[g.u][:, :], in_=most[g.u][:, :].rearrange("p (c h) -> p h c", h=H),
                                        axis=AX.X, op=ALU.max).then_inc(joined[g.u], 1)

            def update(g):
                t = tiles[g.u]
                g.wait(joined)
                g.back(1).wait(maxed)
                into = node_max[:, bass.ds(t, 1), 0:H].rearrange("p o w -> p (o w)")
                nc.vector.tensor_tensor(into, into, most_of[g.u][:, :], ALU.max).then_inc(maxed[g.u], 1)

            if layer == 1:
                over_groups(dve, (2, multiply), (0, one_hot), (2, reduce), (4, chunk_max(0)), (2, add_term),
                            (4, chunk_max(1)), (2, split(0)), (4, chunk_max(2)), (2, split(1)), (4, chunk_max(3)),
                            (2, split(2)), (2, split(3)), (4, join), (2, split(4)), (4, update))
            else:
                over_groups(dve, (0, one_hot), (1, join_edge), (2, leaky), (4, chunk_max(0)), (2, times_w2), (4, chunk_max(1)),
                            (2, reduce), (4, join), (4, update))

        @block.tensor
        def _(pe):
            def turn(g):
                g.wait(oh_in)
                g.back(1 if layer == 1 else 2).wait(oht_in)
                turn_one_hot(kit, oh[g.u], turn_bank(g)).then_inc(turned[g.u], 1)

            def spread_own(g):
                bank = kit.bank[2 + g.u % 2]
                t = node_tile(pe, tab, g)
                g.wait(oht_in)
                if layer == 1:
                    g.back(2).wait(termed)
                else:
                    g.back(2).wait(hidden)
                wide = D + H if layer == 1 else D
                rows = own[:, bass.ds(t, 1), 0:wide].rearrange("p o f -> p (o f)")
                for c in range(G):
                    if layer == 1 and c == G - 1:
                        g.back(1).wait(termed)
                        into = kit.bank[1][:, 0:wide]
                    else:
                        into = bank[:, c * wide:(c + 1) * wide]
                    last = nc.tensor.matmul(into, oht[g.u][:, c, :],
                                            rows, start=layer == 1 or c == 0, stop=layer == 1)
                if layer == 2:
                    g.wait(joint)
                    last = nc.tensor.matmul(bank[:, :], kit.ident[:, :], edge[g.u][:, :, 0:D], start=False, stop=True)
                last.then_inc(spread[g.u], 1)

            def line(g):
                g.wait(out_in)
                if layer == 1:
                    g.wait(splits, SPLITS)
                    lines = [(p[g.u], kit.ident4_bf[:, 0, :]) for p in part]
                else:
                    g.wait(scored)
                    lines = [(logit[g.u], kit.ident[:, :])]
                for q in range(CHUNKS):
                    b = max_bank(g, q)
                    g.back(LINED).wait(found, CHUNKS, CHUNKS - 1 - q)
                    for k in range(CHUNK):
                        c = q * CHUNK + k
                        nc.tensor.matmul(b[:, k * H * P:(k + 1) * H * P], out_of[g.u][:, c, :], kit.ident4_bf[:, 0:H, :], start=True, stop=False)
                        for h in range(H):
                            o = (k * H + h) * P
                            for k2, (line_of, ident) in enumerate(lines):
                                last = nc.tensor.matmul(b[:, o:o + P], line_of[:, c, h:h + 1].broadcast_to([P, P]), ident,
                                                        start=False, stop=h == H - 1 and k2 == len(lines) - 1)
                    last.then_inc(lined[q][g.u], 1)

            over_groups(pe, (0, turn), (1, spread_own), (3, line))

        @block.scalar
        def _(act):
            def copy_turned(g):
                g.wait(turned)
                g.back(U).wait(spread)
                nc.scalar.copy(oht[g.u][:, :, :], by_tile(turn_bank(g))).then_inc(oht_in[g.u], 1)
                g.back(U).wait(lined[CHUNKS - 1])
                nc.scalar.activation(out_of[g.u][:, :, :], oh[g.u][:, :, :], ACT.Copy, bias=-BIG, scale=BIG).then_inc(out_in[g.u], 1)

            def leak(g):
                g.wait(spread)
                g.back(U).wait(scored)
                nc.scalar.activation(prod[g.u][:, :, :], by_tile(kit.bank[2 + g.u % 2]), ACT.Relu, scale=1.0 - SLOPE)\
                    .then_inc(leaked[g.u], 1)

            def keep(g):
                first = g.times(G)
                g.wait(scored)
                nc.scalar.copy(alpha[:, bass.ds(first, G), 0:H], logit[g.u][:, :, :]).then_inc(kept[g.u], 1)

            if layer == 1:
                over_groups(act, (0, copy_turned), (3, keep))
            else:
                over_groups(act, (0, copy_turned), (1, leak), (3, keep))

        @block.sync
        def _(sp):
            def load(g):
                first = g.times(G * P)
                sp.wait_ge(ready, 1)
                g.back(U).wait(spread)
                g.back(U).wait(kept_v, 16)
                sp.dma_start(edge[g.u][:, :, :], slot_rows(sorted_rows[:, first_col:first_col + 2 * D], first)).then_inc(edge_in[g.u], 16)

            def keep_values(g):
                first = g.times(G * D)
                sp.wait_ge(ready, 1)
                if layer == 1:
                    g.wait(gat_in, 16 * G)
                else:
                    g.wait(joint)
                value = (gat if layer == 1 else edge)[g.u][:, :, D:2 * D]
                sp.dma_start(v_rows.rearrange("p c f -> p (c f)")[:, bass.ds(first, G * D)].rearrange("p (c f) -> p c f", f=D), value)\
                    .then_inc(kept_v[g.u], 16)

            if layer == 1:
                over_groups(sp, (0, keep_values))
            else:
                over_groups(sp, (4, keep_values), (0, load))
            for u in range(U):
                sp.wait_ge(kept_v[u], TURNS * 16)

        @block.gpsimd
        def _(pool):
            pool.wait_ge(ready, 1)
            free = [(multiplied, 1), (kept_v, 16)] if layer == 1 else [(joint, 1)]
            over_groups(pool, (0, Gather(pool, name, kit, rec, table, idx, gat, 2 * D, gat_in, idx_in, ready, free)))


def weigh_pass(kit, name, by_src, layer, v_rows, alpha, node_max):
    nc = kit.nc
    rec, tab, _ = side(kit, by_src)
    H = HEADS1 if layer == 1 else HEADS2
    C = D // H
    W = D + 2 * H if layer == 1 else D + H
    PARTS = 2 if layer == 1 else 1
    with Phase(kit, name) as ph:
        def each_slot(make, what, *args):
            return [make(f"{what}{u}", *args) for u in range(U)]

        oh = each_slot(ph.sb, "oh", [P, G, P])
        oht = each_slot(ph.sb, "oht", [P, G, P], BF16)
        max_part = [ph.sb(f"max_part{k}", [P, NTG, H], BF16) for k in range(3)]
        max_rest = ph.sb("max_rest", [P, NTG, H])
        oh_bf = each_slot(ph.sb, "oh_bf", [P, G, P], BF16)
        value = each_slot(ph.sb, "value", [P, G, D])
        w = each_slot(ph.sb, "w", [P, G, W])
        below = each_slot(ph.sb, "below", [P, G, H])
        ready = ph.sem("ready")
        oh_in = each_slot(ph.sem, "oh_in")
        narrow = each_slot(ph.sem, "narrow")
        turned = each_slot(ph.sem, "turned")
        oht_in = each_slot(ph.sem, "oht_in")
        spread = each_slot(ph.sem, "spread")
        less = each_slot(ph.sem, "less")
        capped = each_slot(ph.sem, "capped")
        raised = each_slot(ph.sem, "raised")
        value_in = each_slot(ph.sem, "value_in")
        weighed = each_slot(ph.sem, "weighed")
        summed = each_slot(ph.sem, "summed")
        added = each_slot(ph.sem, "added")
        READY = 7
        block = ph.block()

        @block.vector
        def _(dve):
            s = Steps(dve, ready)
            s.mark(nc.vector.memset(kit.acc[:, :, :], 0.0))
            s.link(nc.vector.tensor_copy(max_rest[:, :, :], node_max[:, :, 0:H]))
            for k in range(3):
                s.link(nc.vector.tensor_copy(max_part[k][:, :, :], max_rest[:, :, :]))
                if k < 2:
                    s.link(nc.vector.tensor_tensor(max_rest[:, :, :], max_rest[:, :, :], max_part[k][:, :, :], ALU.subtract))
            assert s.n == READY

            def one_hot(g):
                g.back(U).wait(summed)
                make_one_hot(kit, oh[g.u], rec, g).then_inc(oh_in[g.u], 1)

            def subtract(g):
                first = g.times(G)
                g.wait(spread)
                g.back(U).wait(raised)
                nc.vector.tensor_tensor(below[g.u][:, :, :], alpha[:, bass.ds(first, G), 0:H],
                                        kit.bank[6 + g.u % 2][:, 0:G * H].rearrange("p (c h) -> p c h", c=G), ALU.subtract)\
                    .then_inc(less[g.u], 1)

            def cap(g):
                g.wait(less)
                nc.vector.tensor_scalar(below[g.u][:, :, :], below[g.u][:, :, :], 0.0, None, ALU.min).then_inc(capped[g.u], 1)

            def weigh(g):
                u = g.u
                first = g.times(G)
                g.wait(raised)
                g.wait(value_in, 16)
                nc.vector.tensor_tensor(w[u][:, :, 0:D].rearrange("p c (h f) -> p c h f", h=H),
                                        value[u][:, :, :].rearrange("p c (h f) -> p c h f", h=H),
                                        w[u][:, :, D:D + H].unsqueeze(3).broadcast_to([P, G, H, C]), ALU.mult).then_inc(weighed[u], 1)
                if layer == 1:
                    nc.vector.tensor_tensor(w[u][:, :, D + H:W], w[u][:, :, D:D + H],
                                            rec[:, bass.ds(first, G), 2:3].broadcast_to([P, G, H]), ALU.mult).then_inc(weighed[u], 1)

            def add(g):
                add_sums(kit, dve, tab, g, summed, added, W)

            over_groups(dve, (3, weigh), (0, one_hot), (2, subtract), (2, cap), (4, add))

        @block.tensor
        def _(pe):
            def turn(g):
                g.wait(narrow)
                g.back(2).wait(oht_in)
                turn_one_hot(kit, oh_bf[g.u], kit.bank[4 + g.u % 2]).then_inc(turned[g.u], 1)

            def spread_max(g):
                t = node_tile(pe, tab, g)
                g.wait(oht_in)
                g.back(2).wait(less)
                for c in range(G):
                    for k in range(3):
                        last = nc.tensor.matmul(kit.bank[6 + g.u % 2][:, c * H:(c + 1) * H], oht[g.u][:, c, :],
                                                max_part[k][:, bass.ds(t, 1), :].rearrange("p o f -> p (o f)"),
                                                start=k == 0, stop=k == 2)
                last.then_inc(spread[g.u], 1)

            def sums(g):
                g.wait(weighed, PARTS)
                g.back(U).wait(added)
                sum_group(kit, oh[g.u], w[g.u], W, kit.bank[g.u]).then_inc(summed[g.u], 1)

            pe.wait_ge(ready, READY)
            over_groups(pe, (3, sums), (0, turn), (1, spread_max))

        @block.scalar
        def _(act):
            def copy_turned(g):
                g.wait(turned)
                g.back(U).wait(spread)
                nc.scalar.copy(oht[g.u][:, :, :], by_tile(kit.bank[4 + g.u % 2])).then_inc(oht_in[g.u], 1)

            def narrow_oh(g):
                g.wait(oh_in)
                g.back(U).wait(turned)
                nc.scalar.copy(oh_bf[g.u][:, :, :], oh[g.u][:, :, :]).then_inc(narrow[g.u], 1)

            def raise_(g):
                g.wait(capped)
                g.back(U).wait(summed)
                nc.scalar.activation(w[g.u][:, :, D:D + H], below[g.u][:, :, :], ACT.Exp).then_inc(raised[g.u], 1)

            over_groups(act, (0, narrow_oh), (2, raise_), (1, copy_turned))

        @block.sync
        def _(sp):
            def load(g):
                first = g.times(G)
                g.back(U).wait(weighed, PARTS)
                sp.dma_start(value[g.u][:, :, :], v_rows[:, bass.ds(first, G), :]).then_inc(value_in[g.u], 16)

            over_groups(sp, (0, load))


class Norm:

    def __init__(self, kit, ph, groups, width, tag="norm"):
        self.kit, self.width, self.groups = kit, width, groups
        self.sq = ph.sb(f"{tag}_sq", [P, groups, width])
        self.mean = ph.sb(f"{tag}_mean", [P, groups])
        self.var = ph.sb(f"{tag}_var", [P, groups])
        self.std = ph.sb(f"{tag}_std", [P, groups])
        self.inv = ph.sb(f"{tag}_inv", [P, groups])
        self.asked, self.rooted = ph.sem(f"{tag}_asked"), ph.sem(f"{tag}_rooted")

    def wide(self, ap):
        return ap[:, :].unsqueeze(2).broadcast_to([P, self.groups, self.width])

    def on_vector(self, dve, s, x, out, turn, scale=None, shift=None):
        v, n = self.kit.nc.vector, self.width
        s.link(v.tensor_reduce(out=self.mean[:, :], in_=x, axis=AX.X, op=ALU.add))
        s.link(v.tensor_scalar(self.mean[:, :], self.mean[:, :], 1.0 / n, None, ALU.mult))
        s.link(v.tensor_tensor(out, x, self.wide(self.mean), ALU.subtract))
        s.link(v.tensor_tensor(self.sq[:, :, :], out, out, ALU.mult))
        s.link(v.tensor_reduce(out=self.var[:, :], in_=self.sq[:, :, :], axis=AX.X, op=ALU.add))
        v.tensor_scalar(self.var[:, :], self.var[:, :], 1.0 / n, EPS, ALU.mult, ALU.add).then_inc(self.asked, 1)
        dve.wait_ge(self.rooted, turn)
        s.link(v.reciprocal(self.inv[:, :], self.std[:, :]))
        s.link(v.tensor_tensor(out, out, self.wide(self.inv), ALU.mult))
        if scale is not None:
            s.link(v.tensor_tensor(out, out, scale, ALU.mult))
            s.link(v.tensor_tensor(out, out, shift, ALU.add))
        s.link(v.tensor_scalar(out, out, 0.0, None, ALU.max))

    def on_scalar(self, act, turn):
        act.wait_ge(self.asked, turn)
        self.kit.nc.scalar.activation(self.std[:, :], self.var[:, :], ACT.Sqrt).then_inc(self.rooted, 1)


NORM_STEPS = 8


def node_pass(kit, name, loads, sources, weights, outputs, stores, scratch=(), wide=(), before=None, after=None,
              norm_before=False, norm_after=False, steps=(0, 0)):
    nc = kit.nc
    wide = dict(wide)
    biases = {f"bias{o}": b for o, (_, b) in enumerate(outputs) if b is not None}
    with Phase(kit, name) as ph:
        shared = {n: ph.sb(n, [P, D]) for n in [*weights, *wide]}
        shared.update({n: ph.sb(n, [1, D]) for n in biases})
        norm = Norm(kit, ph, G, D) if norm_before or norm_after else None
        shared["norm"] = norm
        t = [{**shared, **{n: ph.sb(f"{n}_{u}", [P, G, D]) for n in [*loads, *scratch]}} for u in range(2)]
        src_t = [ph.sb(f"src_t{k}", [P, G, P]) for k in range(len(sources))]

        def two(what):
            return [ph.sem(f"{what}{u}") for u in range(2)]

        const_in = ph.sem("const_in")
        loaded = two("loaded")
        prepared = two("prepared")
        turned = two("turned")
        copied = two("copied")
        made = two("made")
        ended = two("ended")
        stored = two("stored")
        step_before, step_after = ph.sem("step_before"), ph.sem("step_after")
        block = ph.block()
        consts = len(weights) + len(wide) + len(biases)
        mark = ph.sb("mark", [1, 1])
        mark2 = ph.sb("mark2", [1, 1])

        @block.sync
        def _(sp):
            for n, ap in weights.items():
                sp.dma_start(shared[n][:, :], ap).then_inc(const_in, 16)
            for n, ap in wide.items():
                sp.dma_start(shared[n][:, :], rows_of(ap).broadcast_to([P, D])).then_inc(const_in, 16)
            for n, ap in biases.items():
                sp.dma_start(shared[n][:, :], rows_of(ap)).then_inc(const_in, 16)
            if consts:
                sp.wait_ge(const_in, 16 * consts)

            def load(g):
                first = g.times(G * P)
                sp.wait_ge(const_in, 16 * consts)
                if stores:
                    g.back(2).wait(stored, 16 * len(stores))
                else:
                    g.back(2).wait(ended)
                for n, ap in loads.items():
                    sp.dma_start(t[g.u][n][:, :, :], slot_rows(ap, first)).then_inc(loaded[g.u], 16)

            def store(g):
                first = g.times(G * P)
                sp.wait_ge(const_in, 16 * consts)
                g.wait(ended)
                for n, ap in stores:
                    sp.dma_start(slot_rows(ap, first), t[g.u][n][:, :, :]).then_inc(stored[g.u], 16)

            stages = ([(0, load)] if loads else []) + ([(1, store)] if stores else [])
            over_groups(sp, *stages, slots=2, count=NG)
            if stores:
                for u in range(2):
                    sp.wait_ge(stored[u], NG // 2 * 16 * len(stores))

        @block.vector
        def _(dve):
            if consts:
                dve.wait_ge(const_in, 16 * consts)

            def prepare(g):
                if loads:
                    g.wait(loaded, 16 * len(loads))
                if stores:
                    g.back(2).wait(stored, 16 * len(stores))
                s = Steps(dve, step_before, g.times(steps[0]))
                if before:
                    before(dve, s, g, t[g.u])
                assert s.n == steps[0], (name, s.n)
                nc.vector.memset(mark[:, :], 0.0).then_inc(prepared[g.u], 1)
                g.wait(prepared)

            def finish(g):
                if outputs:
                    g.wait(made)
                s = Steps(dve, step_after, g.times(steps[1]))
                if after:
                    after(dve, s, g, t[g.u], kit.bank[4:8])
                assert s.n == steps[1], (name, s.n)
                nc.vector.memset(mark2[:, :], 0.0).then_inc(ended[g.u], 1)
                g.wait(ended)

            over_groups(dve, (0, prepare), (1, finish), slots=2, count=NG)

        if outputs:
            @block.tensor
            def _(pe):
                if consts:
                    pe.wait_ge(const_in, 16 * consts)

                def multiply(g):
                    g.wait(prepared)
                    g.back(1).wait(copied, len(sources))
                    for k, n in enumerate(sources):
                        for c in range(G):
                            last = nc.tensor.transpose(kit.bank[k][:, c * P:(c + 1) * P], t[g.u][n][:, c, :], kit.ident[:, :])
                    last.then_inc(turned[g.u], 1)
                    g.wait(copied, len(sources))
                    g.back(1).wait(ended)
                    for o, (terms, bias) in enumerate(outputs):
                        for c in range(G):
                            out = kit.bank[4 + o][:, c * P:(c + 1) * P]
                            for m, (k, n) in enumerate(terms):
                                last = nc.tensor.matmul(out, src_t[k][:, c, :], shared[n][:, :], start=m == 0,
                                                        stop=bias is None and m == len(terms) - 1)
                            if bias is not None:
                                last = nc.tensor.matmul(out, kit.ones[0:1, :], shared[f"bias{o}"][:, :], start=False, stop=True)
                    last.then_inc(made[g.u], 1)

                over_groups(pe, (0, multiply), slots=2, count=NG)

        @block.scalar
        def _(act):
            def root(g):
                norm.on_scalar(act, g.times(1, 1))

            def copy(g):
                g.wait(turned)
                g.back(1).wait(made)
                for k in range(len(sources)):
                    nc.scalar.copy(src_t[k][:, :, :], kit.bank[k][:, :].rearrange("p (c e) -> p c e", c=G)).then_inc(copied[g.u], 1)

            stages = ([(0, root)] if norm_before else []) + ([(0, copy)] if outputs else []) + ([(1, root)] if norm_after else [])
            if stages:
                over_groups(act, *stages, slots=2, count=NG)


def by_tile(bank):
    return bank[:, :].rearrange("p (c f) -> p c f", c=G)


def each(ap):
    return ap[:, :].unsqueeze(1).broadcast_to([P, G, D])


def degree(kit, g, t):
    return kit.acc[:, bass.ds(g.times(G), G), D:D + 1].broadcast_to([P, G, D])


def pad_nodes(kit, x, padded, late):
    nc = kit.nc
    with Phase(kit, "pad") as ph:
        zeros = ph.sb("zeros", [P, D])
        clear, done = ph.sem("clear"), ph.sem("done")
        block = ph.block()
        over = NTG * P - NODES

        @block.vector
        def _(dve):
            nc.vector.memset(zeros[:, :], 0.0).then_inc(clear, 1)

        @block.sync
        def _(sp):
            sp.dma_start(padded[0:NODES, :], x).then_inc(done, 16)
            sp.wait_ge(clear, 1)
            n = 1
            for r in range(0, over, P):
                m = min(P, over - r)
                sp.dma_start(padded[NODES + r:NODES + r + m, :], zeros[0:m, :]).then_inc(done, 16)
                n += 1
            for rows in late:
                for c in range(NT, NTG):
                    sp.dma_start(rows[c * P:(c + 1) * P, :], zeros[:, :]).then_inc(done, 16)
                    n += 1
            sp.wait_ge(done, 16 * n)


def layer_0(kit, ins, x0, x1, h1):
    nc, v = kit.nc, kit.nc.vector
    edge_agg, y = kit.dram("edge_agg", (NTG * P, D)), kit.dram("y0", (NTG * P, D))
    sum_pass(kit, "l0_edges", False, rows=REC)

    def take_sums(dve, s, g, t):
        s.link(v.tensor_copy(t["sums"][:, :, :], kit.acc[:, bass.ds(g.times(G), G), 0:D]))
        s.link(v.tensor_tensor(t["out"][:, :, :], degree(kit, g, t), each(t["be"]), ALU.mult))

    def add_bias(dve, s, g, t, banks):
        s.link(v.tensor_tensor(t["out"][:, :, :], t["out"][:, :, :], by_tile(banks[0]), ALU.add))

    node_pass(kit, "l0_agg", {}, ["sums"], {"we": ins["L0_gnn_We"]}, [([(0, "we")], None)], [("out", edge_agg)],
              scratch=("sums", "out"), wide={"be": ins["L0_gnn_be"]}, before=take_sums, after=add_bias, steps=(2, 1))

    def norm(dve, s, g, t):
        t["norm"].on_vector(dve, s, t["x"][:, :, :], t["h"][:, :, :], g.times(1, 1))

    def keep(dve, s, g, t, banks):
        s.link(v.tensor_copy(t["out"][:, :, :], by_tile(banks[0])))

    node_pass(kit, "l0_y", {"x": x0, "agg": edge_agg}, ["h", "agg"], {"w1a": ins["L0_gnn_W1"][0:D, :], "w1b": ins["L0_gnn_W1"][D:2 * D, :]},
              [([(0, "w1a"), (1, "w1b")], None)], [("out", y)], scratch=("h", "out"), before=norm, after=keep,
              norm_before=True, steps=(NORM_STEPS, 1))
    sum_pass(kit, "l0_neigh", False, table=y)

    def inner(dve, s, g, t):
        s.link(v.tensor_tensor(t["u"][:, :, :], t["y"][:, :, :], kit.acc[:, bass.ds(g.times(G), G), 0:D], ALU.add))
        s.link(v.tensor_tensor(t["u"][:, :, :], t["u"][:, :, :], each(t["b1"]), ALU.add))
        s.link(v.tensor_scalar(t["u"][:, :, :], t["u"][:, :, :], 0.0, None, ALU.max))

    node_pass(kit, "l0_out", {"x": x0, "y": y}, ["u"], {"w2": ins["L0_gnn_W2"]}, [([(0, "w2")], ins["L0_gnn_b2"])],
              [("x", x1), ("h", h1)], scratch=("u", "h"), wide={"b1": ins["L0_gnn_b1"]}, before=inner, after=add_and_norm,
              norm_after=True, steps=(3, 1 + NORM_STEPS))


def add_and_norm(dve, s, g, t, banks):
    v = t["norm"].kit.nc.vector
    s.link(v.tensor_tensor(t["x"][:, :, :], t["x"][:, :, :], by_tile(banks[0]), ALU.add))
    t["norm"].on_vector(dve, s, t["x"][:, :, :], t["h"][:, :, :], g.times(1, 1))


def layer_1(kit, ins, ph, h1, h_out, own, alpha, node_max, v_rows, kv):
    nc, v = kit.nc, kit.nc.vector
    h = [kit.dram(f"l1_h{k}", (NTG * P, D)) for k in range(2)] + [h_out]
    skip = kit.dram("l1_skip", (NTG * P, D))
    C = D // HEADS1

    def relu(dve, s, g, t, banks):
        s.link(v.tensor_scalar(t["out"][:, :, :], by_tile(banks[0]), 0.0, None, ALU.max))

    node_pass(kit, "l1_in", {"x": h1}, ["x"], {"w": ins["L1_gnn_W_in"]}, [([(0, "w")], ins["L1_gnn_b_in"])], [("out", h[0])],
              scratch=("out",), after=relu, steps=(0, 1))
    for l in range(2):
        def tables(dve, s, g, t, banks):
            mine = own[:, bass.ds(g.times(G), G), 0:D]
            s.mark(v.tensor_scalar(mine, by_tile(banks[0]), float(C) ** -0.5, None, ALU.mult))
            s.mark(v.tensor_copy(t["k"][:, :, :], by_tile(banks[1])))
            s.mark(v.tensor_copy(t["v"][:, :, :], by_tile(banks[2])))
            s.mark(v.tensor_copy(t["r"][:, :, :], by_tile(banks[3])))
            s.need(s.n)
            s.link(v.tensor_tensor(t["qw"][:, :, :], mine, each(t["we"]), ALU.mult))
            s.link(v.tensor_reduce(out=own[:, bass.ds(g.times(G), G), D:D + HEADS1],
                                   in_=t["qw"][:, :, :].rearrange("p c (h f) -> p c h f", h=HEADS1), axis=AX.X, op=ALU.add))

        node_pass(kit, f"l1_tables{l}", {"h": h[l]}, ["h"],
                  {n: ins[f"L1_gnn_{n}"][l] for n in ("Wq", "Wk", "Wv", "Wskip")},
                  [([(0, "Wq")], ins["L1_gnn_bq"][l]), ([(0, "Wk")], ins["L1_gnn_bk"][l]), ([(0, "Wv")], ins["L1_gnn_bv"][l]),
                   ([(0, "Wskip")], ins["L1_gnn_bskip"][l])],
                  [("k", kv[:, 0:D]), ("v", kv[:, D:2 * D]), ("r", skip)], scratch=("k", "v", "r", "qw"),
                  wide={"we": ins["L1_gnn_We"][l, 0]}, after=tables, steps=(0, 6))
        score_pass(kit, f"l1_score{l}", False, 1, kv, v_rows, own, alpha, node_max, None)
        weigh_pass(kit, f"l1_weigh{l}", False, 1, v_rows, alpha, node_max)
        mix_and_batchnorm(kit, ins, l, skip, h[l], h[l + 1], own[:, :, 0:D])


def mix_and_batchnorm(kit, ins, l, skip, h_in, h_out, out):
    nc, v = kit.nc, kit.nc.vector
    C = D // HEADS1
    H = HEADS1
    whole = [P, NTG, D]
    with Phase(kit, f"mix{l}") as ph:
        r = ph.sb("r", whole)
        tmp = ph.sb("tmp", whole)
        den = ph.sb("den", [P, NTG, H])
        beta = ph.sb("beta", [P, NTG])
        more = ph.sb("more", [P, NTG])
        vec = {n: ph.sb(n, [P, D]) for n in ("we", "wb_out", "wb_r", "wb_diff", "gamma", "shift")}
        wb = ph.sb("wb", [P, 2, D])
        real = ph.sb("real", [P, 1])
        mean, var, std, factor = (ph.sb(n, [P, D]) for n in ("mean", "var", "std", "factor"))
        loaded, step, stored = ph.sem("loaded"), ph.sem("step"), ph.sem("stored")
        free_r = ph.sem("free_r")
        sig_in, sig_out = ph.sem("sig_in"), ph.sem("sig_out")
        to_sum, summed = ph.sem("to_sum"), ph.sem("summed")
        root_in, root_out = ph.sem("root_in"), ph.sem("root_out")
        block = ph.block()
        wbeta = ins["L1_gnn_Wbeta"][l].rearrange("(k f) o -> k (f o)", k=3)
        small = (("we", ins["L1_gnn_We"][l, 0]), ("wb_out", wbeta[0]), ("wb_r", wbeta[1]), ("wb_diff", wbeta[2]),
                 ("gamma", ins["L1_gnn_bn_gamma"][l]), ("shift", ins["L1_gnn_bn_beta"][l]))

        def all_rows(ap):
            return ap.rearrange("(c p) f -> p c f", p=P)

        def over(ap):
            return ap[:, :].unsqueeze(1).broadcast_to(whole)

        def along(ap):
            return ap[:, :].unsqueeze(2).broadcast_to(whole)

        def by_head(ap):
            return ap.rearrange("p c (h f) -> p c h f", h=H)

        @block.sync
        def _(sp):
            sp.dma_start(r[:, :, :], all_rows(skip)).then_inc(loaded, 16)
            for n, ap in small:
                sp.dma_start(vec[n][:, :], rows_of(ap).broadcast_to([P, D])).then_inc(loaded, 16)
            sp.wait_ge(free_r, 1)
            sp.dma_start(r[:, :, :], all_rows(h_in)).then_inc(loaded, 16)
            sp.wait_ge(free_r, 2)
            sp.dma_start(all_rows(h_out), out[:, :, :]).then_inc(stored, 16)
            sp.wait_ge(stored, 16)

        @block.tensor
        def _(pe):
            for k in range(2):
                pe.wait_ge(to_sum, k + 1)
                x = out if k == 0 else tmp
                for g in range(NG):
                    last = nc.tensor.matmul(kit.bank[k][:, :], kit.ones[:, :], x[:, g * G:(g + 1) * G, :], start=g == 0, stop=g == NG - 1)
                last.then_inc(summed, 1)

        @block.scalar
        def _(act):
            act.wait_ge(sig_in, 1)
            nc.scalar.activation(beta[:, :], more[:, :], ACT.Exp, scale=-1.0).then_inc(sig_out, 1)
            act.wait_ge(root_in, 1)
            nc.scalar.activation(std[:, :], var[:, :], ACT.Sqrt).then_inc(root_out, 1)

        @block.vector
        def _(dve):
            s = Steps(dve, step)
            acc = kit.acc
            dve.wait_ge(loaded, 16 * 7)
            s.link(v.tensor_scalar(den[:, :, :], acc[:, :, D:D + H], 1e-30, None, ALU.max))
            s.link(v.reciprocal(den[:, :, :], den[:, :, :]))
            for h in range(H):
                cols = slice(h * C, (h + 1) * C)
                s.mark(v.tensor_tensor(tmp[:, :, cols], vec["we"][:, cols].unsqueeze(1).broadcast_to([P, NTG, C]),
                                       acc[:, :, D + H + h:D + H + h + 1].broadcast_to([P, NTG, C]), ALU.mult))
            s.need(s.n)
            s.link(v.tensor_tensor(out[:, :, :], tmp[:, :, :], acc[:, :, 0:D], ALU.add))
            for h in range(H):
                cols = slice(h * C, (h + 1) * C)
                s.mark(v.tensor_tensor(out[:, :, cols], out[:, :, cols], den[:, :, h:h + 1].broadcast_to([P, NTG, C]), ALU.mult))
            s.need(s.n)
            s.mark(v.tensor_tensor(wb[:, 0, :], vec["wb_out"][:, :], vec["wb_diff"][:, :], ALU.add))
            s.link(v.tensor_tensor(wb[:, 1, :], vec["wb_r"][:, :], vec["wb_diff"][:, :], ALU.subtract))
            s.link(v.tensor_tensor(tmp[:, :, :], out[:, :, :], wb[:, 0:1, :].broadcast_to(whole), ALU.mult))
            s.link(v.tensor_reduce(out=beta[:, :], in_=tmp[:, :, :], axis=AX.X, op=ALU.add))
            s.link(v.tensor_tensor(tmp[:, :, :], r[:, :, :], wb[:, 1:2, :].broadcast_to(whole), ALU.mult))
            s.link(v.tensor_reduce(out=more[:, :], in_=tmp[:, :, :], axis=AX.X, op=ALU.add))
            v.tensor_tensor(more[:, :], more[:, :], beta[:, :], ALU.add).then_inc(sig_in, 1)
            dve.wait_ge(sig_out, 1)
            s.link(v.tensor_scalar(beta[:, :], beta[:, :], 1.0, None, ALU.add))
            s.link(v.reciprocal(beta[:, :], beta[:, :]))
            s.link(v.tensor_tensor(tmp[:, :, :], r[:, :, :], out[:, :, :], ALU.subtract))
            s.link(v.tensor_tensor(tmp[:, :, :], tmp[:, :, :], along(beta), ALU.mult))
            s.link(v.tensor_tensor(out[:, :, :], out[:, :, :], tmp[:, :, :], ALU.add))
            s.mark(v.tensor_scalar(real[:, :], kit.part[:, :], float(LAST), None, ALU.is_lt))
            s.mark(v.memset(out[:, NT:, :], 0.0))
            s.need(s.n)
            v.tensor_scalar(out[:, NT - 1, :], out[:, NT - 1, :], real[:, :], None, ALU.mult).then_inc(to_sum, 1)
            v.memset(more[0:1, 0:1], 0.0).then_inc(free_r, 1)
            dve.wait_ge(summed, 1)
            four = kit.bank[0][:, :].rearrange("p (c f) -> p f c", c=G)
            s.link(v.tensor_reduce(out=mean[:, :], in_=four, axis=AX.X, op=ALU.add))
            s.link(v.tensor_scalar(mean[:, :], mean[:, :], 1.0 / NODES, None, ALU.mult))
            s.link(v.tensor_tensor(out[:, :, :], out[:, :, :], over(mean), ALU.subtract))
            s.link(v.tensor_tensor(tmp[:, :, :], out[:, :, :], out[:, :, :], ALU.mult))
            s.mark(v.memset(tmp[:, NT:, :], 0.0))
            v.tensor_scalar(tmp[:, NT - 1, :], tmp[:, NT - 1, :], real[:, :], None, ALU.mult).then_inc(to_sum, 1)
            dve.wait_ge(summed, 2)
            four = kit.bank[1][:, :].rearrange("p (c f) -> p f c", c=G)
            s.link(v.tensor_reduce(out=var[:, :], in_=four, axis=AX.X, op=ALU.add))
            v.tensor_scalar(var[:, :], var[:, :], 1.0 / NODES, EPS, ALU.mult, ALU.add).then_inc(root_in, 1)
            dve.wait_ge(root_out, 1)
            s.link(v.reciprocal(factor[:, :], std[:, :]))
            s.link(v.tensor_tensor(factor[:, :], factor[:, :], vec["gamma"][:, :], ALU.mult))
            s.link(v.tensor_tensor(out[:, :, :], out[:, :, :], over(factor), ALU.mult))
            s.link(v.tensor_tensor(out[:, :, :], out[:, :, :], over(vec["shift"]), ALU.add))
            dve.wait_ge(loaded, 16 * 8)
            s.link(v.scalar_tensor_tensor(out=out[:, :, :], in0=out[:, :, :], scalar=0.0, in1=r[:, :, :], op0=ALU.max, op1=ALU.add))
            v.memset(more[0:1, 0:1], 0.0).then_inc(free_r, 1)


def attended(kit, name, rows):
    nc, v = kit.nc, kit.nc.vector
    H = HEADS2
    C = D // H
    with Phase(kit, name) as ph:
        out = ph.sb("out", [P, NTG, D])
        inv = ph.sb("inv", [P, NTG, H])
        step, stored = ph.sem("step"), ph.sem("stored")
        block = ph.block()

        @block.vector
        def _(dve):
            s = Steps(dve, step)
            s.link(v.tensor_scalar(inv[:, :, :], kit.acc[:, :, D:D + H], 1e-16, None, ALU.add))
            s.link(v.reciprocal(inv[:, :, :], inv[:, :, :]))
            s.mark(v.tensor_tensor(out[:, :, 0:C], kit.acc[:, :, 0:C], inv[:, :, 0:1].broadcast_to([P, NTG, C]), ALU.mult))
            s.mark(v.tensor_tensor(out[:, :, C:D], kit.acc[:, :, C:D], inv[:, :, 1:2].broadcast_to([P, NTG, C]), ALU.mult))

        @block.sync
        def _(sp):
            sp.wait_ge(step, 4)
            sp.dma_start(rows.rearrange("(c p) f -> p c f", p=P), out[:, :, :]).then_inc(stored, 16)
            sp.wait_ge(stored, 16)


def layer_2(kit, ins, x1, l1_out, x2, own, alpha, node_max, v_rows, table):
    nc, v = kit.nc, kit.nc.vector
    h2, sent, recv = (kit.dram(n, (NTG * P, D)) for n in ("l2_h", "l2_sent", "l2_recv"))

    def norm(dve, s, g, t):
        s.link(v.tensor_tensor(t["x"][:, :, :], t["x"][:, :, :], t["l1"][:, :, :], ALU.add))
        t["norm"].on_vector(dve, s, t["x"][:, :, :], t["h"][:, :, :], g.times(1, 1))

    def tables(dve, s, g, t, banks):
        s.mark(v.tensor_copy(own[:, bass.ds(g.times(G), G), 0:D], by_tile(banks[0])))
        s.mark(v.tensor_copy(t["b"][:, :, :], by_tile(banks[1])))
        s.mark(v.tensor_copy(t["v"][:, :, :], by_tile(banks[2])))
        s.need(s.n)

    w1 = ins["L2_gnn_w1"]
    node_pass(kit, "l2_tables", {"x": x1, "l1": l1_out}, ["h"], {"w1a": w1[0:D, :], "w1b": w1[D:2 * D, :], "w3a": ins["L2_gnn_w3"][0:D, :]},
              [([(0, "w1a")], ins["L2_gnn_b1"]), ([(0, "w1b")], None), ([(0, "w3a")], ins["L2_gnn_b3"])],
              [("b", table[:, 0:D]), ("v", table[:, D:2 * D]), ("x", x2), ("h", h2)], scratch=("h", "b", "v"),
              before=norm, after=tables, norm_before=True, steps=(1 + NORM_STEPS, 3))
    with Phase(kit, "l2_w2") as ph:
        w2 = ph.sb("w2", [P, D])
        with Phase(kit, "l2_w2_in") as inner:
            done = inner.sem("done")
            block = inner.block()

            @block.sync
            def _(sp):
                sp.dma_start(w2[:, :], rows_of(ins["L2_gnn_w2"].rearrange("h f -> (h f)")).broadcast_to([P, D])).then_inc(done, 16)
                sp.wait_ge(done, 16)

        for name, by_src, rows in (("sent", True, sent), ("recv", False, recv)):
            score_pass(kit, f"l2_score_{name}", by_src, 2, table, v_rows, own, alpha, node_max, w2)
            weigh_pass(kit, f"l2_weigh_{name}", by_src, 2, v_rows, alpha, node_max)
            attended(kit, f"l2_out_{name}", rows)
    return h2, sent, recv


def layer_2_mlp(kit, ins, x2, x3, h3, h2, sent, recv):
    nc, v = kit.nc, kit.nc.vector
    GRAPHS, HID = 500, 512
    CH = 4
    S = 6
    GP = GRAPHS // CH
    with Phase(kit, "mlp") as ph:
        mw0 = ph.sb("mw0", [P, 4, HID])
        mw1 = ph.sb("mw1", [P, 4, HID])
        mw2 = ph.sb("mw2", [P, 4, D])
        rows = {n: ph.sb(n, [1, HID]) for n in ("mb0", "mb1")}
        mb2 = ph.sb("mb2", [1, D])
        vec = {n: ph.sb(n, [P, HID]) for n in ("ls0", "lb0", "ls1", "lb1")}
        u = ph.sb("u", [P, CH, D])
        u_t = ph.sb("u_t", [P, P])
        gu = ph.sb("gu", [P, CH, HID])
        count_i = ph.sb("count_i", [P, CH], I32)
        count = ph.sb("count", [P, CH])
        first = ph.sb("first", [P, CH])
        behind = ph.sb("behind", [P, CH])
        node_no = [ph.sb(f"node_no{k}", [P, P]) for k in range(2)]

        def each_slot(make, what, *args):
            return [make(f"{what}{u}", *args) for u in range(S)]

        def two(what, shape):
            return [ph.sb(f"{what}{u}", shape) for u in range(2)]

        part = {n: each_slot(ph.sb, n, [P, D]) for n in ("h", "s", "r", "x")}
        ge, member = two("ge", [P, CH, P]), two("member", [P, CH, P])
        part_t = ph.sb("part_t", [P, 3, P])
        hid = [two(f"hid{k}_", [P, HID]) for k in range(2)]
        hid_t = [ph.sb(f"hid_t{k}", [P, 4, P]) for k in range(2)]
        square = [ph.sb(f"square{k}", [P, HID]) for k in range(3)]
        out_h = each_slot(ph.sb, "out_h", [P, D])
        stats = [two(f"stats{k}_", [P, 4]) for k in range(3)]
        loaded, counted, placed, u_turned, u_copied, u_made, u_kept = (
            ph.sem(n) for n in ("loaded", "counted", "placed", "u_turned", "u_copied", "u_made", "u_kept"))
        step = ph.sem("step")
        begun = ph.sem("begun")
        membered = ph.sem("membered")
        numbered = ph.sem("numbered")
        tile_in = each_slot(ph.sem, "tile_in")
        turned, copied = ph.sem("turned"), ph.sem("copied")
        made = [ph.sem(f"made{k}") for k in range(3)]
        hid_turned = [ph.sem(f"hid_turned{k}") for k in range(2)]
        hid_copied = [ph.sem(f"hid_copied{k}") for k in range(2)]
        added_up, centred, squared, varied, rooted, inverted, scaled, shifted, stretched, relued = (
            [ph.sem(f"{n}{k}") for k in range(3)]
            for n in ("added_up", "centred", "squared", "varied", "rooted", "inverted", "scaled", "shifted", "stretched", "relued"))
        summed = ph.sem("summed")
        stored = each_slot(ph.sem, "stored")
        block = ph.block()
        SETUP = 6
        LOADS = 11 + CH
        TILE_COUNT = -(-NT // S) * S

        def out_bank(g, k):
            return kit.bank[2 + k + 4 * (g.u % 2)]

        def first_stats(dve, g, k, x, width):
            st = stats[k][g.u % 2]
            g.back(2).past(scaled[k])
            v.tensor_reduce(out=st[:, 0:1], in_=x, axis=AX.X, op=ALU.add).then_inc(added_up[k], 1)
            g.past(added_up[k])
            v.tensor_scalar(st[:, 0:1], st[:, 0:1], -1.0 / width, None, ALU.mult).then_inc(centred[k], 1)

        def variance(dve, g, k, width):
            st = stats[k][g.u % 2]
            g.past(squared[k])
            v.tensor_scalar(st[:, 1:2], st[:, 1:2], 1.0 / width, EPS, ALU.mult, ALU.add).then_inc(varied[k], 1)

        def scale_rows(dve, g, k, x, out):
            st = stats[k][g.u % 2]
            g.past(rooted[k])
            v.reciprocal(st[:, 3:4], st[:, 2:3]).then_inc(inverted[k], 1)
            g.past(inverted[k])
            v.tensor_scalar(out, x, st[:, 0:1], st[:, 3:4], ALU.add, ALU.mult).then_inc(scaled[k], 1)

        def squares(act, g, k, x, width):
            st = stats[k][g.u % 2]
            g.past(centred[k])
            nc.scalar.activation(square[k][:, 0:width], x, ACT.Square, bias=st[:, 0:1], accum_out=st[:, 1:2]).then_inc(squared[k], 1)

        def root(act, g, k):
            st = stats[k][g.u % 2]
            g.past(varied[k])
            nc.scalar.activation(st[:, 2:3], st[:, 1:2], ACT.Sqrt).then_inc(rooted[k], 1)

        @block.sync
        def _(sp):
            sp.dma_start(mw0[:, :, :], ins["L2_gnn_mw0"].rearrange("(k p) f -> p k f", p=P)).then_inc(loaded, 16)
            sp.dma_start(mw1[:, :, :], ins["L2_gnn_mw1"].rearrange("(k p) f -> p k f", p=P)).then_inc(loaded, 16)
            sp.dma_start(mw2[:, :, :], ins["L2_gnn_mw2"].rearrange("(k p) f -> p k f", p=P)).then_inc(loaded, 16)
            for n in rows:
                sp.dma_start(rows[n][:, :], rows_of(ins[f"L2_gnn_{n}"])).then_inc(loaded, 16)
            sp.dma_start(mb2[:, :], rows_of(ins["L2_gnn_mb2"])).then_inc(loaded, 16)
            for n in vec:
                sp.dma_start(vec[n][:, :], rows_of(ins[f"L2_gnn_{n}"]).broadcast_to([P, HID])).then_inc(loaded, 16)
            sp.dma_start(u[0:GP, :, :], ins["L2_gnn_u"].rearrange("(k p) f -> p k f", p=GP)).then_inc(loaded, 16)
            for k in range(CH):
                sp.dma_start(count_i[0:GP, k:k + 1], ins["L2_gnn_num_nodes"][k * GP:(k + 1) * GP].rearrange("(p o) -> p o", o=1)).then_inc(loaded, 16)
            sp.wait_ge(loaded, LOADS * 16)

            def load(g):
                first = g.times(P)
                sp.wait_ge(loaded, LOADS * 16)
                g.back(S).wait(stored, 32)
                for n, ap in (("h", h2), ("s", sent), ("r", recv), ("x", x2)):
                    sp.dma_start(part[n][g.u][:, :], ap[bass.ds(first, P), :]).then_inc(tile_in[g.u], 16)

            def store(g):
                first = g.times(P)
                sp.wait_ge(loaded, LOADS * 16)
                g.past(summed)
                sp.dma_start(x3[bass.ds(first, P), :], part["x"][g.u][:, :]).then_inc(stored[g.u], 16)
                g.past(relued[2])
                sp.dma_start(h3[bass.ds(first, P), :], out_h[g.u][:, :]).then_inc(stored[g.u], 16)

            over_groups(sp, (0, load), (4, store), slots=S, count=TILE_COUNT)
            for slot in range(S):
                sp.wait_ge(stored[slot], TILE_COUNT // S * 32)

        @block.vector
        def _(dve):
            s = Steps(dve, step)
            dve.wait_ge(loaded, LOADS * 16)
            v.tensor_copy(count[0:GP, :], count_i[0:GP, :]).then_inc(counted, 1)
            for k in range(CH):
                dve.wait_ge(u_made, k + 1)
                v.tensor_copy(gu[0:GP, k, :], kit.bank[2][0:GP, :]).then_inc(u_kept, 1)
            dve.wait_ge(placed, 1)
            s.mark(v.tensor_copy(first[0:GP, :], kit.bank[7][0:GP, 0:CH]))
            s.link(v.tensor_copy(node_no[0][:, :], kit.node_of_col[:, :]))
            s.link(v.tensor_tensor(behind[0:GP, :], first[0:GP, :], count[0:GP, :], ALU.add))
            s.link(v.tensor_scalar(count[0:GP, 0:1], kit.part[0:GP, :], float(GP - 1), BIG, ALU.is_equal, ALU.mult))
            s.link(v.tensor_tensor(behind[0:GP, CH - 1:CH], behind[0:GP, CH - 1:CH], count[0:GP, 0:1], ALU.add))
            s.link(v.tensor_scalar(node_no[1][:, :], node_no[0][:, :], float(P), None, ALU.add))
            assert s.n == SETUP

            def members(g):
                numbers = node_no[g.u % 2]
                g.back(2).past(made[0])
                if not isinstance(g.it, int) or g.it * S + g.offset >= 2:
                    dve.wait_ge(numbered, g.times(1, -1))
                for k in range(CH):
                    v.tensor_scalar(ge[g.u % 2][0:GP, k, :], numbers[0:GP, :], first[0:GP, k:k + 1], None, ALU.is_ge).then_inc(begun, 1)
                g.past(begun, CH)
                for k in range(CH):
                    v.scalar_tensor_tensor(out=member[g.u % 2][0:GP, k, :], in0=numbers[0:GP, :], scalar=behind[0:GP, k:k + 1],
                                           in1=ge[g.u % 2][0:GP, k, :], op0=ALU.is_lt, op1=ALU.mult).then_inc(membered, 1)
                g.past(membered, CH)
                v.tensor_scalar(numbers[:, :], numbers[:, :], float(2 * P), None, ALU.add).then_inc(numbered, 1)

            def hidden(k):
                def begin(g):
                    g.past(made[k])
                    first_stats(dve, g, k, out_bank(g, k)[:, :], HID)

                def middle(g):
                    variance(dve, g, k, HID)

                def end(g):
                    out = hid[k][g.u % 2][:, :]
                    g.back(2).past(hid_turned[k])
                    scale_rows(dve, g, k, out_bank(g, k)[:, :], out)
                    g.past(scaled[k])
                    v.tensor_tensor(out, out, vec[f"ls{k}"][:, :], ALU.mult).then_inc(stretched[k], 1)
                    g.past(stretched[k])
                    v.tensor_tensor(out, out, vec[f"lb{k}"][:, :], ALU.add).then_inc(shifted[k], 1)

                return begin, middle, end

            def residual(g):
                x = part["x"][g.u][:, :]
                g.past(made[2])
                g.wait(tile_in, 64)
                v.tensor_tensor(x, x, kit.bank[4][:, 0:D], ALU.add).then_inc(summed, 1)
                g.past(summed)
                first_stats(dve, g, 2, x, D)

            def last_variance(g):
                variance(dve, g, 2, D)

            def last_scale(g):
                g.back(S).wait(stored, 32)
                scale_rows(dve, g, 2, part["x"][g.u][:, :], out_h[g.u][:, :])

            begin0, middle0, end0 = hidden(0)
            begin1, middle1, end1 = hidden(1)
            over_groups(dve, (0, members), (1, begin0), (2, begin1), (1, middle0), (2, middle1), (1, end0), (3, residual),
                        (2, end1), (3, last_variance), (3, last_scale), slots=S, count=TILE_COUNT)

        @block.tensor
        def _(pe):
            pe.wait_ge(loaded, LOADS * 16)
            pe.wait_ge(counted, 1)
            for k in range(CH):
                for j in range(k):
                    nc.tensor.matmul(kit.bank[7][0:GP, k:k + 1], kit.ones[0:GP, 0:GP], count[0:GP, j:j + 1], start=j == 0, stop=False)
                last = nc.tensor.matmul(kit.bank[7][0:GP, k:k + 1], kit.before[0:GP, 0:GP], count[0:GP, k:k + 1], start=k == 0, stop=True)
            last.then_inc(placed, 1)
            for k in range(CH):
                pe.wait_ge(u_copied, k)
                nc.tensor.transpose(kit.bank[1][:, 0:GP], u[0:GP, k, :], kit.ident[0:GP, 0:GP]).then_inc(u_turned, 1)
                pe.wait_ge(u_copied, k + 1)
                pe.wait_ge(u_kept, k)
                nc.tensor.matmul(kit.bank[2][0:GP, :], u_t[:, 0:GP], mw0[:, 3, :], start=True, stop=False)
                nc.tensor.matmul(kit.bank[2][0:GP, :], kit.ones[0:1, 0:GP], rows["mb0"][:, :], start=False, stop=True).then_inc(u_made, 1)
            pe.wait_ge(u_kept, CH)

            def layer0(g):
                g.wait(tile_in, 64)
                g.back(1).past(copied)
                for k, n in enumerate(("h", "s", "r")):
                    last = nc.tensor.transpose(kit.bank[0][:, k * P:(k + 1) * P], part[n][g.u][:, :], kit.ident[:, :])
                last.then_inc(turned, 1)
                g.past(membered, CH)
                bank = out_bank(g, 0)
                g.back(2).past(scaled[0])
                for k in range(CH):
                    nc.tensor.matmul(bank[:, :], member[g.u % 2][0:GP, k, :], gu[0:GP, k, :], start=k == 0, stop=False)
                g.past(copied)
                for k in range(3):
                    last = nc.tensor.matmul(bank[:, :], part_t[:, k, :], mw0[:, k, :], start=False, stop=k == 2)
                last.then_inc(made[0], 1)

            def layer(k):

                def multiply(g):
                    out, w, bias = (out_bank(g, 1)[:, :], mw1, rows["mb1"]) if k == 0 else (kit.bank[4][:, 0:D], mw2, mb2)
                    g.past(relued[k])
                    g.back(1).past(hid_copied[k])
                    for c in range(4):
                        last = nc.tensor.transpose(kit.bank[1 + 4 * k][:, c * P:(c + 1) * P], hid[k][g.u % 2][:, c * P:(c + 1) * P], kit.ident[:, :])
                    last.then_inc(hid_turned[k], 1)
                    if k == 0:
                        g.back(2).past(scaled[1])
                    else:
                        g.back(1).past(summed)
                    nc.tensor.matmul(out, kit.ones[0:1, :], bias[:, :], start=True, stop=False)
                    g.past(hid_copied[k])
                    for c in range(4):
                        last = nc.tensor.matmul(out, hid_t[k][:, c, :], w[:, c, :], start=False, stop=c == 3)
                    last.then_inc(made[k + 1], 1)

                return multiply

            over_groups(pe, (0, layer0), (1, layer(0)), (2, layer(1)), slots=S, count=TILE_COUNT)

        @block.scalar
        def _(act):
            for k in range(CH):
                act.wait_ge(u_turned, k + 1)
                act.wait_ge(u_made, k)
                nc.scalar.copy(u_t[:, 0:GP], kit.bank[1][:, 0:GP]).then_inc(u_copied, 1)

            def copy(g):
                g.past(turned)
                g.back(1).past(made[0])
                nc.scalar.copy(part_t[:, :, :], kit.bank[0][:, 0:3 * P].rearrange("p (c e) -> p c e", c=3)).then_inc(copied, 1)

            def copy_hid(k):
                def copy(g):
                    g.past(hid_turned[k])
                    g.back(1).past(made[k + 1])
                    nc.scalar.copy(hid_t[k][:, :, :], kit.bank[1 + 4 * k][:, :].rearrange("p (c e) -> p c e", c=4)).then_inc(hid_copied[k], 1)
                return copy

            def square_hid(k):
                def square(g):
                    squares(act, g, k, out_bank(g, k)[:, :], HID)
                return square

            def root_hid(k):
                def take(g):
                    root(act, g, k)
                return take

            def relu_hid(k):
                def relu(g):
                    out = hid[k][g.u % 2][:, :]
                    g.past(shifted[k])
                    nc.scalar.activation(out, out, ACT.Relu).then_inc(relued[k], 1)
                return relu

            def root_last(g):
                root(act, g, 2)

            def square_last(g):
                squares(act, g, 2, part["x"][g.u][:, :], D)

            def relu_last(g):
                out = out_h[g.u][:, :]
                g.past(scaled[2])
                nc.scalar.activation(out, out, ACT.Relu).then_inc(relued[2], 1)

            over_groups(act, (0, copy), (1, square_hid(0)), (2, square_hid(1)), (1, root_hid(0)), (2, root_hid(1)), (1, relu_hid(0)),
                        (3, square_last), (1, copy_hid(0)), (2, relu_hid(1)), (3, root_last), (2, copy_hid(1)), (3, relu_last), slots=S, count=TILE_COUNT)


def layer_3(kit, ins, x3, h3, x4, own):
    nc, v = kit.nc, kit.nc.vector
    hw, agg, u = (kit.dram(n, (NTG * P, D)) for n in ("l3_hw", "l3_agg", "l3_u"))

    def tables(dve, s, g, t, banks):
        s.mark(v.tensor_copy(t["out"][:, :, :], by_tile(banks[0])))
        s.mark(v.tensor_tensor(own[:, bass.ds(g.times(G), G), :], by_tile(banks[0]), each(t["b1"]), ALU.add))
        s.need(s.n)

    node_pass(kit, "l3_tables", {"h": h3}, ["h"], {"w1": ins["L3_gnn_e_w1"]}, [([(0, "w1")], None)], [("out", hw)],
              scratch=("out",), wide={"b1": ins["L3_gnn_e_b1"]}, after=tables, steps=(0, 2))
    sum_pass(kit, "l3_sum", True, table=hw, own=own)

    def take_sums(dve, s, g, t):
        s.link(v.tensor_copy(t["sums"][:, :, :], kit.acc[:, bass.ds(g.times(G), G), 0:D]))
        s.link(v.tensor_tensor(t["out"][:, :, :], degree(kit, g, t), each(t["b2"]), ALU.mult))

    def add_bias(dve, s, g, t, banks):
        s.link(v.tensor_tensor(t["out"][:, :, :], t["out"][:, :, :], by_tile(banks[0]), ALU.add))

    node_pass(kit, "l3_agg_", {}, ["sums"], {"w2": ins["L3_gnn_e_w2"]}, [([(0, "w2")], None)], [("out", agg)],
              scratch=("sums", "out"), wide={"b2": ins["L3_gnn_e_b2"]}, before=take_sums, after=add_bias, steps=(2, 1))

    def relu(dve, s, g, t, banks):
        s.link(v.tensor_scalar(t["out"][:, :, :], by_tile(banks[0]), 0.0, None, ALU.max))

    node_pass(kit, "l3_inner", {"h": h3, "agg": agg}, ["h", "agg"], {"w1a": ins["L3_gnn_n_w1"][0:D, :], "w1b": ins["L3_gnn_n_w1"][D:2 * D, :]},
              [([(0, "w1a"), (1, "w1b")], ins["L3_gnn_n_b1"])], [("out", u)], scratch=("out",), after=relu, steps=(0, 1))

    def add(dve, s, g, t, banks):
        s.link(v.tensor_tensor(t["x"][:, :, :], t["x"][:, :, :], by_tile(banks[0]), ALU.add))

    node_pass(kit, "l3_out", {"u": u, "x": x3}, ["u"], {"w2": ins["L3_gnn_n_w2"]}, [([(0, "w2")], ins["L3_gnn_n_b2"])], [("x", x4)],
              after=add, steps=(0, 1))


def build_program(nc, ins, outs, stop=None):
    with ExitStack() as ctx:
        kit = Kit(nc, ctx)
        constants(kit)
        with Phase(kit, "edges") as ph:
            pos = [ph.sb(f"pos{k}", [P, COLS + 1], I32) for k in range(2)]
            pads = [ph.sb(f"pads{k}", [P, PADS], I32) for k in range(2)]
            recs = [ph.sb(f"recs{k}", [P, COLS + 1, REC]) for k in range(2)]
            sort_positions(kit, ins, *pos, *pads, *recs)
            scatter_edges(kit, ins, *pos, *pads, *recs)
        load_records(kit, "recs")
        if stop:
            return stop(kit, outs)
        x = [kit.dram(f"x{k}", (NTG * P, D)) for k in range(5)]
        h1, l1_out, h3 = (kit.dram(n, (NTG * P, D)) for n in ("h1", "l1_out", "h3"))
        pad_nodes(kit, ins["x"], x[0], (x[3], h3))
        layer_0(kit, ins, x[0], x[1], h1)
        table = kit.dram("pair_table", (NTG * P, 2 * D))
        v_rows = kit.dram("values", (P, TILES, D))
        with Phase(kit, "attention") as ph:
            own = ph.sb("own", [P, NTG, D + HEADS1])
            alpha = ph.sb("alpha", [P, TILES, HEADS1])
            node_max = ph.sb("node_max", [P, NTG, HEADS1])
            layer_1(kit, ins, ph, h1, l1_out, own, alpha, node_max, v_rows, table)
            h2, sent, recv = layer_2(kit, ins, x[1], l1_out, x[2], own, alpha, node_max, v_rows, table)
        layer_2_mlp(kit, ins, x[2], x[3], h3, h2, sent, recv)
        with Phase(kit, "last") as ph:
            own = ph.sb("own", [P, NTG, D])
            layer_3(kit, ins, x[3], h3, x[4], own)
        with Phase(kit, "out") as ph:
            done = ph.sem("done")
            block = ph.block()

            @block.sync
            def _(sp):
                sp.dma_start(outs["out"], x[4][0:NODES, :]).then_inc(done, 16)
                sp.wait_ge(done, 16)


def kernel(**inputs):
    import concourse.bacc as bacc
    import numpy as np
    from concourse.bass_utils import run_bass_kernel_spmd

    nc = bacc.Bacc("TRN2", target_bir_lowering=False, num_devices=1)
    arrays, ins = {}, {}
    for name, a in inputs.items():
        a = np.ascontiguousarray(a)
        arrays[f"in_{name}"] = a
        ins[name] = nc.dram_tensor(f"in_{name}", a.shape, mybir.dt.from_np(a.dtype), kind="ExternalInput").ap()
    out = nc.dram_tensor("out_x", (NODES, D), F32, kind="ExternalOutput").ap()
    build_program(nc, ins, {"out": out})
    ran = run_bass_kernel_spmd(nc, [arrays], core_ids=[0])
    return ran.results[0]["out_x"]
```
